# Optimizing a Trainium2 kernel written in Bass

```python
import numpy as np
import jax
import jax.numpy as jnp

def _softmax(x, axis=-1):
    return jax.nn.softmax(x, axis=axis)

def _gelu(x):
    return jax.nn.gelu(x, approximate=True)

def _silu(x):
    return jax.nn.silu(x)

def _sigmoid(x):
    return jax.nn.sigmoid(x)

def _layernorm(x, axis=-1, eps=1e-05):
    m = jnp.mean(x, axis=axis, keepdims=True)
    v = jnp.var(x, axis=axis, keepdims=True)
    return (x - m) / jnp.sqrt(v + eps)

def _scatter_add(tgt, idx, src, axis=0):
    return tgt.at[idx].add(src)

def _segment_sum(src, seg, n):
    return jax.ops.segment_sum(src, seg, n)
kernel_name = 'mk_gnn_resnorm_d4_gnn_r8_cc5766'

def setup_inputs(seed: int=0):
    np.random.seed(seed)
    _w = jnp.asarray

    def _rec_inputs():
        import jax
        import jax.numpy as jnp
        _gk = jax.random.key(seed)
        x = -0.0009044 + 1 * jax.random.normal(jax.random.fold_in(_gk, 1), (12500, 32), jnp.float32)
        _s = jax.random.randint(jax.random.fold_in(_gk, 2), (100000,), 0, 12500, jnp.int32)
        _d = jax.random.randint(jax.random.fold_in(_gk, 3), (100000,), 0, 12500, jnp.int32)
        _loop = jnp.arange(12500, dtype=jnp.int32)
        src = jnp.concatenate([_s, _d, _loop])
        dst = jnp.concatenate([_d, _s, _loop])
        _o = jnp.argsort(dst, stable=True)
        src = src[_o]
        dst = dst[_o]
        edge_attr_2 = -5.09086e-05 + 0.577461 * jax.random.normal(jax.random.fold_in(_gk, 12), (212500, 2), jnp.float32)
        edge_weight = jax.random.uniform(jax.random.fold_in(_gk, 14), (212500,), jnp.float32, 0.0, 0.999999)
        return (x, src, dst, edge_attr_2, edge_weight)
    x, src, dst, edge_attr_2, edge_weight = _rec_inputs()

    def _L0_gnn_setup():
        import jax, jax.numpy as jnp
        import numpy as np
        N_NODES = 6250
        DEG = 16
        N_HEAD = 4
        F_IN = 32
        F_OUT = 32
        key = jax.random.key(seed)
        k_h, k_w, k_fw, k_fb = jax.random.split(key, 4)
        h = jax.random.normal(k_h, (N_NODES, F_IN), dtype=jnp.float32)
        src = jnp.repeat(jnp.arange(N_NODES, dtype=jnp.int64), DEG)
        offs = (jnp.arange(DEG, dtype=jnp.int64) + 1) * 97
        dst = (src.reshape(N_NODES, DEG) + offs[None, :]).reshape(-1) % N_NODES
        edge_index = jnp.stack([src, dst], axis=0)
        gain = 1.414
        bound_w = gain * np.sqrt(6.0 / (F_IN + F_OUT))
        w = jax.random.uniform(k_w, (N_HEAD, F_IN, F_OUT), jnp.float32, -bound_w, bound_w)
        bound_fc = np.sqrt(1.0 / (2 * F_OUT))
        fc_w = jax.random.uniform(k_fw, (1, 2 * F_OUT), jnp.float32, -bound_fc, bound_fc)
        fc_b = jax.random.uniform(k_fb, (1,), jnp.float32, -bound_fc, bound_fc)
        bias = jnp.zeros((F_OUT,), jnp.float32)
        return {'h': h, 'edge_index': edge_index, 'w': w, 'fc_w': fc_w, 'fc_b': fc_b, 'bias': bias}
    _L0_gnn_all = _L0_gnn_setup()
    _L0_gnn_in = {k: v for k, v in _L0_gnn_all.items() if k in ('w', 'fc_w', 'fc_b', 'bias')}
    del _L0_gnn_all

    def _L1_gnn_setup():
        import jax, jax.numpy as jnp
        import numpy as np
        N_NODES = 6250
        N_EDGES = 200000
        F_IN = 32
        F_OUT = 32
        BASIS = (4, 4)

        def _tent_basis(u, n):
            centers = jnp.linspace(-1.0, 1.0, n, dtype=u.dtype)
            h = 2.0 / (n - 1)
            return jnp.maximum(0.0, 1.0 - jnp.abs(u[:, None] - centers[None, :]) / h)
        key = jax.random.key(seed)
        k1, k2, k3, k4, k5 = jax.random.split(key, 5)
        x = jax.random.normal(k1, (N_NODES, F_IN), dtype=jnp.float32)
        edge_attr = jax.random.uniform(k2, (N_EDGES, 2), dtype=jnp.float32, minval=-1.0, maxval=1.0)
        weight = jax.random.uniform(k3, (*BASIS, F_IN, F_OUT), dtype=jnp.float32, minval=-0.05, maxval=0.05)
        src = jax.random.randint(k4, (N_EDGES,), 0, N_NODES)
        tgt = jax.random.randint(k5, (N_EDGES,), 0, N_NODES)
        edge_index = jnp.stack([tgt, src], axis=0).astype(jnp.int64)
        return {'x': x, 'edge_attr': edge_attr, 'weight': weight, 'edge_index': edge_index}
    _L1_gnn_all = _L1_gnn_setup()
    _L1_gnn_in = {k: v for k, v in _L1_gnn_all.items() if k in ('weight',)}
    del _L1_gnn_all

    def _L2_gnn_setup():
        import jax, jax.numpy as jnp
        import numpy as np
        N_NODES = 12500
        N_EDGES = 200000
        D_FEAT = 32
        key = jax.random.key(seed)
        k1, k2, k3 = jax.random.split(key, 3)
        edge_index = jax.random.randint(k1, (2, N_EDGES), 0, N_NODES, dtype=jnp.int64)
        x = jax.random.normal(k2, (N_NODES, D_FEAT), dtype=jnp.float32)
        W = jax.random.uniform(k3, (N_EDGES,), dtype=jnp.float32)
        return {'edge_index': edge_index, 'x': x, 'W': W}
    _L2_gnn_all = _L2_gnn_setup()
    _L2_gnn_in = {k: v for k, v in _L2_gnn_all.items() if k in ()}
    del _L2_gnn_all

    def _L3_gnn_setup():
        import jax, jax.numpy as jnp
        import numpy as np
        N = 12500
        E = 200000
        F_IN = 32
        F_OUT = 32
        key = jax.random.key(seed)
        k1, k2, k3, k4, k5 = jax.random.split(key, 5)
        x = jax.random.normal(k1, (N, F_IN), dtype=jnp.float32)
        edge_src = jax.random.randint(k2, (E,), 0, N, dtype=jnp.int32)
        edge_dst = jax.random.randint(k3, (E,), 0, N, dtype=jnp.int32)
        bound = 1.0 / np.sqrt(2 * F_IN)
        W = jax.random.uniform(k4, (2 * F_IN, F_OUT), minval=-bound, maxval=bound, dtype=jnp.float32)
        b = jax.random.uniform(k5, (F_OUT,), minval=-bound, maxval=bound, dtype=jnp.float32)
        return {'x': x, 'W': W, 'b': b, 'edge_src': edge_src, 'edge_dst': edge_dst}
    _L3_gnn_all = _L3_gnn_setup()
    _L3_gnn_in = {k: v for k, v in _L3_gnn_all.items() if k in ('W', 'b')}
    del _L3_gnn_all
    return {'x': x, 'src': src, 'dst': dst, 'edge_attr_2': edge_attr_2, 'edge_weight': edge_weight, 'L0_gnn_w': _L0_gnn_in['w'], 'L0_gnn_fc_w': _L0_gnn_in['fc_w'], 'L0_gnn_fc_b': _L0_gnn_in['fc_b'], 'L0_gnn_bias': _L0_gnn_in['bias'], 'L1_gnn_weight': _L1_gnn_in['weight'], 'L3_gnn_W': _L3_gnn_in['W'], 'L3_gnn_b': _L3_gnn_in['b']}

def reference(x, src, dst, edge_attr_2, edge_weight, L0_gnn_w, L0_gnn_fc_w, L0_gnn_fc_b, L0_gnn_bias, L1_gnn_weight, L3_gnn_W, L3_gnn_b):
    import jax
    import jax.numpy as jnp

    def _L0_gnn_ref(h, edge_index, w, fc_w, fc_b, bias):
        import jax, jax.numpy as jnp
        import numpy as np
        N_NODES = 6250
        DEG = 16
        N_HEAD = 4
        F_IN = 32
        F_OUT = 32
        n_head, f_in, f_out = w.shape
        n = h.shape[0]
        src, dst = (edge_index[0], edge_index[1])
        hp = jnp.einsum('nf,hfo->hno', h, w)
        w_src = fc_w[0, :f_out]
        w_dst = fc_w[0, f_out:]
        a_src = jnp.einsum('hnf,f->hn', hp, w_src)
        a_dst = jnp.einsum('hnf,f->hn', hp, w_dst)
        e = a_src[:, src] + a_dst[:, dst] + fc_b[0]
        e = jax.nn.leaky_relu(e, negative_slope=0.2)
        seg_max = jax.ops.segment_max(e.T, src, num_segments=n)
        e = jnp.exp(e - seg_max.T[:, src])
        seg_sum = jax.ops.segment_sum(e.T, src, num_segments=n)
        att = e / seg_sum.T[:, src]
        msg = att[:, :, None] * hp[:, dst, :]
        agg = jax.vmap(lambda m: jax.ops.segment_sum(m, src, num_segments=n))(msg)
        out = agg.mean(axis=0) + bias
        return out

    def _L1_gnn_ref(x, edge_attr, weight, edge_index):
        import jax, jax.numpy as jnp
        import numpy as np
        N_NODES = 6250
        N_EDGES = 200000
        F_IN = 32
        F_OUT = 32
        BASIS = (4, 4)

        def _tent_basis(u, n):
            centers = jnp.linspace(-1.0, 1.0, n, dtype=u.dtype)
            h = 2.0 / (n - 1)
            return jnp.maximum(0.0, 1.0 - jnp.abs(u[:, None] - centers[None, :]) / h)
        k1, k2, f_in, f_out = weight.shape
        n_nodes = x.shape[0]
        bu = _tent_basis(edge_attr[:, 0], k1)
        bv = _tent_basis(edge_attr[:, 1], k2)
        basis = (bu[:, :, None] * bv[:, None, :]).reshape(-1, k1 * k2)
        xj = x[edge_index[1]]
        w2 = weight.reshape(k1 * k2, f_in, f_out)
        msg = basis[:, 0:1] * (xj @ w2[0])
        for k in range(1, k1 * k2):
            msg = msg + basis[:, k:k + 1] * (xj @ w2[k])
        out = jax.ops.segment_sum(msg, edge_index[0], num_segments=n_nodes)
        return out

    def _L2_gnn_ref(edge_index, x, W):
        import jax, jax.numpy as jnp
        import numpy as np
        N_NODES = 12500
        N_EDGES = 200000
        D_FEAT = 32
        target = edge_index[1]
        messages = x[target] * W[:, None]
        aggr = jax.ops.segment_sum(messages, target, num_segments=x.shape[0])
        return aggr

    def _L3_gnn_ref(x, W, b, edge_src, edge_dst):
        import jax, jax.numpy as jnp
        import numpy as np
        N = 12500
        E = 200000
        F_IN = 32
        F_OUT = 32
        n = x.shape[0]
        msgs = x[edge_src]
        summed = jax.ops.segment_sum(msgs, edge_dst, num_segments=n)
        cnt = jax.ops.segment_sum(jnp.ones_like(edge_dst, dtype=x.dtype), edge_dst, num_segments=n)
        neigh_mean = summed / jnp.maximum(cnt, 1.0)[:, None]
        h = jnp.concatenate([x, neigh_mean], axis=1)
        return jax.nn.relu(h @ W + b)
    edge_index = jnp.stack([src, dst])
    x = _layernorm(x + _L0_gnn_ref(x, edge_index, L0_gnn_w, L0_gnn_fc_w, L0_gnn_fc_b, L0_gnn_bias), axis=-1)
    x = _layernorm(x + _L1_gnn_ref(x, edge_attr_2, L1_gnn_weight, edge_index), axis=-1)
    x = _layernorm(x + _L2_gnn_ref(edge_index, x, edge_weight), axis=-1)
    x = _layernorm(x + _L3_gnn_ref(x, L3_gnn_W, L3_gnn_b, src, dst), axis=-1)
    return x

_drawn_inputs = setup_inputs


def setup_inputs(seed=0):
    import zlib

    import numpy as np

    out = dict(_drawn_inputs(seed))
    spreads = {'L0_gnn_bias': (0.0, 0.1)}
    factors = {}
    for name, (base, spread) in spreads.items():
        noise = np.random.default_rng([zlib.crc32(name.encode()), seed]).standard_normal(out[name].shape)
        drawn = base * np.exp(spread * noise) if base else spread * noise
        out[name] = jnp.asarray(drawn.astype(out[name].dtype))
    for name, factor in factors.items():
        out[name] = (out[name] * factor).astype(out[name].dtype)
    return out
```

```python
import numpy as np
from contextlib import ExitStack

import concourse.bass as bass
from concourse import mybir

F32 = mybir.dt.float32
I32 = mybir.dt.int32
I16 = mybir.dt.int16
BF16 = mybir.dt.bfloat16
ALU = mybir.AluOpType
ACT = mybir.ActivationFunctionType
AX = mybir.AxisListType.X

P = 128
N = 12500
E = 212500
F = 32
H = 4
B = -(-N // P)
NN = B * P
PAD = NN - 1
C = 32
J = -(-E // (P * 2 * C)) * 2 * C
EP = P * J
CHUNKS = J // C
LASTROW = E - (P - 1) * J
LASTBLOCK = N - (B - 1) * P
GROUPS = -(-B // 4)
REC = 5
T0W = F + H
S0W = H * F + 2 * H
CELLS = 9
T1W = 4 * F
XDW = F + 1
BIG = 1.0e30
EPS = 1e-5


def bcast(ap, axis, n):
    a = ap.unsqueeze(axis)
    shape = list(a.shape)
    shape[axis] = n
    return a.broadcast_to(shape)


def load_split(eng, dst, src, sem):
    w = dst.shape[1] // J
    n = 0
    for lo, hi in ((0, 112), (112, P - 1)):
        eng.dma_start(dst[lo:hi, :], src[lo * J * w:hi * J * w].rearrange("(p j) -> p j", p=hi - lo)).then_inc(sem, 16)
        n += 16
    eng.dma_start(dst[P - 1:P, 0:LASTROW * w], src[(P - 1) * J * w:E * w].rearrange("(p j) -> p j", p=1)).then_inc(sem, 16)
    return n + 16


def prime(eng, m, sems):
    for sem in sems:
        eng.dma_start(m.spare[0:1, m.primed:m.primed + 1], m.first_word).then_inc(sem, 16)
        m.primed += 1


def stage_load(nc, m, x, src, dst, edge_attr, edge_weight):
    with ExitStack() as ctx:
        ki = [ctx.enter_context(nc.sbuf_tensor(f"key_int{k}", [P, J], I32)) for k in range(2)]
        part = ctx.enter_context(nc.sbuf_tensor("part", [P, J], I32))
        row_i = ctx.enter_context(nc.sbuf_tensor("row_i", [P, P], I32))
        col_i = ctx.enter_context(nc.sbuf_tensor("col_i", [P, 1], I32))
        row16 = ctx.enter_context(nc.sbuf_tensor("row16", [P, 2, J], I16))
        row_b = ctx.enter_context(nc.sbuf_tensor("row_b", [P, 2, J], BF16))
        wparts = ctx.enter_context(nc.sbuf_tensor("wbf", [P, J], BF16))
        zeros = ctx.enter_context(nc.sbuf_tensor("zeros_f", [P, H * J], F32))
        pst = [ctx.enter_context(nc.psum_tensor(f"ps_rows{i}", [P, P], F32)) for i in range(4)]
        s_clear = ctx.enter_context(nc.semaphore("s_clear"))
        s_iota = ctx.enter_context(nc.semaphore("s_iota"))
        s_in = ctx.enter_context(nc.semaphore("s_in"))
        s_keys = ctx.enter_context(nc.semaphore("s_keys"))
        s_turned = ctx.enter_context(nc.semaphore("s_turned"))
        s_row = ctx.enter_context(nc.semaphore("s_row"))
        s_out = ctx.enter_context(nc.semaphore("s_out"))
        block = ctx.enter_context(nc.Block())
        blocks = J // P
        arrays = 4

        @block.sync
        def _(sp):
            sp.wait_ge(s_clear, 1)
            n = 0
            for k, a in enumerate((src, dst)):
                n += load_split(sp, ki[k], a, s_in)
            sp.dma_start(m.x[:, 0:(B - 1) * F].rearrange("p (b f) -> p b f", f=F),
                         x[0:(B - 1) * P, :].rearrange("(b p) f -> p b f", p=P)).then_inc(s_in, 16)
            sp.dma_start(m.x[0:LASTBLOCK, (B - 1) * F:B * F], x[(B - 1) * P:N, :]).then_inc(s_in, 16)
            n += 32
            n += load_split(sp, m.attr, edge_attr.rearrange("e a -> (e a)"), s_in)
            n += load_split(sp, m.w, edge_weight, s_in)
            assert n == 14 * 16
            sp.dma_start(m.asrc_at.rearrange("(p j) h -> p (j h)", p=P), zeros[:, :]).then_inc(s_out, 16)
            hv = m.h3.rearrange("(p j) f -> p (j f)", p=P)
            for i in range(F // H):
                sp.dma_start(hv[:, i * H * J:(i + 1) * H * J], zeros[:, :]).then_inc(s_out, 16)
            sp.dma_start(m.rec[0:1, :], m.minus[0:1, 0:REC]).then_inc(s_out, 16)
            sp.dma_start(m.xd[0:1, :], m.minus[0:1, 0:XDW]).then_inc(s_out, 16)
            sp.dma_start(m.s0[EP:EP + 1, :], zeros[0:1, 0:S0W]).then_inc(s_out, 16)
            sp.dma_start(m.s1[EP:EP + 1, :], zeros[0:1, 0:F]).then_inc(s_out, 16)
            sp.dma_start(m.s3[EP:EP + 1, :], zeros[0:1, 0:F]).then_inc(s_out, 16)
            sp.wait_ge(s_row, 4 * blocks)
            for k in range(2):
                for a, t in ((m.keyrow[k], row16), (m.lorow[k], row_b)):
                    sp.dma_start(a.rearrange("(b t p) -> t b p", t=P, p=P),
                                 t[:, k, :].rearrange("t (b p) -> t b p", p=P)).then_inc(s_out, 16)
            sp.wait_ge(s_out, 16 * (1 + F // H + 5 + 4))

        @block.gpsimd
        def _(pool):
            pool.iota(row_i[:, :], pattern=[[1, P]], base=0, channel_multiplier=0).then_inc(s_iota, 1)
            pool.iota(col_i[:, :], pattern=[[0, 1]], base=0, channel_multiplier=1).then_inc(s_iota, 1)

        @block.vector
        def _(dve):
            for k in range(2):
                dve.memset(ki[k][:, :], PAD)
            dve.memset(m.x[:, :], 0.0)
            dve.memset(m.attr[:, :], 0.0)
            dve.memset(m.w[:, :], 0.0)
            dve.memset(zeros[:, :], 0.0)
            dve.memset(m.ones[:, :], 1.0)
            dve.memset(m.eps[:, :], EPS)
            dve.memset(m.minus[:, :], -1.0).then_inc(s_clear, 1)
            dve.wait_ge(s_iota, 2)
            dve.tensor_copy(m.lane[:, :], row_i[:, :])
            dve.tensor_copy(m.part[:, :], col_i[:, :])
            dve.drain()
            dve.tensor_copy(m.lane_b[:, :], m.lane[:, :])
            dve.tensor_scalar(m.ident[:, :], m.lane[:, :], m.part[:, 0:1], None, ALU.is_equal)
            dve.tensor_scalar(m.above[:, :], m.lane[:, :], m.part[:, 0:1], None, ALU.is_gt)
            dve.tensor_scalar(m.below[:, :], m.lane[:, :], m.part[:, 0:1], None, ALU.is_lt)
            dve.wait_ge(s_in, 14 * 16)
            for k in range(2):
                dve.tensor_copy(m.key[k][:, :], ki[k][:, :])
                dve.tensor_scalar(part[:, :], ki[k][:, :], 7, None, ALU.logical_shift_right)
                dve.drain()
                dve.tensor_copy(m.hi[k][:, :], part[:, :])
                dve.drain()
                dve.tensor_scalar(part[:, :], ki[k][:, :], P - 1, None, ALU.bitwise_and)
                dve.drain()
                dve.tensor_copy(m.lo[k][:, :], part[:, :])
                dve.drain()
            dve.drain().then_inc(s_keys, 1)
            for i in range(3):
                prev = m.w if i == 0 else m.wrest
                dve.tensor_copy(wparts[:, :], prev[:, :])
                dve.drain()
                dve.tensor_copy(m.wp[i][:, :], wparts[:, :])
                dve.drain()
                dve.tensor_tensor(m.wrest[:, :], prev[:, :], m.wp[i][:, :], ALU.subtract)
                dve.drain()

        @block.tensor
        def _(pe):
            pe.wait_ge(s_keys, 1)
            for i in range(arrays * blocks):
                a, b = divmod(i, blocks)
                s = (m.key[0], m.lo[0], m.key[1], m.lo[1])[a]
                if i >= 4:
                    pe.wait_ge(s_row, i - 3)
                pe.transpose(pst[i % 4][:, :], s[:, b * P:(b + 1) * P], m.ident[:, :]).then_inc(s_turned, 1)

        @block.scalar
        def _(act):
            for i in range(arrays * blocks):
                a, b = divmod(i, blocks)
                t = (row16, row_b)[a % 2]
                act.wait_ge(s_turned, i + 1)
                act.activation(t[:, a // 2, b * P:(b + 1) * P], pst[i % 4][:, :], ACT.Copy).then_inc(s_row, 1)


def stage_count(nc, m):
    SLOTS, UNROLL = 4, 8
    with ExitStack() as ctx:
        oa = [ctx.enter_context(nc.sbuf_tensor(f"onelane{k}", [P, SLOTS, P], BF16)) for k in range(2)]
        ob = [ctx.enter_context(nc.sbuf_tensor(f"oneblock{k}", [P, SLOTS, B * (1 if k == 0 else 4)], BF16)) for k in range(2)]
        zero = ctx.enter_context(nc.sbuf_tensor("zero_b", [P, 4 * B], BF16))
        ps = [ctx.enter_context(nc.psum_tensor(f"ps_count{k}", [P, 512], F32)) for k in range(2)]
        s_zero = ctx.enter_context(nc.semaphore("s_zero"))
        s_made = ctx.enter_context(nc.semaphore("s_made"))
        s_free = ctx.enter_context(nc.semaphore("s_free"))
        s_sum = ctx.enter_context(nc.semaphore("s_sum"))
        block = ctx.enter_context(nc.Block())

        @block.vector
        def _(dve):
            dve.memset(zero[:, :], 0.0).then_inc(s_zero, 1)
            with dve.Fori(0, J // UNROLL) as it:
                for u in range(UNROLL):
                    s = u % SLOTS
                    t = it * UNROLL + u
                    dve.wait_ge(s_free, t + 1)
                    for k in range(2):
                        dve.tensor_scalar(oa[k][:, s, :], m.lane_b[:, :], m.lo[k][:, bass.ds(t, 1)], None, ALU.is_equal)
                        last = dve.tensor_scalar(ob[k][:, s, 0:B], m.lane_b[:, 0:B], m.hi[k][:, bass.ds(t, 1)], None, ALU.is_equal)
                    for i in range(3):
                        last = dve.tensor_scalar(ob[1][:, s, (i + 1) * B:(i + 2) * B], m.lane_b[:, 0:B],
                                                 m.hi[1][:, bass.ds(t, 1)], m.wp[i][:, bass.ds(t, 1)], ALU.is_equal, ALU.mult)
                    last.then_inc(s_made, 1)
            dve.wait_ge(s_sum, 1)
            dve.tensor_copy(m.cnt[0][:, :], ps[0][:, 0:B])
            dve.tensor_copy(m.cnt[1][:, :], ps[1][:, 0:B])
            dve.tensor_copy(m.sumw[:, :], ps[1][:, B:2 * B])
            dve.drain()
            for i in (2, 3):
                dve.tensor_tensor(m.sumw[:, :], m.sumw[:, :], ps[1][:, i * B:(i + 1) * B], ALU.add)
                dve.drain()

        @block.tensor
        def _(pe):
            pe.wait_ge(s_zero, 1)
            pe.matmul(ps[0][:, 0:B], zero[:, 0:P], zero[:, 0:B], start=True, stop=False)
            pe.matmul(ps[1][:, 0:4 * B], zero[:, 0:P], zero[:, :], start=True, stop=False)
            pe.sem_inc(s_free, SLOTS)
            with pe.Fori(0, J // UNROLL) as it:
                for u in range(UNROLL):
                    s = u % SLOTS
                    pe.wait_ge(s_made, it * UNROLL + (u + 1))
                    pe.sem_inc(m.step_pe, 1)
                    pe.matmul(ps[0][:, 0:B], oa[0][:, s, :], ob[0][:, s, :], start=False, stop=False)
                    pe.matmul(ps[1][:, 0:4 * B], oa[1][:, s, :], ob[1][:, s, :], start=False, stop=False).then_inc(s_free, 1)
            pe.matmul(ps[0][:, 0:B], zero[:, 0:P], zero[:, 0:B], start=False, stop=True)
            pe.matmul(ps[1][:, 0:4 * B], zero[:, 0:P], zero[:, :], start=False, stop=True).then_inc(s_sum, 1)


def stage_places(nc, m, w0, fc_w, fc_b):
    with ExitStack() as ctx:
        def sb(name, shape, dt=F32):
            return ctx.enter_context(nc.sbuf_tensor(name, shape, dt))
        tot, incl, end, ne, r, t1, t2 = (sb(n, [P, B]) for n in ("tot", "incl", "end", "nonempty", "ratio", "work1", "work2"))
        ri = sb("ratio_i", [P, B], I32)
        zb = sb("zb", [P, B])
        vb = sb("carry_of_b", [B, 2, P], BF16)
        wl = sb("w_heads", [P, H * F])
        fc = sb("fc_rows", [P, 2 * F])
        fcb = sb("fcb_rows", [P, 1])
        prod = sb("w_times_fc", [P, 2 * H * F])
        v8 = sb("v8", [P, 2 * H])
        vblk = sb("vblk", [P, 4 * 2 * H])
        xt = sb("xt", [P, 2, P])
        a8 = sb("a8", [P, GROUPS * 4 * 2 * H])
        t0 = sb("t0_rows", [P, B * T0W])
        asr = sb("asrc_rows", [P, B * H])
        ps_a = ctx.enter_context(nc.psum_tensor("ps_a", [P, 512], F32))
        ps_b = ctx.enter_context(nc.psum_tensor("ps_b", [P, 512], F32))
        ps_v = ctx.enter_context(nc.psum_tensor("ps_v", [P, 512], F32))
        ps_t = [ctx.enter_context(nc.psum_tensor(f"ps_t{i}", [P, 512], F32)) for i in range(2)]
        ps_m = [ctx.enter_context(nc.psum_tensor(f"ps_m{i}", [P, 512], F32)) for i in range(2)]
        names = ("s_w", "s_pre", "s_used", "s_v", "s_vt", "s_vc", "s_vblk", "s_xt", "s_xc", "s_m", "s_mc", "s_rows", "s_st", "s_sc")
        s_w, s_pre, s_used, s_v, s_vt, s_vc, s_vblk, s_xt, s_xc, s_m, s_mc, s_rows, s_st, s_sc = (
            ctx.enter_context(nc.semaphore(n)) for n in names)
        block = ctx.enter_context(nc.Block())

        @block.sync
        def _(sp):
            for b in range(4):
                sp.dma_start(wl[b * F:(b + 1) * F, :].rearrange("f (h o) -> f h o", h=H),
                             w0.rearrange("h f o -> f h o")).then_inc(s_w, 16)
            sp.dma_start(fc[:, :], fc_w[0, :].partition_broadcast(P)).then_inc(s_w, 16)
            sp.dma_start(fcb[:, :], fc_b[:].partition_broadcast(P)).then_inc(s_w, 16)
            sp.wait_ge(s_vc, 2)
            for k in range(2):
                sp.dma_start(m.carry_row[k].rearrange("(b p) -> b p", p=P), vb[:, k, :]).then_inc(s_st, 16)
            sp.wait_ge(s_rows, 1)
            sp.dma_start(m.t0.rearrange("(b p) w -> p b w", p=P), t0[:, :].rearrange("p (b w) -> p b w", w=T0W)).then_inc(s_st, 16)
            sp.dma_start(m.asrc_t.rearrange("(b p) w -> p b w", p=P), asr[:, :].rearrange("p (b w) -> p b w", w=H)).then_inc(s_st, 16)
            sp.wait_ge(s_st, 64)

        @block.gpsimd
        def _(pool):
            pool.wait_ge(s_rows, 1)
            for b in range(B):
                pool.indirect_dma_start(out=m.asrc_at, out_offset=bass.IndirectOffsetOnAxis(ap=m.i_start[:, b:b + 1], axis=0),
                                        in_=asr[:, b * H:(b + 1) * H], in_offset=None,
                                        bounds_check=EP - 1, oob_is_err=False).then_inc(s_sc, 16)
            pool.wait_ge(s_sc, 16 * B)

        @block.vector
        def _(dve):
            dve.memset(zb[:, :], 0.0)
            dve.memset(m.x[:, B * F:GROUPS * 4 * F], 0.0)
            for k in range(2):
                dve.wait_ge(s_pre, k + 1)
                dve.tensor_copy(tot[:, :], ps_b[:, 0:B])
                dve.drain()
                dve.tensor_tensor_scan(incl[:, :], zb[:, :], tot[:, :], 0.0, ALU.add, ALU.add)
                dve.drain()
                dve.tensor_tensor(incl[:, :], incl[:, :], tot[:, :], ALU.subtract)
                dve.drain()
                dve.tensor_tensor(m.start[k][:, :], incl[:, :], ps_a[:, 0:B], ALU.add)
                dve.drain().then_inc(s_used, 1)
                dve.tensor_scalar(m.next[k][:, :], m.start[k][:, :], 1.0, None, ALU.add)
                dve.tensor_tensor(end[:, :], m.start[k][:, :], m.cnt[k][:, :], ALU.add)
                dve.tensor_scalar(ne[:, :], m.cnt[k][:, :], 1.0, None, ALU.min)
                dve.drain()
                dve.tensor_scalar(end[:, :], end[:, :], 1.0, None, ALU.subtract)
                dve.drain()
                dve.scalar_tensor_tensor(t1[:, :], end[:, :], float(EP), ne[:, :], ALU.subtract, ALU.mult)
                dve.drain()
                dve.tensor_scalar(m.i_end[k][:, :], t1[:, :], float(EP), None, ALU.add)
                dve.tensor_scalar(ri[:, :], end[:, :], 1.0 / J, None, ALU.mult)
                dve.drain()
                dve.tensor_copy(r[:, :], ri[:, :])
                dve.drain()
                dve.scalar_tensor_tensor(t1[:, :], r[:, :], float(J), end[:, :], ALU.mult, ALU.is_gt)
                dve.drain()
                dve.tensor_tensor(r[:, :], r[:, :], t1[:, :], ALU.subtract)
                dve.drain()
                dve.tensor_scalar(t1[:, :], r[:, :], 1.0, float(J), ALU.add, ALU.mult)
                dve.drain()
                dve.tensor_tensor(t1[:, :], t1[:, :], end[:, :], ALU.is_le)
                dve.drain()
                dve.tensor_tensor(r[:, :], r[:, :], t1[:, :], ALU.add)
                dve.drain()
                dve.scalar_tensor_tensor(t1[:, :], r[:, :], float(J), m.start[k][:, :], ALU.mult, ALU.is_gt)
                dve.drain()
                dve.tensor_tensor(m.has[k][:, :], t1[:, :], ne[:, :], ALU.mult)
                dve.drain()
                dve.scalar_tensor_tensor(t1[:, :], r[:, :], 1.0, m.has[k][:, :], ALU.add, ALU.mult)
                dve.drain()
                dve.tensor_scalar(t2[:, :], t1[:, :], 1.0, None, ALU.subtract)
                dve.drain().then_inc(s_v, 1)
                if k == 0:
                    dve.tensor_scalar(t1[:, :], ne[:, :], -1.0e6, 1.0e6, ALU.mult, ALU.add)
                    dve.drain()
                    dve.tensor_tensor(m.i_start[:, :], t1[:, :], m.start[k][:, :], ALU.add)
                    dve.drain()
                dve.wait_ge(s_vt, k + 1)
                dve.tensor_copy(vb[:, k, :], ps_v[0:B, k * P:(k + 1) * P])
                dve.drain().then_inc(s_vc, 1)
            dve.wait_ge(s_w, 96)
            for i in range(2):
                dve.tensor_tensor(prod[:, i * H * F:(i + 1) * H * F].rearrange("p (h o) -> p h o", h=H),
                                  wl[:, :].rearrange("p (h o) -> p h o", h=H),
                                  bcast(fc[:, i * F:(i + 1) * F], 1, H), ALU.mult)
            dve.memset(vblk[:, :], 0.0)
            dve.drain()
            dve.tensor_reduce(v8[:, :], prod[:, :].rearrange("p (h o) -> p h o", o=F), AX, ALU.add)
            dve.drain()
            for b in range(4):
                dve.tensor_copy(vblk[b * F:(b + 1) * F, b * 2 * H:(b + 1) * 2 * H], v8[b * F:(b + 1) * F, :])
            dve.drain().then_inc(s_vblk, 1)
            for g in range(GROUPS):
                dve.wait_ge(s_m, g + 1)
                dve.tensor_copy(a8[:, g * 8 * H:(g + 1) * 8 * H], ps_m[g % 2][:, 0:8 * H]).then_inc(s_mc, 1)
            dve.drain()
            a8v = a8[:, :].rearrange("p (b w) -> p b w", w=2 * H)
            t0v = t0[:, :].rearrange("p (b w) -> p b w", w=T0W)
            dve.tensor_copy(t0v[:, :, 0:F], m.x[:, 0:B * F].rearrange("p (b f) -> p b f", f=F))
            dve.tensor_copy(t0v[:, :, F:T0W], a8v[:, 0:B, H:2 * H])
            dve.tensor_scalar(asr[:, :].rearrange("p (b h) -> p b h", h=H), a8v[:, 0:B, 0:H], fcb[:, 0:1], None, ALU.add)
            dve.drain().then_inc(s_rows, 1)

        @block.tensor
        def _(pe):
            for k in range(2):
                if k == 1:
                    pe.wait_ge(s_used, 1)
                pe.matmul(ps_a[:, 0:B], m.above[:, :], m.cnt[k][:, :], start=True, stop=True)
                pe.matmul(ps_b[:, 0:B], m.ones[:, :], m.cnt[k][:, :], start=True, stop=True).then_inc(s_pre, 1)
                pe.wait_ge(s_v, k + 1)
                pe.transpose(ps_v[0:B, k * P:(k + 1) * P], t2[:, :], m.ident[:, :]).then_inc(s_vt, 1)
            pe.wait_ge(s_vblk, 1)
            for g in range(GROUPS):
                if g >= 2:
                    pe.wait_ge(s_xc, g - 1)
                pe.transpose(ps_t[g % 2][:, 0:P], m.x[:, g * P:(g + 1) * P], m.ident[:, :]).then_inc(s_xt, 1)
                if g >= 2:
                    pe.wait_ge(s_mc, g - 1)
                pe.wait_ge(s_xc, g + 1)
                pe.matmul(ps_m[g % 2][:, 0:8 * H], xt[:, g % 2, :], vblk[:, :], start=True, stop=True).then_inc(s_m, 1)

        @block.scalar
        def _(act):
            for g in range(GROUPS):
                if g >= 2:
                    act.wait_ge(s_m, g - 1)
                act.wait_ge(s_xt, g + 1)
                act.activation(xt[:, g % 2, :], ps_t[g % 2][:, 0:P], ACT.Copy).then_inc(s_xc, 1)


def stage_rank(nc, m):
    T = 16
    R = 4
    LAG = 2
    with ExitStack() as ctx:
        def sb(name, shape, dt=F32):
            return ctx.enter_context(nc.sbuf_tensor(name, shape, dt))
        krow = [[sb(f"krow{h}{k}", [P, T * P], I16) for k in range(2)] for h in range(2)]
        lrow = [[sb(f"lrow{h}{k}", [P, T * P], BF16) for k in range(2)] for h in range(2)]
        oat = [sb(f"lane_onehot_t{k}", [P, R, P]) for k in range(2)]
        oa = [sb(f"lane_onehot{k}", [P, R, P], BF16) for k in range(2)]
        ob = [sb(f"block_onehot{k}", [P, R, B], BF16) for k in range(2)]
        nxt = [sb(f"next_sb{k}", [P, 2, B]) for k in range(2)]
        junk = sb("junk", [P, R, 4, P], BF16)
        base = [sb(f"base{k}", [P, T]) for k in range(2)]
        rank = [sb(f"rank{k}", [P, T]) for k in range(2)]
        place = [sb(f"place{h}", [P, T], I32) for h in range(2)]
        recs = [sb(f"recs{h}", [P, T * REC]) for h in range(2)]
        ps_n = [ctx.enter_context(nc.psum_tensor(f"ps_next{k}", [P, 512], F32)) for k in range(2)]
        ps_f = [[ctx.enter_context(nc.psum_tensor(f"ps_fetch{k}{i}", [P, 512], F32)) for i in range(2)] for k in range(2)]
        def sem(n):
            return ctx.enter_context(nc.semaphore(n))
        s_row = [sem(f"s_row{h}") for h in range(2)]
        s_rowfree = sem("s_rowfree")
        s_hot, s_upd, s_cur, s_fet, s_sel = ([sem(f"{n}{k}") for k in range(2)] for n in ("s_hot", "s_upd", "s_cur", "s_fet", "s_sel"))
        s_rec = sem("s_rec")
        s_sent = [sem(f"s_sent{h}") for h in range(2)]
        block = ctx.enter_context(nc.Block())
        TURNS = J // (2 * T)

        @block.sync
        def _(sp):
            with sp.Fori(0, TURNS) as it:
                for h in range(2):
                    sp.wait_ge(s_rowfree, it * 2 + (h + 1))
                    sp.sem_inc(m.step_sp, 1)
                    for k in range(2):
                        for t, a in ((krow[h][k], m.keyrow[k]), (lrow[h][k], m.lorow[k])):
                            sp.dma_start(t[:, :], a[bass.ds((it * 2 + h) * (T * P), T * P)].partition_broadcast(P)).then_inc(s_row[h], 16)

        @block.gpsimd
        def _(pool):
            prime(pool, m, s_sent)
            with pool.Fori(0, TURNS) as it:
                for h in range(2):
                    pool.wait_ge(s_rec, it * 2 + (h + 1))
                    pool.sem_inc(m.step_pool, 1)
                    for t in range(T):
                        pool.indirect_dma_start(out=m.rec, out_offset=bass.IndirectOffsetOnAxis(ap=place[h][:, t:t + 1], axis=0),
                                                in_=recs[h][:, t * REC:(t + 1) * REC], in_offset=None).then_inc(s_sent[h], 16)
            for h in range(2):
                pool.wait_ge(s_sent[h], 16 + 16 * T * TURNS)

        @block.vector
        def _(dve):
            def make(n, h, t, c):
                s = t % R
                for k in range(2):
                    dve.wait_ge(s_upd[k], n + (t + 1))
                    dve.tensor_scalar(oat[k][:, s, :], lrow[h][k][:, t * P:(t + 1) * P], m.part[:, 0:1], None, ALU.is_equal)
                    dve.tensor_scalar(oa[k][:, s, :], m.lane_b[:, :], m.lo[k][:, bass.ds(c + t, 1)], None, ALU.is_equal)
                    dve.tensor_scalar(ob[k][:, s, :], m.lane_b[:, 0:B], m.hi[k][:, bass.ds(c + t, 1)], None, ALU.is_equal).then_inc(s_hot[k], 1)

            def select(n, h, t, c):
                for k in range(2):
                    dve.scalar_tensor_tensor(junk[:, t % R, 2 * k, :], krow[h][k][:, t * P:(t + 1) * P], m.key[k][:, bass.ds(c + t, 1)], m.below[:, :],
                                             ALU.is_equal, ALU.mult, accum_out=rank[k][:, t:t + 1])
                    dve.wait_ge(s_fet[k], n + (t + 1 + 2))
                    dve.scalar_tensor_tensor(junk[:, t % R, 2 * k + 1, 0:B], m.lane[:, 0:B], m.hi[k][:, bass.ds(c + t, 1)], ps_f[k][t % 2][:, 0:B],
                                             ALU.is_equal, ALU.mult, accum_out=base[k][:, t:t + 1]).then_inc(s_sel[k], 1)

            dve.sem_inc(s_rowfree, 2)
            for k in range(2):
                dve.sem_inc(s_sel[k], 2)
            with dve.Fori(0, TURNS) as it:
                for h in range(2):
                    n = (it * 2 + h) * T
                    dve.wait_ge(s_row[h], (it + 1) * 64)
                    dve.sem_inc(m.step_dve, 1)
                    for t in range(LAG):
                        make(n, h, t, n)
                    for t in range(T):
                        if t + LAG < T:
                            make(n, h, t + LAG, n)
                        select(n, h, t, n)
                    dve.drain().then_inc(s_rowfree, 1)
                    dve.wait_ge(s_sent[h], it * (16 * T) + 16)
                    dve.sem_inc(m.step_dve, 1)
                    rv = recs[h][:, :].rearrange("p (t w) -> p t w", w=REC)
                    ri = recs[h][:, :].bitcast(I32).rearrange("p (t w) -> p t w", w=REC)
                    dve.tensor_tensor(place[h][:, :], base[0][:, :], rank[0][:, :], ALU.add)
                    dve.tensor_tensor(ri[:, :, 4], base[1][:, :], rank[1][:, :], ALU.add)
                    dve.tensor_copy(rv[:, :, 0], m.key[0][:, bass.ds(n, T)])
                    dve.tensor_copy(rv[:, :, 1], m.key[1][:, bass.ds(n, T)])
                    dve.tensor_copy(rv[:, :, 2:4], m.attr[:, bass.ds(n * 2, 2 * T)].rearrange("p (t a) -> p t a", a=2))
                    dve.drain().then_inc(s_rec, 1)

        @block.tensor
        def _(pe):
            for k in range(2):
                pe.matmul(ps_n[k][:, 0:B], m.ident[:, :], m.next[k][:, :], start=True, stop=True).then_inc(s_upd[k], R)
                pe.sem_inc(s_fet[k], 2)
            with pe.Fori(0, J // T) as it:
                for t in range(T):
                    n = it * T + (t + 1)
                    for k in range(2):
                        pe.wait_ge(s_hot[k], n)
                        pe.wait_ge(s_cur[k], n)
                        pe.wait_ge(s_sel[k], n)
                        pe.sem_inc(m.step_pe, 1)
                        pe.matmul(ps_f[k][t % 2][:, 0:B], oat[k][:, t % R, :], nxt[k][:, t % 2, :], start=True, stop=True).then_inc(s_fet[k], 1)
                        pe.matmul(ps_n[k][:, 0:B], m.ident[:, :], nxt[k][:, t % 2, :], start=True, stop=False)
                        pe.matmul(ps_n[k][:, 0:B], oa[k][:, t % R, :], ob[k][:, t % R, :], start=False, stop=True).then_inc(s_upd[k], 1)

        @block.scalar
        def _(act):
            with act.Fori(0, J // 2) as it:
                for t in range(2):
                    for k in range(2):
                        act.wait_ge(s_upd[k], it * 2 + (R + t))
                        act.wait_ge(s_fet[k], it * 2 + (t + 1))
                        act.sem_inc(m.step_act, 1)
                        act.activation(nxt[k][:, t, :], ps_n[k][:, 0:B], ACT.Copy).then_inc(s_cur[k], 1)


def stage_attend(nc, m):
    TURNS = CHUNKS // 2
    with ExitStack() as ctx:
        def sb(name, shape, dt=F32):
            return ctx.enter_context(nc.sbuf_tensor(name, shape, dt))
        def sem(n):
            return ctx.enter_context(nc.semaphore(n))
        prev = sb("prev_key", [P, 1])
        pen = sb("pen", [P, J])
        first = sb("first_i", [P, 1], I32)
        first_a = sb("first_asrc", [P, H])
        asrc = sb("asrc_edges", [P, J * H])
        idx = sb("idx_dst", [P, J + 2 * C])
        ask = [sb(f"ask{h}", [P, C], I32) for h in range(2)]
        got = [sb(f"got{h}", [P, C * T0W]) for h in range(2)]
        sc = [sb(f"scanned{h}", [P, C * S0W]) for h in range(2)]
        e = sb("logits", [P, C * H])
        arg = sb("exp_args", [P, C * 2 * H])
        ex = sb("exps", [P, C * 2 * H])
        prod = sb("p_times_x", [P, C * H * F])
        s_load, s_first, s_begin = sem("s_load"), sem("s_first"), sem("s_begin")
        s_ask = sem("s_ask")
        s_got = [sem(f"s_got{h}") for h in range(2)]
        s_arg, s_exp, s_done = sem("s_arg"), sem("s_exp"), sem("s_done")
        s_put = [sem(f"s_put{h}") for h in range(2)]
        block = ctx.enter_context(nc.Block())
        rec3 = m.recs[:, :].rearrange("p (j w) -> p j w", w=REC)

        @block.sync
        def _(sp):
            prime(sp, m, s_put)
            sp.dma_start(m.recs[:, :], m.rec[1:EP + 1, :].rearrange("(p j) w -> p (j w)", p=P)).then_inc(s_load, 16)
            sp.dma_start(prev[:, :], m.rec[0:EP, :].rearrange("(p j) w -> p j w", p=P)[:, 0, 0:1], allow_slow_non_contiguous=True).then_inc(s_load, 16)
            sp.dma_start(asrc[:, :], m.asrc_at.rearrange("(p j) h -> p (j h)", p=P)).then_inc(s_load, 16)
            out = m.s0[0:EP, :].rearrange("(p j) w -> p (j w)", p=P)
            with sp.Fori(0, TURNS) as it:
                for h in range(2):
                    sp.wait_ge(s_done, it * 2 + (h + 1))
                    sp.sem_inc(m.step_sp, 1)
                    sp.dma_start(out[:, bass.ds((it * 2 + h) * (C * S0W), C * S0W)], sc[h][:, :]).then_inc(s_put[h], 16)
            for h in range(2):
                sp.wait_ge(s_put[h], 16 + 16 * TURNS)

        @block.gpsimd
        def _(pool):
            pool.wait_ge(s_first, 1)
            pool.indirect_dma_start(out=first_a[:, :], out_offset=None, in_=m.asrc_t,
                                    in_offset=bass.IndirectOffsetOnAxis(ap=first[:, 0:1], axis=0)).then_inc(s_begin, 16)
            with pool.Fori(0, TURNS) as it:
                for h in range(2):
                    pool.wait_ge(s_ask, it * 2 + (h + 1))
                    pool.sem_inc(m.step_pool, 1)
                    for c in range(C):
                        pool.indirect_dma_start(out=got[h][:, c * T0W:(c + 1) * T0W], out_offset=None, in_=m.t0,
                                                in_offset=bass.IndirectOffsetOnAxis(ap=ask[h][:, c:c + 1], axis=0)).then_inc(s_got[h], 16)

        @block.vector
        def _(dve):
            dve.memset(idx[:, :], 0.0)
            dve.memset(sc[1][:, :], 0.0)
            dve.drain()
            dve.memset(sc[1][:, C * S0W - H:C * S0W], -BIG)
            dve.wait_ge(s_load, 48)
            dve.tensor_copy(first[:, :], rec3[:, 0, 0:1])
            dve.drain().then_inc(s_first, 1)
            dve.tensor_copy(idx[:, 0:J], rec3[:, :, 1])
            dve.tensor_tensor(m.same[:, 1:J], rec3[:, 1:J, 0], rec3[:, 0:J - 1, 0], ALU.is_equal)
            dve.tensor_tensor(m.same[:, 0:1], rec3[:, 0, 0:1], prev[:, :], ALU.is_equal)
            dve.drain()
            for h in range(2):
                dve.tensor_copy(ask[h][:, :], idx[:, h * C:(h + 1) * C])
            dve.drain().then_inc(s_ask, 2)
            dve.tensor_scalar(pen[:, :], m.same[:, :], BIG, -BIG, ALU.mult, ALU.add)
            dve.tensor_reduce(m.whole[0][:, :], m.same[:, :], AX, ALU.min)
            dve.wait_ge(s_begin, 16)
            for k in range(H):
                dve.tensor_tensor_scan(asrc[:, k::H], m.same[:, :], asrc[:, k::H], first_a[:, k:k + 1], ALU.mult, ALU.add)
            dve.drain()
            with dve.Fori(0, TURNS) as it:
                for h in range(2):
                    n = it * 2 + h
                    g3 = got[h][:, :].rearrange("p (c w) -> p c w", w=T0W)
                    s3 = sc[h][:, :].rearrange("p (c w) -> p c w", w=S0W)
                    before = sc[1 - h][:, (C - 1) * S0W:C * S0W]
                    e3 = e[:, :].rearrange("p (c h) -> p c h", h=H)
                    a3 = arg[:, :].rearrange("p (c w) -> p c w", w=2 * H)
                    x3 = ex[:, :].rearrange("p (c w) -> p c w", w=2 * H)
                    M = S0W - H
                    dve.wait_ge(s_got[h], (it + 1) * (16 * C))
                    dve.wait_ge(s_put[h], (it + 1) * 16)
                    dve.sem_inc(m.step_dve, 1)
                    dve.tensor_tensor(e3, g3[:, :, F:T0W], asrc[:, bass.ds(n * (C * H), C * H)].rearrange("p (c h) -> p c h", h=H), ALU.add)
                    dve.drain()
                    dve.scalar_tensor_tensor(e[:, :], e[:, :], 0.2, e[:, :], ALU.mult, ALU.max)
                    dve.drain()
                    for k in range(H):
                        dve.tensor_tensor_scan(s3[:, :, M + k], pen[:, bass.ds(n * C, C)], e[:, k::H], before[:, M + k:M + k + 1], ALU.add, ALU.max)
                    dve.drain()
                    dve.tensor_tensor(a3[:, 1:C, 0:H], s3[:, 0:C - 1, M:S0W], s3[:, 1:C, M:S0W], ALU.subtract)
                    dve.tensor_tensor(a3[:, 0, 0:H], before[:, M:S0W], s3[:, 0, M:S0W], ALU.subtract)
                    dve.tensor_tensor(a3[:, :, H:2 * H], e3, s3[:, :, M:S0W], ALU.subtract)
                    dve.drain()
                    dve.tensor_scalar(arg[:, :], arg[:, :], 0.0, None, ALU.min)
                    dve.drain().then_inc(s_arg, 1)
                    dve.wait_ge(s_exp, n + 1)
                    dve.sem_inc(m.step_dve, 1)
                    dve.tensor_tensor(x3[:, :, 0:H], x3[:, :, 0:H], bcast(m.same[:, bass.ds(n * C, C)], 2, H), ALU.mult)
                    dve.tensor_tensor(prod[:, :].rearrange("p (c h f) -> p c h f", h=H, f=F),
                                      bcast(g3[:, :, 0:F], 2, H), bcast(x3[:, :, H:2 * H], 3, F), ALU.mult)
                    dve.drain()
                    for k in range(H):
                        dve.tensor_tensor_scan(s3[:, :, H * F + k], ex[:, k::2 * H], ex[:, H + k::2 * H], before[:, H * F + k:H * F + k + 1], ALU.mult, ALU.add)
                        for f in range(k * F, (k + 1) * F):
                            dve.tensor_tensor_scan(s3[:, :, f], ex[:, k::2 * H], prod[:, f::H * F], before[:, f:f + 1], ALU.mult, ALU.add)
                    dve.tensor_copy(ask[h][:, :], idx[:, bass.ds((n + 2) * C, C)])
                    dve.drain().then_inc(s_done, 1)
                    dve.sem_inc(s_ask, 1)
            dve.tensor_copy(m.fin[:, :], sc[1][:, (C - 1) * S0W:C * S0W])

        @block.scalar
        def _(act):
            with act.Fori(0, CHUNKS) as it:
                act.wait_ge(s_arg, it + 1)
                act.activation(ex[:, :], arg[:, :], ACT.Exp).then_inc(s_exp, 1)


def layer_norm(nc, m, dve, s_var, s_std, count):
    x3 = m.x[:, 0:B * F].rearrange("p (b f) -> p b f", f=F)
    q3 = m.sq[:, :].rearrange("p (b f) -> p b f", f=F)
    dve.tensor_reduce(m.mean[:, :], x3, AX, ALU.add)
    dve.drain()
    dve.tensor_scalar(m.mean[:, :], m.mean[:, :], 1.0 / F, None, ALU.mult)
    dve.drain()
    dve.tensor_tensor(x3, x3, bcast(m.mean[:, :], 2, F), ALU.subtract)
    dve.drain()
    dve.tensor_tensor(m.sq[:, :], m.x[:, 0:B * F], m.x[:, 0:B * F], ALU.mult)
    dve.drain()
    dve.tensor_reduce(m.var[:, :], q3, AX, ALU.add)
    dve.drain().then_inc(s_var, 1)
    dve.wait_ge(s_std, count)
    dve.reciprocal(m.std[:, :], m.std[:, :])
    dve.drain()
    dve.tensor_tensor(x3, x3, bcast(m.std[:, :], 2, F), ALU.mult)
    dve.drain()


def root(nc, m, act, s_var, s_std, count):
    act.wait_ge(s_var, count)
    act.activation(m.std[:, :], m.var[:, :], ACT.Sqrt, bias=m.eps[:, 0:1], scale=1.0 / F).then_inc(s_std, 1)


def stage_attend_nodes(nc, m, w0, bias0):
    HALF = B // 2
    HF = H * F
    with ExitStack() as ctx:
        def sb(name, shape, dt=F32):
            return ctx.enter_context(nc.sbuf_tensor(name, shape, dt))
        def sem(n):
            return ctx.enter_context(nc.semaphore(n))
        rep = sb("rep", [P, 3, HF])
        tr = sb("tr", [P, 4, P])
        mc = sb("mc", [P, P])
        dg = sb("dg", [P, 2, P])
        edg = sb("edg", [P, 2, P])
        gs = sb("gs", [P, 2, P])
        shifted = sb("shifted", [P, 3, P])
        table = sb("carry_table", [P, S0W])
        row = sb("carry_row_sb", [P, NN], BF16)
        sel = sb("sel", [P, 4, P])
        ge = sb("ends", [P, HALF * S0W])
        ce = sb("carries", [P, HALF * S0W])
        mm = sb("mm", [P, 3, HALF * H])
        arg = sb("arg2", [P, 2, HALF * H])
        ex = sb("ex2", [P, 2, HALF * H])
        at = sb("agg_t", [P, 2, P])
        ws = sb("w_stacked", [HF, F])
        bs = sb("bias_rows", [P, F])
        ps_t = ctx.enter_context(nc.psum_tensor("ps_tr", [P, 4 * P], F32))
        ps_b = ctx.enter_context(nc.psum_tensor("ps_back", [P, 3 * P], F32))
        ps_c = [ctx.enter_context(nc.psum_tensor(f"ps_c{i}", [P, 512], F32)) for i in range(2)]
        ps_a = [ctx.enter_context(nc.psum_tensor(f"ps_at{i}", [P, 512], F32)) for i in range(2)]
        ps_o = [ctx.enter_context(nc.psum_tensor(f"ps_o{i}", [P, 512], F32)) for i in range(2)]
        (s_w, s_end, s_rep, s_tr, s_dg, s_edg, s_shift, s_back, s_tab, s_sel, s_cps, s_cc, s_arg, s_ex, s_agg, s_at, s_atc,
         s_o, s_oc, s_var, s_std) = (sem(n) for n in (
             "s_w", "s_end", "s_rep", "s_tr", "s_dg", "s_edg", "s_shift", "s_back", "s_tab", "s_sel", "s_cps", "s_cc", "s_arg", "s_ex",
             "s_agg", "s_at", "s_atc", "s_o", "s_oc", "s_var", "s_std"))
        block = ctx.enter_context(nc.Block())

        @block.sync
        def _(sp):
            sp.dma_start(ws[:, :], w0.rearrange("h f o -> (h f) o")).then_inc(s_w, 16)
            sp.dma_start(bs[:, :], bias0.partition_broadcast(P)).then_inc(s_w, 16)
            sp.dma_start(row[:, :], m.carry_row[0].partition_broadcast(P)).then_inc(s_w, 16)
            sp.wait_ge(s_w, 48)

        @block.gpsimd
        def _(pool):
            for b in range(B):
                if b == HALF:
                    pool.wait_ge(s_agg, 1)
                o = b % HALF
                pool.indirect_dma_start(out=ge[:, o * S0W:(o + 1) * S0W], out_offset=None, in_=m.s0,
                                        in_offset=bass.IndirectOffsetOnAxis(ap=m.i_end[0][:, b:b + 1], axis=0)).then_inc(s_end, 16)

        @block.vector
        def _(dve):
            for i in range(2):
                dve.tensor_copy(rep[:, i, :].rearrange("p (h f) -> p h f", f=F), bcast(m.fin[:, HF + i * H:HF + (i + 1) * H], 2, F))
            dve.tensor_copy(rep[:, 2, :], m.whole[0][:, 0:1].broadcast_to([P, HF]))
            dve.drain().then_inc(s_rep, 1)
            dve.wait_ge(s_tr, 1)
            dve.tensor_copy(tr[:, :, :], ps_t[:, :].rearrange("p (a q) -> p a q", q=P))
            dve.drain()
            dve.tensor_scalar(dg[:, 0, :], tr[:, 3, :], BIG, -BIG, ALU.mult, ALU.add)
            dve.drain()
            dve.tensor_tensor_scan(mc[:, :], dg[:, 0, :], tr[:, 2, :], -BIG, ALU.add, ALU.max)
            dve.drain()
            dve.memset(dg[:, 0, 0:1], 0.0)
            dve.tensor_tensor(dg[:, 0, 1:P], mc[:, 0:P - 1], mc[:, 1:P], ALU.subtract)
            dve.tensor_tensor(dg[:, 1, :], tr[:, 2, :], mc[:, :], ALU.subtract)
            dve.drain()
            dve.tensor_scalar(dg[:, :, :], dg[:, :, :], 0.0, None, ALU.min)
            dve.drain().then_inc(s_dg, 1)
            dve.wait_ge(s_edg, 1)
            dve.tensor_tensor(edg[:, 0, :], edg[:, 0, :], tr[:, 3, :], ALU.mult)
            for i in range(2):
                dve.tensor_tensor(gs[:, i, :], tr[:, i, :], edg[:, 1, :], ALU.mult)
            dve.drain()
            for i in range(2):
                dve.tensor_tensor_scan(tr[:, i, :], edg[:, 0, :], gs[:, i, :], 0.0, ALU.mult, ALU.add)
            dve.memset(shifted[:, :, 0:1], 0.0)
            dve.drain()
            for i in range(2):
                dve.tensor_copy(shifted[:, i, 1:P], tr[:, i, 0:P - 1])
            dve.tensor_copy(shifted[:, 2, 1:P], mc[:, 0:P - 1])
            dve.drain().then_inc(s_shift, 1)
            dve.wait_ge(s_back, 1)
            dve.tensor_copy(table[:, 0:HF], ps_b[:, 0:P])
            for i in range(2):
                dve.tensor_copy(table[:, HF + i * H:HF + (i + 1) * H], ps_b[:, (i + 1) * P:(i + 2) * P:F])
            dve.drain().then_inc(s_tab, 1)
            dve.wait_ge(s_w, 48)
            x3 = m.x[:, 0:B * F].rearrange("p (b f) -> p b f", f=F)
            dve.tensor_tensor(x3, x3, bcast(bs[:, :], 1, B), ALU.add)
            for half in range(2):
                for b in range(half * HALF, (half + 1) * HALF):
                    if b >= 4:
                        dve.wait_ge(s_cps, b - 3)
                    dve.tensor_scalar(sel[:, b % 4, :], row[:, b * P:(b + 1) * P], m.part[:, 0:1], None, ALU.is_equal).then_inc(s_sel, 1)
                dve.wait_ge(s_cc, (half + 1) * HALF)
                dve.wait_ge(s_end, 16 * B if half else 16 * HALF)
                g3 = ge[:, :].rearrange("p (b w) -> p b w", w=S0W)
                c3 = ce[:, :].rearrange("p (b w) -> p b w", w=S0W)
                a3 = [arg[:, i, :].rearrange("p (b h) -> p b h", h=H) for i in range(2)]
                x2 = [ex[:, i, :].rearrange("p (b h) -> p b h", h=H) for i in range(2)]
                m3 = [mm[:, i, :].rearrange("p (b h) -> p b h", h=H) for i in range(3)]
                has = m.has[0][:, half * HALF:(half + 1) * HALF]
                M = HF + H
                dve.tensor_scalar(mm[:, 2, 0:HALF], has, BIG, -BIG, ALU.mult, ALU.add)
                dve.drain()
                dve.tensor_tensor(m3[0], c3[:, :, M:S0W], bcast(mm[:, 2, 0:HALF], 2, H), ALU.add)
                dve.drain()
                dve.tensor_tensor(m3[1], m3[0], g3[:, :, M:S0W], ALU.max)
                dve.drain()
                dve.tensor_tensor(a3[0], g3[:, :, M:S0W], m3[1], ALU.subtract)
                dve.tensor_tensor(a3[1], m3[0], m3[1], ALU.subtract)
                dve.drain().then_inc(s_arg, 1)
                dve.wait_ge(s_ex, half + 1)
                for i, t in enumerate((g3, c3)):
                    dve.tensor_tensor(t[:, :, HF:M], t[:, :, HF:M], x2[i], ALU.mult)
                    for k in range(H):
                        v = t[:, :, k * F:(k + 1) * F]
                        dve.tensor_tensor(v, v, bcast(x2[i][:, :, k], 2, F), ALU.mult)
                dve.drain()
                dve.tensor_tensor(g3[:, :, 0:M], g3[:, :, 0:M], c3[:, :, 0:M], ALU.add)
                dve.drain()
                dve.tensor_scalar(m3[2], g3[:, :, HF:M], 1.0e-30, float(H), ALU.max, ALU.mult)
                dve.drain()
                dve.reciprocal(mm[:, 2, :], mm[:, 2, :])
                dve.drain()
                if half == 1:
                    dve.wait_ge(s_at, HALF)
                for k in range(H):
                    dve.tensor_tensor(c3[:, :, k * F:(k + 1) * F], g3[:, :, k * F:(k + 1) * F], bcast(m3[2][:, :, k], 2, F), ALU.mult)
                dve.drain().then_inc(s_agg, 1)
                for b in range(half * HALF, (half + 1) * HALF):
                    dve.wait_ge(s_o, b + 1)
                    dve.tensor_tensor(m.x[:, b * F:(b + 1) * F], m.x[:, b * F:(b + 1) * F], ps_o[b % 2][:, 0:F], ALU.add).then_inc(s_oc, 1)
            dve.drain()
            layer_norm(nc, m, dve, s_var, s_std, 1)

        @block.tensor
        def _(pe):
            pe.wait_ge(s_rep, 1)
            pe.transpose(ps_t[:, 0:P], m.fin[:, 0:HF], m.ident[:, :])
            pe.transpose(ps_t[:, P:2 * P], rep[:, 0, :], m.ident[:, :])
            pe.transpose(ps_t[:, 2 * P:3 * P], rep[:, 1, :], m.ident[:, :])
            pe.transpose(ps_t[:, 3 * P:4 * P], rep[:, 2, :], m.ident[:, :]).then_inc(s_tr, 1)
            pe.wait_ge(s_shift, 1)
            for i in range(3):
                last = pe.transpose(ps_b[:, i * P:(i + 1) * P], shifted[:, i, :], m.ident[:, :])
            last.then_inc(s_back, 1)
            pe.wait_ge(s_tab, 1)
            pe.wait_ge(s_w, 48)
            for half in range(2):
                for b in range(half * HALF, (half + 1) * HALF):
                    pe.wait_ge(s_sel, b + 1)
                    if b >= 2:
                        pe.wait_ge(s_cc, b - 1)
                    pe.matmul(ps_c[b % 2][:, 0:S0W], sel[:, b % 4, :], table[:, :], start=True, stop=True).then_inc(s_cps, 1)
                pe.wait_ge(s_agg, half + 1)
                for b in range(half * HALF, (half + 1) * HALF):
                    o = b % HALF
                    if b >= 2:
                        pe.wait_ge(s_atc, b - 1)
                    pe.transpose(ps_a[b % 2][:, 0:P], ce[:, o * S0W:o * S0W + HF], m.ident[:, :]).then_inc(s_at, 1)
                    pe.wait_ge(s_atc, b + 1)
                    if b >= 2:
                        pe.wait_ge(s_oc, b - 1)
                    pe.matmul(ps_o[b % 2][:, 0:F], at[:, b % 2, :], ws[:, :], start=True, stop=True).then_inc(s_o, 1)

        @block.scalar
        def _(act):
            act.wait_ge(s_dg, 1)
            act.activation(edg[:, :, :], dg[:, :, :], ACT.Exp).then_inc(s_edg, 1)
            for half in range(2):
                if half == 1:
                    act.wait_ge(s_at, HALF)
                for b in range(half * HALF, (half + 1) * HALF):
                    o = b % HALF
                    act.wait_ge(s_cps, b + 1)
                    act.activation(ce[:, o * S0W:(o + 1) * S0W], ps_c[b % 2][:, 0:S0W], ACT.Copy).then_inc(s_cc, 1)
                act.wait_ge(s_arg, half + 1)
                act.activation(ex[:, :, :], arg[:, :, :], ACT.Exp).then_inc(s_ex, 1)
                for b in range(half * HALF, (half + 1) * HALF):
                    if b >= 2:
                        act.wait_ge(s_o, b - 1)
                    act.wait_ge(s_at, b + 1)
                    act.activation(at[:, b % 2, :], ps_a[b % 2][:, 0:P], ACT.Copy).then_inc(s_atc, 1)
            root(nc, m, act, s_var, s_std, 1)


def stage_spline_table(nc, m, w1):
    K = 16
    with ExitStack() as ctx:
        def sb(name, shape, dt=F32):
            return ctx.enter_context(nc.sbuf_tensor(name, shape, dt))
        def sem(n):
            return ctx.enter_context(nc.semaphore(n))
        wp = sb("w_padded", [P, 4, K * F])
        xt = sb("xt1", [P, 2, P])
        rows = [sb(f"t1_rows{i}", [P, CELLS * T1W]) for i in range(4)]
        ps_t = [ctx.enter_context(nc.psum_tensor(f"ps_t1{i}", [P, 512], F32)) for i in range(2)]
        ps_y = [ctx.enter_context(nc.psum_tensor(f"ps_y{i}", [P, 512], F32)) for i in range(4)]
        s_zero, s_w, s_xt, s_xc, s_y = (sem(n) for n in ("s_zero", "s_w", "s_xt", "s_xc", "s_y"))
        s_copied = [sem("s_copied_act"), sem("s_copied_dve")]
        s_out = [sem(f"s_out{i}") for i in range(4)]
        block = ctx.enter_context(nc.Block())

        def corners(b):
            t = rows[b % 4][:, :].rearrange("p (u v k o) -> p u v k o", u=3, v=3, k=4)
            y = ps_y[b % 4][:, :].rearrange("p (u v o) -> p u v o", u=4, v=4)
            for i in range(2):
                for j in range(2):
                    yield t[:, :, :, i * 2 + j, :], y[:, i:i + 3, j:j + 3, :]

        @block.sync
        def _(sp):
            sp.wait_ge(s_zero, 1)
            for b in range(4):
                sp.dma_start(wp[b * F:(b + 1) * F, b, :].rearrange("f (k o) -> f k o", o=F),
                             w1.rearrange("u v f o -> f (u v) o")).then_inc(s_w, 16)
            for b in range(B):
                sp.wait_ge(s_copied[b % 2], b // 2 + 1)
                sp.dma_start(m.t1[b * P * CELLS:(b + 1) * P * CELLS, :].rearrange("(p c) w -> p (c w)", c=CELLS),
                             rows[b % 4][:, :]).then_inc(s_out[b % 4], 16)
            for i in range(4):
                sp.wait_ge(s_out[i], 16 * len(range(i, B, 4)))

        @block.vector
        def _(dve):
            dve.memset(wp[:, :, :], 0.0).then_inc(s_zero, 1)
            for b in range(1, B, 2):
                dve.wait_ge(s_y, b + 1)
                if b >= 4:
                    dve.wait_ge(s_out[b % 4], 16 * (b // 4))
                for o, i in corners(b):
                    last = dve.tensor_copy(o, i)
                last.then_inc(s_copied[1], 1)

        @block.scalar
        def _(act):
            for b in range(0, B, 2):
                if b % 4 == 0:
                    g = b // 4
                    act.wait_ge(s_xt, g + 1)
                    act.activation(xt[:, g % 2, :], ps_t[g % 2][:, 0:P], ACT.Copy).then_inc(s_xc, 1)
                act.wait_ge(s_y, b + 1)
                if b >= 4:
                    act.wait_ge(s_out[b % 4], 16 * (b // 4))
                for o, i in corners(b):
                    last = act.activation(o, i, ACT.Copy)
                last.then_inc(s_copied[0], 1)

        @block.tensor
        def _(pe):
            pe.wait_ge(s_w, 64)
            for g in range(GROUPS):
                if g >= 2:
                    pe.wait_ge(s_xc, g - 1)
                pe.transpose(ps_t[g % 2][:, 0:P], m.x[:, g * P:(g + 1) * P], m.ident[:, :]).then_inc(s_xt, 1)
                pe.wait_ge(s_xc, g + 1)
                for b in range(4 * g, min(4 * g + 4, B)):
                    if b >= 4:
                        pe.wait_ge(s_copied[b % 2], b // 2 - 1)
                    pe.matmul(ps_y[b % 4][:, :], xt[:, g % 2, :], wp[:, b % 4, :], start=True, stop=True).then_inc(s_y, 1)


def stage_spline(nc, m):
    TURNS = CHUNKS // 2
    with ExitStack() as ctx:
        def sb(name, shape, dt=F32):
            return ctx.enter_context(nc.sbuf_tensor(name, shape, dt))
        def sem(n):
            return ctx.enter_context(nc.semaphore(n))
        cell, up, t = sb("cell", [P, J]), sb("up", [P, J]), sb("t_sp", [P, J])
        tent = [[sb(f"tent{a}{i}", [P, J]) for i in range(2)] for a in range(2)]
        w4 = sb("w4", [P, J * 4])
        idx = sb("idx_cell", [P, J + 2 * C])
        ask = [sb(f"ask1{h}", [P, C], I32) for h in range(2)]
        got = [sb(f"got1{h}", [P, C * T1W]) for h in range(2)]
        sc = [sb(f"scanned1{h}", [P, C * F]) for h in range(2)]
        msg = sb("msg", [P, C * F])
        s_ask, s_done = sem("s_ask"), sem("s_done")
        s_got = [sem(f"s_got{h}") for h in range(2)]
        s_put = [sem(f"s_put{h}") for h in range(2)]
        block = ctx.enter_context(nc.Block())
        rec3 = m.recs[:, :].rearrange("p (j w) -> p j w", w=REC)
        step = 2.0 / 3.0

        @block.sync
        def _(sp):
            prime(sp, m, s_put)
            out = m.s1[0:EP, :].rearrange("(p j) w -> p (j w)", p=P)
            with sp.Fori(0, TURNS) as it:
                for h in range(2):
                    sp.wait_ge(s_done, it * 2 + (h + 1))
                    sp.sem_inc(m.step_sp, 1)
                    sp.dma_start(out[:, bass.ds((it * 2 + h) * (C * F), C * F)], sc[h][:, :]).then_inc(s_put[h], 16)
            for h in range(2):
                sp.wait_ge(s_put[h], 16 + 16 * TURNS)

        @block.gpsimd
        def _(pool):
            with pool.Fori(0, TURNS) as it:
                for h in range(2):
                    pool.wait_ge(s_ask, it * 2 + (h + 1))
                    pool.sem_inc(m.step_pool, 1)
                    for c in range(C):
                        pool.indirect_dma_start(out=got[h][:, c * T1W:(c + 1) * T1W], out_offset=None, in_=m.t1,
                                                in_offset=bass.IndirectOffsetOnAxis(ap=ask[h][:, c:c + 1], axis=0)).then_inc(s_got[h], 16)

        @block.vector
        def _(dve):
            dve.memset(idx[:, :], 0.0)
            dve.memset(sc[1][:, :], 0.0)
            dve.drain()
            dve.tensor_scalar(idx[:, 0:J], rec3[:, :, 1], float(CELLS), None, ALU.mult)
            dve.drain()
            for a in range(2):
                u = rec3[:, :, 2 + a]
                dve.tensor_scalar(cell[:, :], u, -1.0 + step, None, ALU.is_ge)
                dve.tensor_scalar(up[:, :], u, -1.0 + 2 * step, None, ALU.is_ge)
                dve.drain()
                dve.tensor_tensor(cell[:, :], cell[:, :], up[:, :], ALU.add)
                dve.drain()
                dve.scalar_tensor_tensor(idx[:, 0:J], cell[:, :], float(3 if a == 0 else 1), idx[:, 0:J], ALU.mult, ALU.add)
                for i in range(2):
                    dve.tensor_scalar(t[:, :], cell[:, :], step, -1.0 + step * i, ALU.mult, ALU.add)
                    dve.drain()
                    dve.tensor_tensor(t[:, :], u, t[:, :], ALU.subtract)
                    dve.drain()
                    dve.scalar_tensor_tensor(t[:, :], t[:, :], -1.0, t[:, :], ALU.mult, ALU.max)
                    dve.drain()
                    dve.tensor_scalar(t[:, :], t[:, :], -1.0 / step, 1.0, ALU.mult, ALU.add)
                    dve.drain()
                    dve.tensor_scalar(tent[a][i][:, :], t[:, :], 0.0, None, ALU.max)
                    dve.drain()
            for h in range(2):
                dve.tensor_copy(ask[h][:, :], idx[:, h * C:(h + 1) * C])
            dve.drain().then_inc(s_ask, 2)
            for i in range(2):
                for j in range(2):
                    dve.tensor_tensor(w4[:, i * 2 + j::4], tent[0][i][:, :], tent[1][j][:, :], ALU.mult)
            dve.drain()
            with dve.Fori(0, TURNS) as it:
                for h in range(2):
                    n = it * 2 + h
                    dve.wait_ge(s_got[h], (it + 1) * (16 * C))
                    dve.wait_ge(s_put[h], (it + 1) * 16)
                    dve.sem_inc(m.step_dve, 1)
                    g3 = got[h][:, :].rearrange("p (c f) -> p c f", f=F)
                    dve.tensor_tensor(g3, g3, bcast(w4[:, bass.ds(n * (C * 4), C * 4)], 2, F), ALU.mult)
                    dve.drain()
                    dve.tensor_reduce(msg[:, :].rearrange("p (c f) -> p c f", f=F),
                                      got[h][:, :].rearrange("p (c k f) -> p c f k", k=4, f=F), AX, ALU.add)
                    dve.drain()
                    for f in range(F):
                        dve.tensor_tensor_scan(sc[h][:, f::F], m.same[:, bass.ds(n * C, C)], msg[:, f::F],
                                               sc[1 - h][:, (C - 1) * F + f:(C - 1) * F + f + 1], ALU.mult, ALU.add)
                    dve.tensor_copy(ask[h][:, :], idx[:, bass.ds((n + 2) * C, C)])
                    dve.drain().then_inc(s_done, 1)
                    dve.sem_inc(s_ask, 1)
            dve.tensor_copy(m.fin[:, 0:F], sc[1][:, (C - 1) * F:C * F])


def node_sums(nc, m, ctx, block, k, sums, then_dve, then_pe, then_act, then_sp=None, loads=0, s_w=None):
    def sb(name, shape, dt=F32):
        return ctx.enter_context(nc.sbuf_tensor(f"{name}{k}", shape, dt))
    def sem(n):
        return ctx.enter_context(nc.semaphore(n))
    PER = 16
    banks = -(-B // PER)
    rep = sb("rep_s", [P, F])
    tr = sb("tr_s", [F, 2, P])
    shifted = sb("shifted_s", [F, P])
    table = sb("table_s", [P, F])
    row = sb("row_s", [P, NN], BF16)
    sel = sb("sel_s", [P, 4, P])
    ge = sb("ends_s", [P, B * F])
    ps_t = ctx.enter_context(nc.psum_tensor(f"ps_ts{k}", [P, 512], F32))
    ps_c = [ctx.enter_context(nc.psum_tensor(f"ps_cs{k}{i}", [P, 512], F32)) for i in range(2)]
    s_row, s_end, s_rep, s_tr, s_shift, s_back, s_tab, s_sel, s_cps, s_cc = (sem(n) for n in (
        "s_row", "s_end", "s_rep", "s_tr", "s_shift", "s_back", "s_tab", "s_sel", "s_cps", "s_cc"))

    @block.sync
    def _(sp):
        sp.dma_start(row[:, :], m.carry_row[k].partition_broadcast(P)).then_inc(s_row, 16)
        sp.wait_ge(s_row, 16)
        if then_sp:
            then_sp(sp)

    @block.gpsimd
    def _(pool):
        for b in range(B):
            pool.indirect_dma_start(out=ge[:, b * F:(b + 1) * F], out_offset=None, in_=sums,
                                    in_offset=bass.IndirectOffsetOnAxis(ap=m.i_end[k][:, b:b + 1], axis=0)).then_inc(s_end, 16)

    @block.vector
    def _(dve):
        dve.tensor_copy(rep[:, :], m.whole[k][:, 0:1].broadcast_to([P, F]))
        dve.drain().then_inc(s_rep, 1)
        dve.wait_ge(s_tr, 1)
        dve.tensor_copy(tr[:, :, :], ps_t[0:F, 0:2 * P].rearrange("p (a q) -> p a q", q=P))
        dve.memset(shifted[:, 0:1], 0.0)
        dve.drain()
        dve.tensor_tensor_scan(shifted[:, 1:P], tr[:, 1, 0:P - 1], tr[:, 0, 0:P - 1], 0.0, ALU.mult, ALU.add)
        dve.drain().then_inc(s_shift, 1)
        dve.wait_ge(s_back, 1)
        dve.tensor_copy(table[:, :], ps_t[:, 2 * P:2 * P + F])
        dve.drain().then_inc(s_tab, 1)
        dve.wait_ge(s_row, 16)
        for b in range(B):
            if b >= 4:
                dve.wait_ge(s_cps, b - 3)
            dve.tensor_scalar(sel[:, b % 4, :], row[:, b * P:(b + 1) * P], m.part[:, 0:1], None, ALU.is_equal).then_inc(s_sel, 1)
            if (b + 1) % PER == 0 or b == B - 1:
                q, w = b // PER, (b % PER + 1) * F
                dve.wait_ge(s_end, 16 * B)
                dve.wait_ge(s_cps, b + 1)
                g = ge[:, q * PER * F:q * PER * F + w]
                dve.tensor_tensor(g, g, ps_c[q % 2][:, 0:w], ALU.add).then_inc(s_cc, 1)
        dve.drain()
        then_dve(dve, ge)

    @block.tensor
    def _(pe):
        pe.wait_ge(s_rep, 1)
        pe.transpose(ps_t[0:F, 0:P], m.fin[:, 0:F], m.ident[:, :])
        pe.transpose(ps_t[0:F, P:2 * P], rep[:, :], m.ident[:, :]).then_inc(s_tr, 1)
        pe.wait_ge(s_shift, 1)
        pe.transpose(ps_t[:, 2 * P:2 * P + F], shifted[:, :], m.ident[0:F, 0:F]).then_inc(s_back, 1)
        pe.wait_ge(s_tab, 1)
        for b in range(B):
            q = b // PER
            pe.wait_ge(s_sel, b + 1)
            if b % PER == 0 and q >= 2:
                pe.wait_ge(s_cc, q - 1)
            pe.matmul(ps_c[q % 2][:, (b % PER) * F:(b % PER + 1) * F], sel[:, b % 4, :], table[:, :], start=True, stop=True).then_inc(s_cps, 1)
        then_pe(pe)

    @block.scalar
    def _(act):
        then_act(act)


def stage_spline_nodes(nc, m):
    with ExitStack() as ctx:
        s_var = ctx.enter_context(nc.semaphore("s_var"))
        s_std = ctx.enter_context(nc.semaphore("s_std"))
        block = ctx.enter_context(nc.Block())

        def dve_part(dve, ge):
            dve.tensor_tensor(m.x[:, 0:B * F], m.x[:, 0:B * F], ge[:, :], ALU.add)
            dve.drain()
            layer_norm(nc, m, dve, s_var, s_std, 1)
            x3 = m.x[:, 0:B * F].rearrange("p (b f) -> p b f", f=F)
            q3 = m.sq[:, :].rearrange("p (b f) -> p b f", f=F)
            dve.tensor_tensor(q3, x3, bcast(m.sumw[:, :], 2, F), ALU.mult)
            dve.drain()
            dve.tensor_tensor(m.x[:, 0:B * F], m.x[:, 0:B * F], m.sq[:, :], ALU.add)
            dve.drain()
            layer_norm(nc, m, dve, s_var, s_std, 2)

        def act_part(act):
            root(nc, m, act, s_var, s_std, 1)
            root(nc, m, act, s_var, s_std, 2)

        node_sums(nc, m, ctx, block, 0, m.s1, dve_part, lambda pe: None, act_part)


def stage_starts(nc, m):
    with ExitStack() as ctx:
        s_sc = ctx.enter_context(nc.semaphore("s_sc"))
        s_x = ctx.enter_context(nc.semaphore("s_x"))
        block = ctx.enter_context(nc.Block())

        @block.sync
        def _(sp):
            sp.dma_start(m.x3t.rearrange("(b p) f -> p b f", p=P), m.x[:, 0:B * F].rearrange("p (b f) -> p b f", f=F)).then_inc(s_x, 16)
            sp.wait_ge(s_x, 16)

        @block.gpsimd
        def _(pool):
            for b in range(B):
                pool.indirect_dma_start(out=m.h3, out_offset=bass.IndirectOffsetOnAxis(ap=m.i_start[:, b:b + 1], axis=0),
                                        in_=m.x[:, b * F:(b + 1) * F], in_offset=None,
                                        bounds_check=EP - 1, oob_is_err=False).then_inc(s_sc, 16)
            pool.wait_ge(s_sc, 16 * B)


def stage_exchange(nc, m):
    TURNS = CHUNKS // 2
    with ExitStack() as ctx:
        def sb(name, shape, dt=F32):
            return ctx.enter_context(nc.sbuf_tensor(name, shape, dt))
        def sem(n):
            return ctx.enter_context(nc.semaphore(n))
        first = sb("first3", [P, 1], I32)
        first_x = sb("first_x", [P, F])
        starts = [sb(f"starts{h}", [P, C * F]) for h in range(2)]
        rows = [sb(f"xd_rows{h}", [P, C * XDW]) for h in range(2)]
        to = [sb(f"to{h}", [P, C], I32) for h in range(2)]
        s_first, s_begin, s_done, s_free = (sem(n) for n in ("s_first", "s_begin", "s_done", "s_free"))
        s_in = [sem(f"s_in{h}") for h in range(2)]
        s_sent = [sem(f"s_sent{h}") for h in range(2)]
        block = ctx.enter_context(nc.Block())
        rec3 = m.recs[:, :].rearrange("p (j w) -> p j w", w=REC)
        reci = m.recs[:, :].bitcast(I32)

        @block.sync
        def _(sp):
            src = m.h3.rearrange("(p j) f -> p (j f)", p=P)
            with sp.Fori(0, TURNS) as it:
                for h in range(2):
                    sp.wait_ge(s_free, it * 2 + (h + 1))
                    sp.sem_inc(m.step_sp, 1)
                    sp.dma_start(starts[h][:, :], src[:, bass.ds((it * 2 + h) * (C * F), C * F)]).then_inc(s_in[h], 16)

        @block.gpsimd
        def _(pool):
            prime(pool, m, s_sent)
            pool.wait_ge(s_first, 1)
            pool.indirect_dma_start(out=first_x[:, :], out_offset=None, in_=m.x3t,
                                    in_offset=bass.IndirectOffsetOnAxis(ap=first[:, 0:1], axis=0)).then_inc(s_begin, 16)
            with pool.Fori(0, TURNS) as it:
                for h in range(2):
                    pool.wait_ge(s_done, it * 2 + (h + 1))
                    pool.sem_inc(m.step_pool, 1)
                    for c in range(C):
                        pool.indirect_dma_start(out=m.xd, out_offset=bass.IndirectOffsetOnAxis(ap=to[h][:, c:c + 1], axis=0),
                                                in_=rows[h][:, c * XDW:(c + 1) * XDW], in_offset=None).then_inc(s_sent[h], 16)
            for h in range(2):
                pool.wait_ge(s_sent[h], 16 + 16 * C * TURNS)

        @block.vector
        def _(dve):
            dve.sem_inc(s_free, 2)
            dve.tensor_copy(first[:, :], rec3[:, 0, 0:1])
            dve.drain().then_inc(s_first, 1)
            dve.wait_ge(s_begin, 16)
            dve.tensor_copy(rows[1][:, (C - 1) * XDW:(C - 1) * XDW + F], first_x[:, :])
            dve.drain()
            with dve.Fori(0, TURNS) as it:
                for h in range(2):
                    n = it * 2 + h
                    dve.wait_ge(s_in[h], (it + 1) * 16)
                    dve.wait_ge(s_sent[h], it * (16 * C) + 16)
                    dve.sem_inc(m.step_dve, 1)
                    for f in range(F):
                        dve.tensor_tensor_scan(rows[h][:, f::XDW], m.same[:, bass.ds(n * C, C)], starts[h][:, f::F],
                                               rows[1 - h][:, (C - 1) * XDW + f:(C - 1) * XDW + f + 1], ALU.mult, ALU.add)
                    dve.tensor_copy(rows[h][:, F::XDW], m.recs[:, bass.ds(n * (C * REC), C * REC)].rearrange("p (c w) -> p c w", w=REC)[:, :, 1])
                    dve.tensor_copy(to[h][:, :], reci[:, bass.ds(n * (C * REC), C * REC)].rearrange("p (c w) -> p c w", w=REC)[:, :, 4])
                    dve.drain().then_inc(s_done, 1)
                    dve.sem_inc(s_free, 1)


def stage_neighbours(nc, m):
    TURNS = CHUNKS // 2
    with ExitStack() as ctx:
        def sb(name, shape, dt=F32):
            return ctx.enter_context(nc.sbuf_tensor(name, shape, dt))
        def sem(n):
            return ctx.enter_context(nc.semaphore(n))
        rows = [sb(f"rows3{h}", [P, C * XDW]) for h in range(2)]
        sc = [sb(f"scanned3{h}", [P, C * F]) for h in range(2)]
        same = sb("same_d", [P, C])
        low = sb("low", [P, 1])
        prev = sb("prev_d", [P, 1])
        s_prev, s_done, s_free = (sem(n) for n in ("s_prev", "s_done", "s_free"))
        s_in = [sem(f"s_in{h}") for h in range(2)]
        s_put = [sem(f"s_put{h}") for h in range(2)]
        block = ctx.enter_context(nc.Block())

        @block.sync
        def _(sp):
            sp.dma_start(prev[:, :], m.xd[0:EP, :].rearrange("(p j) w -> p j w", p=P)[:, 0, F:XDW], allow_slow_non_contiguous=True).then_inc(s_prev, 16)
            src = m.xd[1:EP + 1, :].rearrange("(p j) w -> p (j w)", p=P)
            with sp.Fori(0, TURNS) as it:
                for h in range(2):
                    sp.wait_ge(s_free, it * 2 + (h + 1))
                    sp.sem_inc(m.step_sp, 1)
                    sp.dma_start(rows[h][:, :], src[:, bass.ds((it * 2 + h) * (C * XDW), C * XDW)]).then_inc(s_in[h], 16)

        @block.scalar
        def _(act):
            prime(act, m, s_put)
            out = m.s3[0:EP, :].rearrange("(p j) w -> p (j w)", p=P)
            with act.Fori(0, TURNS) as it:
                for h in range(2):
                    act.wait_ge(s_done, it * 2 + (h + 1))
                    act.sem_inc(m.step_act, 1)
                    act.dma_start(out[:, bass.ds((it * 2 + h) * (C * F), C * F)], sc[h][:, :]).then_inc(s_put[h], 16)
            for h in range(2):
                act.wait_ge(s_put[h], 16 + 16 * TURNS)

        @block.vector
        def _(dve):
            dve.sem_inc(s_free, 2)
            dve.memset(sc[1][:, :], 0.0)
            dve.memset(m.whole[1][:, :], 1.0)
            dve.drain()
            dve.wait_ge(s_prev, 16)
            with dve.Fori(0, TURNS) as it:
                for h in range(2):
                    n = it * 2 + h
                    dve.wait_ge(s_in[h], (it + 1) * 16)
                    dve.wait_ge(s_put[h], (it + 1) * 16)
                    dve.sem_inc(m.step_dve, 1)
                    key = rows[h][:, F::XDW]
                    dve.tensor_tensor(same[:, 1:C], key[:, 1:C], key[:, 0:C - 1], ALU.is_equal)
                    dve.tensor_tensor(same[:, 0:1], key[:, 0:1], prev[:, :], ALU.is_equal)
                    dve.drain()
                    dve.tensor_copy(prev[:, :], key[:, C - 1:C])
                    dve.tensor_reduce(low[:, :], same[:, :], AX, ALU.min)
                    dve.drain()
                    dve.tensor_tensor(m.whole[1][:, :], m.whole[1][:, :], low[:, :], ALU.min)
                    for f in range(F):
                        dve.tensor_tensor_scan(sc[h][:, f::F], same[:, :], rows[h][:, f::XDW],
                                               sc[1 - h][:, (C - 1) * F + f:(C - 1) * F + f + 1], ALU.mult, ALU.add)
                    dve.drain().then_inc(s_done, 1)
                    dve.sem_inc(s_free, 1)
            dve.tensor_copy(m.fin[:, 0:F], sc[1][:, (C - 1) * F:C * F])


def stage_neighbour_nodes(nc, m, w3, b3, out):
    with ExitStack() as ctx:
        def sb(name, shape, dt=F32):
            return ctx.enter_context(nc.sbuf_tensor(name, shape, dt))
        def sem(n):
            return ctx.enter_context(nc.semaphore(n))
        ws = sb("w3_sb", [2 * F, F])
        bs = sb("b3_rows", [P, F])
        cat = sb("cat", [P, B * 2 * F])
        inv = sb("inv", [P, B])
        ct = sb("cat_t", [2 * F, 2, P])
        ps_x = [ctx.enter_context(nc.psum_tensor(f"ps_x3{i}", [P, 512], F32)) for i in range(2)]
        ps_o = [ctx.enter_context(nc.psum_tensor(f"ps_o3{i}", [P, 512], F32)) for i in range(2)]
        s_var, s_std, s_w, s_cat, s_ct, s_ctc, s_o, s_oc, s_fin, s_out = (
            sem(n) for n in ("s_var", "s_std", "s_w", "s_cat", "s_ct", "s_ctc", "s_o", "s_oc", "s_fin", "s_out"))
        block = ctx.enter_context(nc.Block())

        def sp_part(sp):
            sp.dma_start(ws[:, :], w3).then_inc(s_w, 16)
            sp.dma_start(bs[:, :], b3.partition_broadcast(P)).then_inc(s_w, 16)
            sp.wait_ge(s_fin, 1)
            sp.dma_start(out[0:(B - 1) * P, :].rearrange("(b p) f -> p b f", p=P),
                         m.x[:, 0:(B - 1) * F].rearrange("p (b f) -> p b f", f=F)).then_inc(s_out, 16)
            sp.dma_start(out[(B - 1) * P:N, :], m.x[0:LASTBLOCK, (B - 1) * F:B * F]).then_inc(s_out, 16)
            sp.wait_ge(s_out, 32)

        def dve_part(dve, ge):
            c3 = cat[:, :].rearrange("p (b w) -> p b w", w=2 * F)
            x3 = m.x[:, 0:B * F].rearrange("p (b f) -> p b f", f=F)
            dve.tensor_scalar(inv[:, :], m.cnt[1][:, :], 1.0, None, ALU.max)
            dve.tensor_copy(c3[:, :, 0:F], x3)
            dve.drain()
            dve.reciprocal(inv[:, :], inv[:, :])
            dve.drain()
            dve.tensor_tensor(c3[:, :, F:2 * F], ge[:, :].rearrange("p (b f) -> p b f", f=F), bcast(inv[:, :], 2, F), ALU.mult)
            dve.drain().then_inc(s_cat, 1)
            dve.wait_ge(s_w, 32)
            for b in range(B):
                q = m.sq[:, b * F:(b + 1) * F]
                dve.wait_ge(s_o, b + 1)
                dve.tensor_tensor(q, ps_o[b % 2][:, 0:F], bs[:, :], ALU.add).then_inc(s_oc, 1)
            dve.drain()
            dve.scalar_tensor_tensor(m.x[:, 0:B * F], m.sq[:, :], 0.0, m.x[:, 0:B * F], ALU.max, ALU.add)
            dve.drain()
            layer_norm(nc, m, dve, s_var, s_std, 1)
            dve.drain().then_inc(s_fin, 1)

        def pe_part(pe):
            pe.wait_ge(s_cat, 1)
            pe.wait_ge(s_w, 32)
            for b in range(B):
                if b >= 2:
                    pe.wait_ge(s_ctc, b - 1)
                pe.transpose(ps_x[b % 2][0:2 * F, 0:P], cat[:, b * 2 * F:(b + 1) * 2 * F], m.ident[:, :]).then_inc(s_ct, 1)
                pe.wait_ge(s_ctc, b + 1)
                if b >= 2:
                    pe.wait_ge(s_oc, b - 1)
                pe.matmul(ps_o[b % 2][:, 0:F], ct[:, b % 2, :], ws[:, :], start=True, stop=True).then_inc(s_o, 1)

        def act_part(act):
            for b in range(B):
                if b >= 2:
                    act.wait_ge(s_o, b - 1)
                act.wait_ge(s_ct, b + 1)
                act.activation(ct[:, b % 2, :], ps_x[b % 2][0:2 * F, 0:P], ACT.Copy).then_inc(s_ctc, 1)
            root(nc, m, act, s_var, s_std, 1)

        node_sums(nc, m, ctx, block, 1, m.s3, dve_part, pe_part, act_part, sp_part)


class Memory:
    pass


def gnn(nc, x, src, dst, edge_attr_2, edge_weight, w0, fc_w, fc_b, bias0, w1, w3, b3, out):
    m = Memory()

    def dram(name, shape, dt=F32):
        return nc.dram_tensor(f"{name}_dram", shape, dt).ap()

    m.keyrow = [dram(f"keyrow{k}", (EP,), I16) for k in range(2)]
    m.lorow = [dram(f"lorow{k}", (EP,), BF16) for k in range(2)]
    m.carry_row = [dram(f"carry_row{k}", (NN,), BF16) for k in range(2)]
    m.rec = dram("rec", (EP + 1, REC))
    m.xd = dram("xd", (EP + 1, XDW))
    m.t0, m.asrc_t, m.asrc_at = dram("t0", (NN, T0W)), dram("asrc_t", (NN, H)), dram("asrc_at", (EP, H))
    m.t1 = dram("t1", (NN * CELLS, T1W))
    m.x3t, m.h3 = dram("x3t", (NN, F)), dram("h3", (EP, F))
    m.s0, m.s1, m.s3 = dram("s0", (EP + 1, S0W)), dram("s1", (EP + 1, F)), dram("s3", (EP + 1, F))

    with ExitStack() as ctx:
        def sb(name, shape, dt=F32):
            return ctx.enter_context(nc.sbuf_tensor(name, shape, dt))
        m.step_pool, m.step_sp, m.step_act, m.step_dve, m.step_pe = (
            ctx.enter_context(nc.semaphore(f"step_{n}")) for n in ("pool", "sp", "act", "dve", "pe"))
        m.x = sb("x_sb", [P, GROUPS * 4 * F])
        m.sq = sb("sq", [P, B * F])
        m.mean, m.var, m.std = sb("mean", [P, B]), sb("var", [P, B]), sb("std", [P, B])
        m.lane, m.lane_b, m.part = sb("lane", [P, P]), sb("lane_b", [P, P], BF16), sb("part_index", [P, 1])
        m.ident, m.above, m.below, m.ones = (sb(n, [P, P]) for n in ("ident", "above", "below", "ones"))
        m.minus, m.eps = sb("minus", [P, XDW]), sb("eps", [P, 1])
        m.cnt, m.start, m.next, m.has = ([sb(f"{n}{k}", [P, B]) for k in range(2)] for n in ("cnt", "start", "next", "has"))
        m.i_end = [sb(f"i_end{k}", [P, B], I32) for k in range(2)]
        m.i_start = sb("i_start", [P, B], I32)
        m.sumw = sb("sumw", [P, B])
        m.spare, m.primed, m.first_word = sb("spare", [1, 16]), 0, x[0:1, 0:1]
        m.fin = sb("fin", [P, S0W])
        m.whole = [sb(f"whole{k}", [P, 1]) for k in range(2)]
        with ExitStack() as front:
            def sf(name, shape, dt=F32):
                return front.enter_context(nc.sbuf_tensor(name, shape, dt))
            m.key, m.hi, m.lo = ([sf(f"{n}{k}", [P, J]) for k in range(2)] for n in ("key", "hi", "lo"))
            m.attr = sf("attr", [P, 2 * J])
            with ExitStack() as early:
                def se(name, shape, dt=F32):
                    return early.enter_context(nc.sbuf_tensor(name, shape, dt))
                m.w, m.wrest = se("w", [P, J]), se("wrest", [P, J])
                m.wp = [se(f"wp{i}", [P, J]) for i in range(3)]
                stage_load(nc, m, x, src, dst, edge_attr_2, edge_weight)
                stage_count(nc, m)
            stage_places(nc, m, w0, fc_w, fc_b)
            stage_rank(nc, m)
        m.recs = sb("recs_sb", [P, J * REC])
        m.same = sb("same", [P, J])
        stage_attend(nc, m)
        stage_attend_nodes(nc, m, w0, bias0)
        stage_spline_table(nc, m, w1)
        stage_spline(nc, m)
        stage_spline_nodes(nc, m)
        stage_starts(nc, m)
        stage_exchange(nc, m)
        stage_neighbours(nc, m)
        stage_neighbour_nodes(nc, m, w3, b3, out)


_INS = ['x', 'src', 'dst', 'edge_attr_2', 'edge_weight', 'L0_gnn_w', 'L0_gnn_fc_w', 'L0_gnn_fc_b', 'L0_gnn_bias',
        'L1_gnn_weight', 'L3_gnn_W', 'L3_gnn_b']
_OUTS = [((N, F), 'float32')]


def kernel(**inputs):
    import numpy as _np
    import concourse.bacc as _bacc
    from concourse import mybir as _mybir
    from concourse.bass_utils import run_bass_kernel_spmd as _run

    nc = _bacc.Bacc("TRN2", target_bir_lowering=False, num_devices=1)
    arrays, args = {}, []
    for name in _INS:
        a = _np.ascontiguousarray(inputs[name])
        arrays[f"in_{name}_dram"] = a
        args.append(nc.dram_tensor(f"in_{name}_dram", a.shape, _mybir.dt.from_np(a.dtype), kind="ExternalInput").ap())
    for i, (shape, dtype) in enumerate(_OUTS):
        dt = _mybir.dt.from_np(_np.dtype(dtype))
        args.append(nc.dram_tensor(f"out_{i}_dram", shape, dt, kind="ExternalOutput").ap())
    gnn(nc, *args)
    r = _run(nc, [arrays], core_ids=[0])
    got = tuple(r.results[0][f"out_{i}_dram"] for i in range(len(_OUTS)))
    return got[0]
```

```python
import numpy as np
from contextlib import ExitStack

import concourse.bass as bass
from concourse import mybir

F32 = mybir.dt.float32
I32 = mybir.dt.int32
I16 = mybir.dt.int16
BF16 = mybir.dt.bfloat16
ALU = mybir.AluOpType
ACT = mybir.ActivationFunctionType
AX = mybir.AxisListType.X

P = 128
N = 12500
E = 212500
F = 32
H = 4
B = -(-N // P)
NN = B * P
PAD = NN - 1
C = 32
J = -(-E // (P * 2 * C)) * 2 * C
EP = P * J
CHUNKS = J // C
LASTROW = E - (P - 1) * J
LASTBLOCK = N - (B - 1) * P
GROUPS = -(-B // 4)
REC = 5
T0W = F + H
S0W = H * F + 2 * H
CELLS = 9
T1W = 4 * F
XDW = F + 1
BIG = 1.0e30
EPS = 1e-5


def bcast(ap, axis, n):
    a = ap.unsqueeze(axis)
    shape = list(a.shape)
    shape[axis] = n
    return a.broadcast_to(shape)


def load_split(eng, dst, src, sem):
    w = dst.shape[1] // J
    n = 0
    for lo, hi in ((0, 112), (112, P - 1)):
        eng.dma_start(dst[lo:hi, :], src[lo * J * w:hi * J * w].rearrange("(p j) -> p j", p=hi - lo)).then_inc(sem, 16)
        n += 16
    eng.dma_start(dst[P - 1:P, 0:LASTROW * w], src[(P - 1) * J * w:E * w].rearrange("(p j) -> p j", p=1)).then_inc(sem, 16)
    return n + 16


def prime(eng, m, sems):
    for sem in sems:
        eng.dma_start(m.spare[0:1, m.primed:m.primed + 1], m.first_word).then_inc(sem, 16)
        m.primed += 1


def stage_load(nc, m, x, src, dst, edge_attr, edge_weight):
    with ExitStack() as ctx:
        ki = [ctx.enter_context(nc.sbuf_tensor(f"key_int{k}", [P, J], I32)) for k in range(2)]
        part = ctx.enter_context(nc.sbuf_tensor("part", [P, J], I32))
        row_i = ctx.enter_context(nc.sbuf_tensor("row_i", [P, P], I32))
        col_i = ctx.enter_context(nc.sbuf_tensor("col_i", [P, 1], I32))
        row16 = ctx.enter_context(nc.sbuf_tensor("row16", [P, 2, J], I16))
        row_b = ctx.enter_context(nc.sbuf_tensor("row_b", [P, 2, J], BF16))
        last_i = ctx.enter_context(nc.sbuf_tensor("last_i", [P, 1], I32))
        last_f = ctx.enter_context(nc.sbuf_tensor("last_f", [P, 1], F32))
        down = ctx.enter_context(nc.sbuf_tensor("down", [P, J], F32))
        downs = ctx.enter_context(nc.sbuf_tensor("downs", [P, 1], F32))
        off = ctx.enter_context(nc.sbuf_tensor("off", [P, P], F32))
        off2 = ctx.enter_context(nc.sbuf_tensor("off2", [P, P], F32))
        zeros = m.zeros
        pst = [ctx.enter_context(nc.psum_tensor(f"ps_rows{i}", [P, P], F32)) for i in range(4)]
        ps_all = ctx.enter_context(nc.psum_tensor("ps_all", [P, 512], F32))
        s_downs = ctx.enter_context(nc.semaphore("s_downs"))
        s_all = ctx.enter_context(nc.semaphore("s_all"))
        s_clear = ctx.enter_context(nc.semaphore("s_clear"))
        s_iota = ctx.enter_context(nc.semaphore("s_iota"))
        s_in = ctx.enter_context(nc.semaphore("s_in"))
        s_keys = ctx.enter_context(nc.semaphore("s_keys"))
        s_turned = ctx.enter_context(nc.semaphore("s_turned"))
        s_row = ctx.enter_context(nc.semaphore("s_row"))
        s_out = ctx.enter_context(nc.semaphore("s_out"))
        block = ctx.enter_context(nc.Block())
        blocks = J // P
        arrays = 4
        INPUTS = 15

        @block.sync
        def _(sp):
            sp.wait_ge(s_clear, 1)
            n = 0
            for k, a in enumerate((src, dst)):
                n += load_split(sp, ki[k], a, s_in)
            sp.dma_start(m.x[:, 0:(B - 1) * F].rearrange("p (b f) -> p b f", f=F),
                         x[0:(B - 1) * P, :].rearrange("(b p) f -> p b f", p=P)).then_inc(s_in, 16)
            sp.dma_start(m.x[0:LASTBLOCK, (B - 1) * F:B * F], x[(B - 1) * P:N, :]).then_inc(s_in, 16)
            n += 32
            n += load_split(sp, m.attr, edge_attr.rearrange("e a -> (e a)"), s_in)
            n += load_split(sp, m.w, edge_weight, s_in)
            sp.dma_start(last_i[1:P, :], dst[0:(P - 1) * J].rearrange("(p j) -> p j", j=J)[:, J - 1:J],
                         allow_slow_non_contiguous=True).then_inc(s_in, 16)
            n += 16
            assert n == INPUTS * 16
            sp.dma_start(m.asrc_at.rearrange("(p j) h -> p (j h)", p=P), zeros[:, :]).then_inc(s_out, 16)
            sp.dma_start(m.rec[0:1, :], m.minus[0:1, 0:REC]).then_inc(s_out, 16)
            sp.dma_start(m.xd[0:1, :], m.minus[0:1, 0:XDW]).then_inc(s_out, 16)
            sp.dma_start(m.s0[EP:EP + 1, :], zeros[0:1, 0:S0W]).then_inc(s_out, 16)
            sp.dma_start(m.s1[EP:EP + 1, :], zeros[0:1, 0:F]).then_inc(s_out, 16)
            sp.dma_start(m.s3[EP:EP + 1, :], zeros[0:1, 0:F]).then_inc(s_out, 16)
            sp.wait_ge(s_row, 4 * blocks)
            for k in range(2):
                for a, t in ((m.keyrow[k], row16), (m.lorow[k], row_b)):
                    sp.dma_start(a.rearrange("(b t p) -> t b p", t=P, p=P),
                                 t[:, k, :].rearrange("t (b p) -> t b p", p=P)).then_inc(s_out, 16)
            sp.wait_ge(s_out, 16 * (1 + 5 + 4))

        @block.gpsimd
        def _(pool):
            pool.iota(row_i[:, :], pattern=[[1, P]], base=0, channel_multiplier=0).then_inc(s_iota, 1)
            pool.iota(col_i[:, :], pattern=[[0, 1]], base=0, channel_multiplier=1).then_inc(s_iota, 1)
            pool.iota(m.natural[:, :], pattern=[[1, J]], base=1, channel_multiplier=J).then_inc(s_iota, 1)

        @block.vector
        def _(dve):
            for k in range(2):
                dve.memset(ki[k][:, :], PAD)
            dve.memset(m.x[:, :], 0.0)
            dve.memset(m.attr[:, :], 0.0)
            dve.memset(m.w[:, :], 0.0)
            dve.memset(zeros[:, :], 0.0)
            dve.memset(m.zero[:, :], 0.0)
            dve.memset(m.ones[:, :], 1.0)
            dve.memset(m.eps[:, :], EPS)
            dve.memset(last_i[:, :], 0)
            dve.memset(m.lo[1][:, J:J + 4], 0.0)
            dve.memset(m.hi[1][:, J:J + 4], 0.0)
            dve.memset(m.minus[:, :], -1.0).then_inc(s_clear, 1)
            dve.wait_ge(s_iota, 3)
            dve.tensor_copy(m.lane[:, :], row_i[:, :])
            dve.tensor_copy(m.part[:, :], col_i[:, :])
            dve.drain()
            dve.tensor_copy(m.lane_b[:, :], m.lane[:, :])
            dve.tensor_scalar(m.ident[:, :], m.lane[:, :], m.part[:, 0:1], None, ALU.is_equal)
            dve.tensor_scalar(m.above[:, :], m.lane[:, :], m.part[:, 0:1], None, ALU.is_gt)
            dve.tensor_scalar(m.below[:, :], m.lane[:, :], m.part[:, 0:1], None, ALU.is_lt)
            dve.wait_ge(s_in, INPUTS * 16)
            for k in range(2):
                dve.tensor_copy(m.key[k][:, :], ki[k][:, :])
                dve.tensor_scalar(part[:, :], ki[k][:, :], 7, None, ALU.logical_shift_right)
                dve.drain()
                dve.tensor_copy(m.hi[k][:, 0:J], part[:, :])
                dve.drain()
                dve.tensor_scalar(part[:, :], ki[k][:, :], P - 1, None, ALU.bitwise_and)
                dve.drain()
                dve.tensor_copy(m.lo[k][:, 0:J], part[:, :])
                dve.drain()
            dve.drain().then_inc(s_keys, 1)
            for k in range(2):
                dve.tensor_copy(m.lo_b[k][:, :], m.lo[k][:, 0:J])
                dve.tensor_copy(m.hi_b[k][:, :], m.hi[k][:, 0:J])
                dve.tensor_scalar(m.half_minus_lo[k][:, :], m.lo[k][:, 0:J], -1.0, 0.5, ALU.mult, ALU.add)
            dve.tensor_copy(last_f[:, :], last_i[:, :])
            dve.tensor_tensor(down[:, 1:J], m.key[1][:, 1:J], m.key[1][:, 0:J - 1], ALU.is_lt)
            dve.drain()
            dve.tensor_tensor(down[:, 0:1], m.key[1][:, 0:1], last_f[:, :], ALU.is_lt)
            dve.drain()
            dve.tensor_reduce(downs[:, :], down[:, :], AX, ALU.add)
            dve.tensor_scalar(off[:, :], m.lane[:, :], m.part[:, 0:1], None, ALU.subtract)
            dve.drain()
            dve.tensor_scalar(m.undo[:, :], off[:, :], 0.0, 0.5, ALU.is_equal, ALU.mult)
            dve.tensor_scalar(off2[:, :], off[:, :], 1.0, -0.5, ALU.is_equal, ALU.mult)
            dve.drain()
            dve.tensor_tensor(m.undo[:, :], m.undo[:, :], off2[:, :], ALU.add)
            dve.drain()
            dve.tensor_scalar(off2[:, :], off[:, :], float(1 - P), 0.5, ALU.is_equal, ALU.mult)
            dve.drain()
            dve.tensor_tensor(m.undo[:, :], m.undo[:, :], off2[:, :], ALU.add)
            dve.drain().then_inc(s_downs, 1)
            dve.wait_ge(s_all, 1)
            dve.tensor_copy(m.unsorted[:, :], ps_all[:, 0:1])
            dve.drain()

        @block.tensor
        def _(pe):
            pe.wait_ge(s_keys, 1)
            for i in range(arrays * blocks):
                a, b = divmod(i, blocks)
                s = (m.key[0], m.lo[0], m.key[1], m.lo[1])[a]
                if i >= 4:
                    pe.wait_ge(s_row, i - 3)
                pe.transpose(pst[i % 4][:, :], s[:, b * P:(b + 1) * P], m.ident[:, :]).then_inc(s_turned, 1)
            pe.wait_ge(s_downs, 1)
            pe.matmul(ps_all[:, 0:1], m.ones[:, :], downs[:, :], start=True, stop=True).then_inc(s_all, 1)

        @block.scalar
        def _(act):
            for i in range(arrays * blocks):
                a, b = divmod(i, blocks)
                t = (row16, row_b)[a % 2]
                act.wait_ge(s_turned, i + 1)
                act.activation(t[:, a // 2, b * P:(b + 1) * P], pst[i % 4][:, :], ACT.Copy).then_inc(s_row, 1)


def if_unsorted(eng, m, work):
    downs = eng.value_load(m.unsorted[0:1, 0:1], min_val=0, max_val=E)
    with eng.If(downs > 0):
        work()


def stage_count(nc, m):
    T = 16
    SIGNS = 9
    ONES = T - SIGNS
    TURNS = J // (2 * T)
    with ExitStack() as ctx:
        def sb(name, shape, dt=BF16):
            return ctx.enter_context(nc.sbuf_tensor(name, shape, dt))
        def sem(n):
            return ctx.enter_context(nc.semaphore(n))
        oa = [sb(f"onelane{h}", [P, ONES, P]) for h in range(2)]
        sg = [sb(f"signlane{h}", [P, SIGNS, P]) for h in range(2)]
        ob = [sb(f"oneblock{h}", [P, T, B]) for h in range(2)]
        zero = sb("zero_b", [P, P])
        cum = sb("cum", [P, 2, B], F32)
        part = sb("part_counts", [P, B], F32)
        ps_ones = [ctx.enter_context(nc.psum_tensor(f"ps_ones{i}", [P, 512], F32)) for i in range(2)]
        ps_signs = [ctx.enter_context(nc.psum_tensor(f"ps_signs{i}", [P, 512], F32)) for i in range(2)]
        ps_d = ctx.enter_context(nc.psum_tensor("ps_diff", [P, 512], F32))
        s_banks, s_made, s_signs, s_free, s_sum, s_cum, s_diff = (
            sem(n) for n in ("s_banks", "s_made", "s_signs", "s_free", "s_sum", "s_cum", "s_diff"))
        s_fill = sem("s_fill")
        block = ctx.enter_context(nc.Block())

        @block.sync
        def _(sp):
            hv = m.h3.rearrange("(p j) f -> p (j f)", p=P)
            for i in range(F // H):
                sp.dma_start(hv[:, i * H * J:(i + 1) * H * J], m.zeros[:, :]).then_inc(s_fill, 16)
            sp.wait_ge(s_fill, 16 * (F // H))

        @block.vector
        def _(dve):
            def count(k):
                with dve.Fori(0, TURNS) as it:
                    for h in range(2):
                        n = it * 2 + h
                        dve.wait_ge(s_free, it * 2 + (h + 1 + k * 2 * TURNS))
                        dve.sem_inc(m.step_dve, 1)
                        dve.tensor_tensor(oa[h][:, :, :], bcast(m.lane_b[:, :], 1, ONES), bcast(m.lo_b[k][:, bass.ds(n * T, ONES)], 2, P), ALU.is_equal)
                        dve.tensor_tensor(ob[h][:, :, :], bcast(m.lane_b[:, 0:B], 1, T), bcast(m.hi_b[k][:, bass.ds(n * T, T)], 2, B), ALU.is_equal).then_inc(s_made, 1)
                dve.wait_ge(s_sum, k + 1)
                for i in range(2):
                    dve.tensor_copy(cum[:, i, :], ps_signs[i][:, 0:B])
                dve.drain().then_inc(s_cum, 1)
                dve.tensor_copy(part[:, :], ps_ones[0][:, 0:B])
                dve.drain()
                dve.tensor_tensor(m.cnt[k][:, :], part[:, :], ps_ones[1][:, 0:B], ALU.add)
                dve.wait_ge(s_diff, k + 1)
                if k == 0:
                    dve.tensor_tensor(m.cnt_first[:, :], part[:, :], ps_d[:, 0:B], ALU.add)
                for i in range(2):
                    dve.drain()
                    dve.tensor_tensor(m.cnt[k][:, :], m.cnt[k][:, :], ps_d[:, i * B:(i + 1) * B], ALU.add)
                dve.drain().then_inc(s_banks, 1)
            dve.memset(m.cnt[1][:, :], 0.0)
            dve.memset(zero[:, :], 0.0).then_inc(s_banks, 1)
            count(0)
            if_unsorted(dve, m, lambda: count(1))

        @block.scalar
        def _(act):
            def count(k):
                with act.Fori(0, TURNS) as it:
                    for h in range(2):
                        act.wait_ge(s_free, it * 2 + (h + 1 + k * 2 * TURNS))
                        act.sem_inc(m.step_act, 1)
                        for t in range(SIGNS):
                            last = act.activation(sg[h][:, t, :], m.lane_b[:, :], ACT.Sign,
                                                  bias=m.half_minus_lo[k][:, bass.ds((it * 2 + h) * T + (ONES + t), 1)])
                        last.then_inc(s_signs, 1)
            count(0)
            if_unsorted(act, m, lambda: count(1))

        @block.tensor
        def _(pe):
            def count(k):
                pe.wait_ge(s_banks, k + 1)
                for bank in (*ps_ones, *ps_signs):
                    pe.matmul(bank[:, 0:B], zero[:, :], zero[:, 0:B], start=True, stop=False)
                for half in range(2):
                    with pe.Fori(half * TURNS // 2, (half + 1) * TURNS // 2) as it:
                        for h in range(2):
                            pe.wait_ge(s_made, it * 2 + (h + 1 + k * 2 * TURNS))
                            pe.wait_ge(s_signs, it * 2 + (h + 1 + k * 2 * TURNS))
                            pe.sem_inc(m.step_pe, 1)
                            for t in range(ONES):
                                pe.matmul(ps_ones[half][:, 0:B], oa[h][:, t, :], ob[h][:, t, :], start=False, stop=False)
                            for t in range(SIGNS):
                                last = pe.matmul(ps_signs[half][:, 0:B], sg[h][:, t, :], ob[h][:, ONES + t, :], start=False, stop=False)
                            last.then_inc(s_free, 1)
                for bank in (*ps_ones, *ps_signs):
                    last = pe.matmul(bank[:, 0:B], zero[:, :], zero[:, 0:B], start=False, stop=True)
                last.then_inc(s_sum, 1)
                pe.wait_ge(s_cum, k + 1)
                pe.matmul(ps_d[:, 0:2 * B], m.undo[:, :], cum[:, :, :], start=True, stop=True).then_inc(s_diff, 1)
            pe.sem_inc(s_free, 2)
            count(0)
            if_unsorted(pe, m, lambda: count(1))


class Places:

    def __init__(self, nc, ctx, tag):
        def sb(name, shape, dt=F32):
            return ctx.enter_context(nc.sbuf_tensor(name + tag, shape, dt))
        self.tot, self.incl, self.end, self.ne, self.r, self.t1, self.t2 = (
            sb(n, [P, B]) for n in ("tot", "incl", "end", "nonempty", "ratio", "work1", "work2"))
        self.ri = sb("ratio_i", [P, B], I32)
        self.zb = sb("zb", [P, B])
        self.vb = sb("carry_of_b", [B, 2, P], BF16)
        self.ps_a, self.ps_b, self.ps_v = (ctx.enter_context(nc.psum_tensor(n + tag, [P, 512], F32)) for n in ("ps_a", "ps_b", "ps_v"))
        self.s_products, self.s_operands, self.s_vc = (
            ctx.enter_context(nc.semaphore(n)) for n in ("s_products", "s_operands", "s_vc"))


def places_pe(pe, m, w, k, turn):
    if turn:
        pe.wait_ge(w.s_operands, 2 * turn)
    pe.matmul(w.ps_a[:, 0:B], m.above[:, :], m.cnt[k][:, :], start=True, stop=True)
    pe.matmul(w.ps_b[:, 0:B], m.ones[:, :], m.cnt[k][:, :], start=True, stop=True).then_inc(w.s_products, 1)
    pe.wait_ge(w.s_operands, 2 * turn + 2)
    pe.transpose(w.ps_v[0:B, k * P:(k + 1) * P], w.t2[:, :], m.ident[:, :]).then_inc(w.s_products, 1)


def places_dve(dve, m, w, k, turn):
    tot, incl, end, ne, r, t1, t2, ri = w.tot, w.incl, w.end, w.ne, w.r, w.t1, w.t2, w.ri
    dve.wait_ge(w.s_products, 2 * turn + 1)
    dve.tensor_copy(tot[:, :], w.ps_b[:, 0:B])
    dve.drain()
    dve.tensor_tensor_scan(incl[:, :], w.zb[:, :], tot[:, :], 0.0, ALU.add, ALU.add)
    dve.drain()
    dve.tensor_tensor(incl[:, :], incl[:, :], tot[:, :], ALU.subtract)
    dve.drain()
    dve.tensor_tensor(m.start[k][:, :], incl[:, :], w.ps_a[:, 0:B], ALU.add)
    dve.drain().then_inc(w.s_operands, 1)
    dve.tensor_scalar(m.next[k][:, :], m.start[k][:, :], 1.0, None, ALU.add)
    dve.tensor_tensor(end[:, :], m.start[k][:, :], m.cnt[k][:, :], ALU.add)
    dve.tensor_scalar(ne[:, :], m.cnt[k][:, :], 1.0, None, ALU.min)
    dve.drain()
    dve.tensor_scalar(end[:, :], end[:, :], 1.0, None, ALU.subtract)
    dve.drain()
    dve.scalar_tensor_tensor(t1[:, :], end[:, :], float(EP), ne[:, :], ALU.subtract, ALU.mult)
    dve.drain()
    dve.tensor_scalar(m.i_end[k][:, :], t1[:, :], float(EP), None, ALU.add)
    dve.tensor_scalar(ri[:, :], end[:, :], 1.0 / J, None, ALU.mult)
    dve.drain()
    dve.tensor_copy(r[:, :], ri[:, :])
    dve.drain()
    dve.scalar_tensor_tensor(t1[:, :], r[:, :], float(J), end[:, :], ALU.mult, ALU.is_gt)
    dve.drain()
    dve.tensor_tensor(r[:, :], r[:, :], t1[:, :], ALU.subtract)
    dve.drain()
    dve.tensor_scalar(t1[:, :], r[:, :], 1.0, float(J), ALU.add, ALU.mult)
    dve.drain()
    dve.tensor_tensor(t1[:, :], t1[:, :], end[:, :], ALU.is_le)
    dve.drain()
    dve.tensor_tensor(r[:, :], r[:, :], t1[:, :], ALU.add)
    dve.drain()
    dve.scalar_tensor_tensor(t1[:, :], r[:, :], float(J), m.start[k][:, :], ALU.mult, ALU.is_gt)
    dve.drain()
    dve.tensor_tensor(m.has[k][:, :], t1[:, :], ne[:, :], ALU.mult)
    dve.drain()
    dve.scalar_tensor_tensor(t1[:, :], r[:, :], 1.0, m.has[k][:, :], ALU.add, ALU.mult)
    dve.drain()
    dve.tensor_scalar(t2[:, :], t1[:, :], 1.0, None, ALU.subtract)
    dve.drain().then_inc(w.s_operands, 1)
    if k == 0:
        dve.tensor_tensor(m.next_half[:, :], m.next[0][:, :], m.cnt_first[:, :], ALU.add)
        dve.tensor_scalar(t1[:, :], ne[:, :], -1.0e6, 1.0e6, ALU.mult, ALU.add)
        dve.drain()
        dve.tensor_tensor(m.i_start[:, :], t1[:, :], m.start[k][:, :], ALU.add)
        dve.drain()
    dve.wait_ge(w.s_products, 2 * turn + 2)
    dve.tensor_copy(w.vb[:, k, :], w.ps_v[0:B, k * P:(k + 1) * P])
    dve.drain().then_inc(w.s_vc, 1)


def stage_places(nc, m, w0, fc_w, fc_b):
    with ExitStack() as ctx:
        def sb(name, shape, dt=F32):
            return ctx.enter_context(nc.sbuf_tensor(name, shape, dt))
        w = Places(nc, ctx, "0")
        wl = sb("w_heads", [P, H * F])
        fc = sb("fc_rows", [P, 2 * F])
        fcb = sb("fcb_rows", [P, 1])
        prod = sb("w_times_fc", [P, 2 * H * F])
        v8 = sb("v8", [P, 2 * H])
        vblk = sb("vblk", [P, 4 * 2 * H])
        xt = sb("xt", [P, 2, P])
        a8 = sb("a8", [P, GROUPS * 4 * 2 * H])
        t0 = sb("t0_rows", [P, B * T0W])
        asr = sb("asrc_rows", [P, B * H])
        ps_t = [ctx.enter_context(nc.psum_tensor(f"ps_t{i}", [P, 512], F32)) for i in range(2)]
        ps_m = [ctx.enter_context(nc.psum_tensor(f"ps_m{i}", [P, 512], F32)) for i in range(2)]
        names = ("s_w", "s_vblk", "s_xt", "s_xc", "s_m", "s_mc", "s_rows", "s_st", "s_sc")
        s_w, s_vblk, s_xt, s_xc, s_m, s_mc, s_rows, s_st, s_sc = (
            ctx.enter_context(nc.semaphore(n)) for n in names)
        block = ctx.enter_context(nc.Block())

        @block.sync
        def _(sp):
            for b in range(4):
                sp.dma_start(wl[b * F:(b + 1) * F, :].rearrange("f (h o) -> f h o", h=H),
                             w0.rearrange("h f o -> f h o")).then_inc(s_w, 16)
            sp.dma_start(fc[:, :], fc_w[0, :].partition_broadcast(P)).then_inc(s_w, 16)
            sp.dma_start(fcb[:, :], fc_b[:].partition_broadcast(P)).then_inc(s_w, 16)
            sp.wait_ge(w.s_vc, 2)
            for k in range(2):
                sp.dma_start(m.carry_row[k].rearrange("(b p) -> b p", p=P), w.vb[:, k, :]).then_inc(s_st, 16)
            sp.wait_ge(s_rows, 1)
            sp.dma_start(m.t0.rearrange("(b p) w -> p b w", p=P), t0[:, :].rearrange("p (b w) -> p b w", w=T0W)).then_inc(s_st, 16)
            sp.dma_start(m.asrc_t.rearrange("(b p) w -> p b w", p=P), asr[:, :].rearrange("p (b w) -> p b w", w=H)).then_inc(s_st, 16)
            sp.wait_ge(s_st, 64)

        @block.gpsimd
        def _(pool):
            pool.wait_ge(s_rows, 1)
            for b in range(B):
                pool.indirect_dma_start(out=m.asrc_at, out_offset=bass.IndirectOffsetOnAxis(ap=m.i_start[:, b:b + 1], axis=0),
                                        in_=asr[:, b * H:(b + 1) * H], in_offset=None,
                                        bounds_check=EP - 1, oob_is_err=False).then_inc(s_sc, 16)
            pool.wait_ge(s_sc, 16 * B)

        @block.vector
        def _(dve):
            dve.memset(w.zb[:, :], 0.0)
            dve.memset(m.x[:, B * F:GROUPS * 4 * F], 0.0)
            for k in range(2):
                places_dve(dve, m, w, k, k)
            dve.wait_ge(s_w, 96)
            for i in range(2):
                dve.tensor_tensor(prod[:, i * H * F:(i + 1) * H * F].rearrange("p (h o) -> p h o", h=H),
                                  wl[:, :].rearrange("p (h o) -> p h o", h=H),
                                  bcast(fc[:, i * F:(i + 1) * F], 1, H), ALU.mult)
            dve.memset(vblk[:, :], 0.0)
            dve.drain()
            dve.tensor_reduce(v8[:, :], prod[:, :].rearrange("p (h o) -> p h o", o=F), AX, ALU.add)
            dve.drain()
            for b in range(4):
                dve.tensor_copy(vblk[b * F:(b + 1) * F, b * 2 * H:(b + 1) * 2 * H], v8[b * F:(b + 1) * F, :])
            dve.drain().then_inc(s_vblk, 1)
            for g in range(GROUPS):
                dve.wait_ge(s_m, g + 1)
                dve.tensor_copy(a8[:, g * 8 * H:(g + 1) * 8 * H], ps_m[g % 2][:, 0:8 * H]).then_inc(s_mc, 1)
            dve.drain()
            a8v = a8[:, :].rearrange("p (b w) -> p b w", w=2 * H)
            t0v = t0[:, :].rearrange("p (b w) -> p b w", w=T0W)
            dve.tensor_copy(t0v[:, :, 0:F], m.x[:, 0:B * F].rearrange("p (b f) -> p b f", f=F))
            dve.tensor_copy(t0v[:, :, F:T0W], a8v[:, 0:B, H:2 * H])
            dve.tensor_scalar(asr[:, :].rearrange("p (b h) -> p b h", h=H), a8v[:, 0:B, 0:H], fcb[:, 0:1], None, ALU.add)
            dve.drain().then_inc(s_rows, 1)

        @block.tensor
        def _(pe):
            for k in range(2):
                places_pe(pe, m, w, k, k)
            pe.wait_ge(s_vblk, 1)
            for g in range(GROUPS):
                if g >= 2:
                    pe.wait_ge(s_xc, g - 1)
                pe.transpose(ps_t[g % 2][:, 0:P], m.x[:, g * P:(g + 1) * P], m.ident[:, :]).then_inc(s_xt, 1)
                if g >= 2:
                    pe.wait_ge(s_mc, g - 1)
                pe.wait_ge(s_xc, g + 1)
                pe.matmul(ps_m[g % 2][:, 0:8 * H], xt[:, g % 2, :], vblk[:, :], start=True, stop=True).then_inc(s_m, 1)

        @block.scalar
        def _(act):
            for g in range(GROUPS):
                if g >= 2:
                    act.wait_ge(s_m, g - 1)
                act.wait_ge(s_xt, g + 1)
                act.activation(xt[:, g % 2, :], ps_t[g % 2][:, 0:P], ACT.Copy).then_inc(s_xc, 1)


def stage_rank(nc, m):
    T = 16
    R = 4
    LAG = 2
    BOTH = ((0, 0), (1, 0))
    HALVES = ((0, 0), (0, J // 2))
    CHAINS = range(2)
    with ExitStack() as ctx:
        def sb(name, shape, dt=F32):
            return ctx.enter_context(nc.sbuf_tensor(name, shape, dt))
        krow = [[sb(f"krow{h}{c}", [P, T * P], I16) for c in CHAINS] for h in range(2)]
        lrow = [[sb(f"lrow{h}{c}", [P, T * P], BF16) for c in CHAINS] for h in range(2)]
        oat = [[sb(f"lane_onehot_t{h}{c}", [P, T * P]) for c in CHAINS] for h in range(2)]
        oa = [sb(f"lane_onehot{c}", [P, R, P], BF16) for c in CHAINS]
        ob = [sb(f"block_onehot{c}", [P, R, B], BF16) for c in CHAINS]
        nxt = [sb(f"next_sb{c}", [P, 2, B]) for c in CHAINS]
        junk = sb("junk", [P, R, 4, P], BF16)
        base = [sb(f"base{c}", [P, T]) for c in CHAINS]
        rank = [sb(f"rank{c}", [P, T]) for c in CHAINS]
        place = [sb(f"place{h}", [P, 2 * T], I32) for h in range(2)]
        recs = [sb(f"recs{h}", [P, 2 * T * REC]) for h in range(2)]
        ps_n = [ctx.enter_context(nc.psum_tensor(f"ps_next{c}", [P, 512], F32)) for c in CHAINS]
        ps_f = [[ctx.enter_context(nc.psum_tensor(f"ps_fetch{c}{i}", [P, 512], F32)) for i in range(2)] for c in CHAINS]
        def sem(n):
            return ctx.enter_context(nc.semaphore(n))
        s_row = [sem(f"s_row{h}") for h in range(2)]
        s_rowfree = sem("s_rowfree")
        s_lane = [sem(f"s_lane{c}") for c in CHAINS]
        s_hot, s_upd, s_cur, s_fet, s_sel = ([sem(f"{n}{c}") for c in CHAINS] for n in ("s_hot", "s_upd", "s_cur", "s_fet", "s_sel"))
        s_rec = sem("s_rec")
        s_sent = [sem(f"s_sent{h}") for h in range(2)]
        block = ctx.enter_context(nc.Block())

        def either(eng, ranked):
            downs = eng.value_load(m.unsorted[0:1, 0:1], min_val=0, max_val=E)
            with eng.If(downs == 0):
                ranked(HALVES, J // (4 * T), 2 * T)
            with eng.Else():
                ranked(BOTH, J // (2 * T), T)

        @block.sync
        def _(sp):
            def ranked(chains, turns, tiles):
                with sp.Fori(0, turns) as it:
                    for h in range(2):
                        sp.wait_ge(s_rowfree, it * 2 + (h + 1))
                        sp.sem_inc(m.step_sp, 1)
                        for c, (k, col) in enumerate(chains):
                            for t, a in ((krow[h][c], m.keyrow[k]), (lrow[h][c], m.lorow[k])):
                                sp.dma_start(t[:, :], a[bass.ds((it * 2 + h) * (T * P) + col * P, T * P)].partition_broadcast(P)).then_inc(s_row[h], 16)
                sp.wait_ge(s_rowfree, turns * 2 + 1)
                for c, (k, col) in enumerate(chains):
                    for t, a in ((krow[0][c], m.keyrow[k]), (lrow[0][c], m.lorow[k])):
                        sp.dma_start(t[:, :], a[0:T * P].partition_broadcast(P)).then_inc(s_row[0], 16)
                sp.wait_ge(s_row[0], (turns + 1) * 64)
            either(sp, ranked)

        @block.gpsimd
        def _(pool):
            def ranked(chains, turns, tiles):
                with pool.Fori(0, turns) as it:
                    for h in range(2):
                        pool.wait_ge(s_rec, it * 2 + (h + 1))
                        pool.sem_inc(m.step_pool, 1)
                        for t in range(tiles):
                            pool.indirect_dma_start(out=m.rec, out_offset=bass.IndirectOffsetOnAxis(ap=place[h][:, t:t + 1], axis=0),
                                                    in_=recs[h][:, t * REC:(t + 1) * REC], in_offset=None).then_inc(s_sent[h], 16)
            prime(pool, m, s_sent)
            either(pool, ranked)
            for h in range(2):
                pool.wait_ge(s_sent[h], 16 + 16 * J // 2)

        @block.vector
        def _(dve):
            def make(chains, n, t):
                s = t % R
                for c, (k, col) in enumerate(chains):
                    dve.wait_ge(s_upd[c], n + (t + 1))
                    dve.tensor_scalar(oa[c][:, s, :], m.lane_b[:, :], m.lo[k][:, bass.ds(n + (t + col), 1)], None, ALU.is_equal)
                    dve.tensor_scalar(ob[c][:, s, :], m.lane_b[:, 0:B], m.hi[k][:, bass.ds(n + (t + col), 1)], None, ALU.is_equal).then_inc(s_hot[c], 1)

            def select(chains, n, h, t):
                for c, (k, col) in enumerate(chains):
                    dve.scalar_tensor_tensor(junk[:, t % R, 2 * c, :], krow[h][c][:, t * P:(t + 1) * P], m.key[k][:, bass.ds(n + (t + col), 1)], m.below[:, :],
                                             ALU.is_equal, ALU.mult, accum_out=rank[c][:, t:t + 1])
                    dve.wait_ge(s_fet[c], n + (t + 1 + 2))
                    dve.scalar_tensor_tensor(junk[:, t % R, 2 * c + 1, 0:B], m.lane[:, 0:B], m.hi[k][:, bass.ds(n + (t + col), 1)], ps_f[c][t % 2][:, 0:B],
                                             ALU.is_equal, ALU.mult, accum_out=base[c][:, t:t + 1]).then_inc(s_sel[c], 1)

            def lanes(h, count):
                dve.wait_ge(s_row[h], count)
                dve.sem_inc(m.step_dve, 1)
                for c in CHAINS:
                    dve.tensor_scalar(oat[h][c][:, :], lrow[h][c][:, :], m.part[:, 0:1], None, ALU.is_equal).then_inc(s_lane[c], 1)

            def ranked(chains, turns, tiles):
                lanes(0, 64)
                for t in range(LAG):
                    make(chains, 0, t)
                with dve.Fori(0, turns) as it:
                    for h in range(2):
                        n = (it * 2 + h) * T
                        for t in range(T):
                            make(chains, n, t + LAG)
                            if t == T - 4:
                                lanes(1 - h, (it + (h + 1)) * 64)
                            select(chains, n, h, t)
                        dve.drain().then_inc(s_rowfree, 1)
                        dve.wait_ge(s_sent[h], it * (16 * tiles) + 16)
                        dve.sem_inc(m.step_dve, 1)
                        rv = recs[h][:, :].rearrange("p (t w) -> p t w", w=REC)
                        ri = recs[h][:, :].bitcast(I32).rearrange("p (t w) -> p t w", w=REC)
                        for c, (k, col) in enumerate(chains if chains is HALVES else chains[:1]):
                            lot = slice(c * T, (c + 1) * T)
                            dve.tensor_tensor(place[h][:, lot], base[c][:, :], rank[c][:, :], ALU.add)
                            if chains is HALVES:
                                dve.tensor_copy(ri[:, lot, 4], m.natural[:, bass.ds(n + col, T)])
                            else:
                                dve.tensor_tensor(ri[:, lot, 4], base[1][:, :], rank[1][:, :], ALU.add)
                            dve.tensor_copy(rv[:, lot, 0], m.key[0][:, bass.ds(n + col, T)])
                            dve.tensor_copy(rv[:, lot, 1], m.key[1][:, bass.ds(n + col, T)])
                            dve.tensor_copy(rv[:, lot, 2:4], m.attr[:, bass.ds(n * 2 + 2 * col, 2 * T)].rearrange("p (t a) -> p t a", a=2))
                        dve.drain().then_inc(s_rec, 1)

            dve.sem_inc(s_rowfree, 2)
            for c in CHAINS:
                dve.sem_inc(s_sel[c], 2)
            either(dve, ranked)

        @block.tensor
        def _(pe):
            def ranked(chains, turns, tiles):
                for c, (k, col) in enumerate(chains):
                    table = m.next[k] if col == 0 else m.next_half
                    pe.matmul(ps_n[c][:, 0:B], m.ident[:, :], table[:, :], start=True, stop=True).then_inc(s_upd[c], R)
                    pe.sem_inc(s_fet[c], 2)
                with pe.Fori(0, turns) as it:
                    for h, t in ((h, t) for h in range(2) for t in range(T)):
                        n = it * (2 * T) + (h * T + t + 1)
                        for c in CHAINS:
                            if t == 0:
                                pe.wait_ge(s_lane[c], it * 2 + (h + 1))
                            pe.wait_ge(s_hot[c], n)
                            pe.wait_ge(s_cur[c], n)
                            pe.wait_ge(s_sel[c], n)
                            pe.sem_inc(m.step_pe, 1)
                            pe.matmul(ps_f[c][t % 2][:, 0:B], oat[h][c][:, t * P:(t + 1) * P], nxt[c][:, t % 2, :], start=True, stop=True).then_inc(s_fet[c], 1)
                            pe.matmul(ps_n[c][:, 0:B], m.ident[:, :], nxt[c][:, t % 2, :], start=True, stop=False)
                            pe.matmul(ps_n[c][:, 0:B], oa[c][:, t % R, :], ob[c][:, t % R, :], start=False, stop=True).then_inc(s_upd[c], 1)
            either(pe, ranked)

        @block.scalar
        def _(act):
            def ranked(chains, turns, tiles):
                with act.Fori(0, turns * T) as it:
                    for t in range(2):
                        for c in CHAINS:
                            act.wait_ge(s_upd[c], it * 2 + (R + t))
                            act.wait_ge(s_fet[c], it * 2 + (t + 1))
                            act.sem_inc(m.step_act, 1)
                            act.activation(nxt[c][:, t, :], ps_n[c][:, 0:B], ACT.Copy).then_inc(s_cur[c], 1)
            either(act, ranked)


def stage_attend(nc, m):
    TURNS = CHUNKS // 2
    with ExitStack() as ctx:
        def sb(name, shape, dt=F32):
            return ctx.enter_context(nc.sbuf_tensor(name, shape, dt))
        def sem(n):
            return ctx.enter_context(nc.semaphore(n))
        prev = sb("prev_key", [P, 1])
        pen = sb("pen", [P, C])
        first = sb("first_i", [P, 1], I32)
        first_a = sb("first_asrc", [P, H])
        asrc = sb("asrc_edges", [P, J * H])
        idx = sb("idx_dst", [P, J + 2 * C])
        ask = [sb(f"ask{h}", [P, C], I32) for h in range(2)]
        got = [sb(f"got{h}", [P, C * T0W]) for h in range(2)]
        sc = [sb(f"scanned{h}", [P, C * S0W]) for h in range(2)]
        e = sb("logits", [P, C * H])
        arg = sb("exp_args", [P, C * 2 * H])
        ex = sb("exps", [P, C * 2 * H])
        prod = sb("p_times_x", [P, C * H * F])
        s_load, s_first, s_begin = sem("s_load"), sem("s_first"), sem("s_begin")
        s_ask = sem("s_ask")
        s_got = [sem(f"s_got{h}") for h in range(2)]
        s_arg, s_exp, s_done = sem("s_arg"), sem("s_exp"), sem("s_done")
        s_put = [sem(f"s_put{h}") for h in range(2)]
        block = ctx.enter_context(nc.Block())
        rec3 = m.recs[:, :].rearrange("p (j w) -> p j w", w=REC)

        @block.sync
        def _(sp):
            prime(sp, m, s_put)
            sp.dma_start(m.recs[:, :], m.rec[1:EP + 1, :].rearrange("(p j) w -> p (j w)", p=P)).then_inc(s_load, 16)
            sp.dma_start(prev[:, :], m.rec[0:EP, :].rearrange("(p j) w -> p j w", p=P)[:, 0, 0:1], allow_slow_non_contiguous=True).then_inc(s_load, 16)
            sp.dma_start(asrc[:, :], m.asrc_at.rearrange("(p j) h -> p (j h)", p=P)).then_inc(s_load, 16)
            out = m.s0[0:EP, :].rearrange("(p j) w -> p (j w)", p=P)
            with sp.Fori(0, TURNS) as it:
                for h in range(2):
                    sp.wait_ge(s_done, it * 2 + (h + 1))
                    sp.sem_inc(m.step_sp, 1)
                    sp.dma_start(out[:, bass.ds((it * 2 + h) * (C * S0W), C * S0W)], sc[h][:, :]).then_inc(s_put[h], 16)
            for h in range(2):
                sp.wait_ge(s_put[h], 16 + 16 * TURNS)

        @block.gpsimd
        def _(pool):
            pool.wait_ge(s_first, 1)
            pool.indirect_dma_start(out=first_a[:, :], out_offset=None, in_=m.asrc_t,
                                    in_offset=bass.IndirectOffsetOnAxis(ap=first[:, 0:1], axis=0)).then_inc(s_begin, 16)
            with pool.Fori(0, TURNS) as it:
                for h in range(2):
                    pool.wait_ge(s_ask, it * 2 + (h + 1))
                    pool.sem_inc(m.step_pool, 1)
                    for c in range(C):
                        pool.indirect_dma_start(out=got[h][:, c * T0W:(c + 1) * T0W], out_offset=None, in_=m.t0,
                                                in_offset=bass.IndirectOffsetOnAxis(ap=ask[h][:, c:c + 1], axis=0)).then_inc(s_got[h], 16)

        @block.vector
        def _(dve):
            dve.memset(idx[:, :], 0.0)
            dve.memset(sc[1][:, :], 0.0)
            dve.drain()
            dve.memset(sc[1][:, C * S0W - H:C * S0W], -BIG)
            dve.wait_ge(s_load, 48)
            dve.tensor_copy(first[:, :], rec3[:, 0, 0:1])
            dve.drain().then_inc(s_first, 1)
            dve.tensor_copy(idx[:, 0:J], rec3[:, :, 1])
            dve.tensor_tensor(m.same[:, 1:J], rec3[:, 1:J, 0], rec3[:, 0:J - 1, 0], ALU.is_equal)
            dve.tensor_tensor(m.same[:, 0:1], rec3[:, 0, 0:1], prev[:, :], ALU.is_equal)
            dve.drain()
            for h in range(2):
                dve.tensor_copy(ask[h][:, :], idx[:, h * C:(h + 1) * C])
            dve.drain().then_inc(s_ask, 2)
            dve.tensor_reduce(m.whole[0][:, :], m.same[:, :], AX, ALU.min)
            dve.wait_ge(s_begin, 16)
            for k in range(H):
                dve.tensor_tensor_scan(asrc[:, k::H], m.same[:, :], asrc[:, k::H], first_a[:, k:k + 1], ALU.mult, ALU.add)
            dve.drain()
            with dve.Fori(0, TURNS) as it:
                for h in range(2):
                    n = it * 2 + h
                    g3 = got[h][:, :].rearrange("p (c w) -> p c w", w=T0W)
                    s3 = sc[h][:, :].rearrange("p (c w) -> p c w", w=S0W)
                    before = sc[1 - h][:, (C - 1) * S0W:C * S0W]
                    e3 = e[:, :].rearrange("p (c h) -> p c h", h=H)
                    a3 = arg[:, :].rearrange("p (c w) -> p c w", w=2 * H)
                    x3 = ex[:, :].rearrange("p (c w) -> p c w", w=2 * H)
                    M = S0W - H
                    dve.wait_ge(s_got[h], (it + 1) * (16 * C))
                    dve.wait_ge(s_put[h], (it + 1) * 16)
                    dve.sem_inc(m.step_dve, 1)
                    dve.tensor_scalar(pen[:, :], m.same[:, bass.ds(n * C, C)], BIG, -BIG, ALU.mult, ALU.add)
                    dve.tensor_tensor(e3, g3[:, :, F:T0W], asrc[:, bass.ds(n * (C * H), C * H)].rearrange("p (c h) -> p c h", h=H), ALU.add)
                    dve.drain()
                    dve.scalar_tensor_tensor(e[:, :], e[:, :], 0.2, e[:, :], ALU.mult, ALU.max)
                    dve.drain()
                    for k in range(H):
                        dve.tensor_tensor_scan(s3[:, :, M + k], pen[:, :], e[:, k::H], before[:, M + k:M + k + 1], ALU.add, ALU.max)
                    dve.drain()
                    dve.tensor_tensor(a3[:, 1:C, 0:H], s3[:, 0:C - 1, M:S0W], s3[:, 1:C, M:S0W], ALU.subtract)
                    dve.tensor_tensor(a3[:, 0, 0:H], before[:, M:S0W], s3[:, 0, M:S0W], ALU.subtract)
                    dve.tensor_tensor(a3[:, :, H:2 * H], e3, s3[:, :, M:S0W], ALU.subtract)
                    dve.drain()
                    dve.tensor_scalar(arg[:, :], arg[:, :], 0.0, None, ALU.min)
                    dve.drain().then_inc(s_arg, 1)
                    dve.wait_ge(s_exp, n + 1)
                    dve.sem_inc(m.step_dve, 1)
                    dve.tensor_tensor(x3[:, :, 0:H], x3[:, :, 0:H], bcast(m.same[:, bass.ds(n * C, C)], 2, H), ALU.mult)
                    dve.tensor_tensor(prod[:, :].rearrange("p (c h f) -> p c h f", h=H, f=F),
                                      bcast(g3[:, :, 0:F], 2, H), bcast(x3[:, :, H:2 * H], 3, F), ALU.mult)
                    dve.drain()
                    for k in range(H):
                        dve.tensor_tensor_scan(s3[:, :, H * F + k], ex[:, k::2 * H], ex[:, H + k::2 * H], before[:, H * F + k:H * F + k + 1], ALU.mult, ALU.add)
                        for f in range(k * F, (k + 1) * F):
                            dve.tensor_tensor_scan(s3[:, :, f], ex[:, k::2 * H], prod[:, f::H * F], before[:, f:f + 1], ALU.mult, ALU.add)
                    dve.tensor_copy(ask[h][:, :], idx[:, bass.ds((n + 2) * C, C)])
                    dve.drain().then_inc(s_done, 1)
                    dve.sem_inc(s_ask, 1)
            dve.tensor_copy(m.fin[:, :], sc[1][:, (C - 1) * S0W:C * S0W])

        @block.scalar
        def _(act):
            with act.Fori(0, CHUNKS) as it:
                act.wait_ge(s_arg, it + 1)
                act.activation(ex[:, :], arg[:, :], ACT.Exp).then_inc(s_exp, 1)


def layer_norm(nc, m, dve, s_var, s_std, count):
    x3 = m.x[:, 0:B * F].rearrange("p (b f) -> p b f", f=F)
    q3 = m.sq[:, :].rearrange("p (b f) -> p b f", f=F)
    dve.tensor_reduce(m.mean[:, :], x3, AX, ALU.add)
    dve.drain()
    dve.tensor_scalar(m.mean[:, :], m.mean[:, :], 1.0 / F, None, ALU.mult)
    dve.drain()
    dve.tensor_tensor(x3, x3, bcast(m.mean[:, :], 2, F), ALU.subtract)
    dve.drain()
    dve.tensor_tensor(m.sq[:, :], m.x[:, 0:B * F], m.x[:, 0:B * F], ALU.mult)
    dve.drain()
    dve.tensor_reduce(m.var[:, :], q3, AX, ALU.add)
    dve.drain().then_inc(s_var, 1)
    dve.wait_ge(s_std, count)
    dve.reciprocal(m.std[:, :], m.std[:, :])
    dve.drain()
    dve.tensor_tensor(x3, x3, bcast(m.std[:, :], 2, F), ALU.mult)
    dve.drain()


def root(nc, m, act, s_var, s_std, count):
    act.wait_ge(s_var, count)
    act.activation(m.std[:, :], m.var[:, :], ACT.Sqrt, bias=m.eps[:, 0:1], scale=1.0 / F).then_inc(s_std, 1)


def stage_attend_nodes(nc, m, w0, bias0):
    HALF = B // 2
    HF = H * F
    with ExitStack() as ctx:
        def sb(name, shape, dt=F32):
            return ctx.enter_context(nc.sbuf_tensor(name, shape, dt))
        def sem(n):
            return ctx.enter_context(nc.semaphore(n))
        rep = sb("rep", [P, 3, HF])
        tr = sb("tr", [P, 4, P])
        mc = sb("mc", [P, P])
        dg = sb("dg", [P, 2, P])
        edg = sb("edg", [P, 2, P])
        gs = sb("gs", [P, 2, P])
        shifted = sb("shifted", [P, 3, P])
        table = sb("carry_table", [P, S0W])
        row = sb("carry_row_sb", [P, NN], BF16)
        sel = sb("sel", [P, 4, P])
        ge = sb("ends", [P, HALF * S0W])
        ce = sb("carries", [P, HALF * S0W])
        mm = sb("mm", [P, 3, HALF * H])
        arg = sb("arg2", [P, 2, HALF * H])
        ex = sb("ex2", [P, 2, HALF * H])
        at = sb("agg_t", [P, 2, P])
        ws = sb("w_stacked", [HF, F])
        bs = sb("bias_rows", [P, F])
        ps_t = ctx.enter_context(nc.psum_tensor("ps_tr", [P, 4 * P], F32))
        ps_b = ctx.enter_context(nc.psum_tensor("ps_back", [P, 3 * P], F32))
        ps_c = [ctx.enter_context(nc.psum_tensor(f"ps_c{i}", [P, 512], F32)) for i in range(2)]
        ps_a = [ctx.enter_context(nc.psum_tensor(f"ps_at{i}", [P, 512], F32)) for i in range(2)]
        ps_o = [ctx.enter_context(nc.psum_tensor(f"ps_o{i}", [P, 512], F32)) for i in range(2)]
        (s_w, s_end, s_rep, s_tr, s_dg, s_edg, s_shift, s_back, s_tab, s_sel, s_cps, s_cc, s_arg, s_ex, s_agg, s_at, s_atc,
         s_o, s_oc, s_var, s_std) = (sem(n) for n in (
             "s_w", "s_end", "s_rep", "s_tr", "s_dg", "s_edg", "s_shift", "s_back", "s_tab", "s_sel", "s_cps", "s_cc", "s_arg", "s_ex",
             "s_agg", "s_at", "s_atc", "s_o", "s_oc", "s_var", "s_std"))
        block = ctx.enter_context(nc.Block())

        @block.sync
        def _(sp):
            sp.dma_start(ws[:, :], w0.rearrange("h f o -> (h f) o")).then_inc(s_w, 16)
            sp.dma_start(bs[:, :], bias0.partition_broadcast(P)).then_inc(s_w, 16)
            sp.dma_start(row[:, :], m.carry_row[0].partition_broadcast(P)).then_inc(s_w, 16)
            sp.wait_ge(s_w, 48)

        @block.gpsimd
        def _(pool):
            for b in range(B):
                if b == HALF:
                    pool.wait_ge(s_agg, 1)
                o = b % HALF
                pool.indirect_dma_start(out=ge[:, o * S0W:(o + 1) * S0W], out_offset=None, in_=m.s0,
                                        in_offset=bass.IndirectOffsetOnAxis(ap=m.i_end[0][:, b:b + 1], axis=0)).then_inc(s_end, 16)

        @block.vector
        def _(dve):
            for i in range(2):
                dve.tensor_copy(rep[:, i, :].rearrange("p (h f) -> p h f", f=F), bcast(m.fin[:, HF + i * H:HF + (i + 1) * H], 2, F))
            dve.tensor_copy(rep[:, 2, :], m.whole[0][:, 0:1].broadcast_to([P, HF]))
            dve.drain().then_inc(s_rep, 1)
            dve.wait_ge(s_tr, 1)
            dve.tensor_copy(tr[:, :, :], ps_t[:, :].rearrange("p (a q) -> p a q", q=P))
            dve.drain()
            dve.tensor_scalar(dg[:, 0, :], tr[:, 3, :], BIG, -BIG, ALU.mult, ALU.add)
            dve.drain()
            dve.tensor_tensor_scan(mc[:, :], dg[:, 0, :], tr[:, 2, :], -BIG, ALU.add, ALU.max)
            dve.drain()
            dve.memset(dg[:, 0, 0:1], 0.0)
            dve.tensor_tensor(dg[:, 0, 1:P], mc[:, 0:P - 1], mc[:, 1:P], ALU.subtract)
            dve.tensor_tensor(dg[:, 1, :], tr[:, 2, :], mc[:, :], ALU.subtract)
            dve.drain()
            dve.tensor_scalar(dg[:, :, :], dg[:, :, :], 0.0, None, ALU.min)
            dve.drain().then_inc(s_dg, 1)
            dve.wait_ge(s_edg, 1)
            dve.tensor_tensor(edg[:, 0, :], edg[:, 0, :], tr[:, 3, :], ALU.mult)
            for i in range(2):
                dve.tensor_tensor(gs[:, i, :], tr[:, i, :], edg[:, 1, :], ALU.mult)
            dve.drain()
            for i in range(2):
                dve.tensor_tensor_scan(tr[:, i, :], edg[:, 0, :], gs[:, i, :], 0.0, ALU.mult, ALU.add)
            dve.memset(shifted[:, :, 0:1], 0.0)
            dve.drain()
            for i in range(2):
                dve.tensor_copy(shifted[:, i, 1:P], tr[:, i, 0:P - 1])
            dve.tensor_copy(shifted[:, 2, 1:P], mc[:, 0:P - 1])
            dve.drain().then_inc(s_shift, 1)
            dve.wait_ge(s_back, 1)
            dve.tensor_copy(table[:, 0:HF], ps_b[:, 0:P])
            for i in range(2):
                dve.tensor_copy(table[:, HF + i * H:HF + (i + 1) * H], ps_b[:, (i + 1) * P:(i + 2) * P:F])
            dve.drain().then_inc(s_tab, 1)
            dve.wait_ge(s_w, 48)
            x3 = m.x[:, 0:B * F].rearrange("p (b f) -> p b f", f=F)
            dve.tensor_tensor(x3, x3, bcast(bs[:, :], 1, B), ALU.add)
            for half in range(2):
                for b in range(half * HALF, (half + 1) * HALF):
                    if b >= 4:
                        dve.wait_ge(s_cps, b - 3)
                    dve.tensor_scalar(sel[:, b % 4, :], row[:, b * P:(b + 1) * P], m.part[:, 0:1], None, ALU.is_equal).then_inc(s_sel, 1)
                dve.wait_ge(s_cc, (half + 1) * HALF)
                dve.wait_ge(s_end, 16 * B if half else 16 * HALF)
                g3 = ge[:, :].rearrange("p (b w) -> p b w", w=S0W)
                c3 = ce[:, :].rearrange("p (b w) -> p b w", w=S0W)
                a3 = [arg[:, i, :].rearrange("p (b h) -> p b h", h=H) for i in range(2)]
                x2 = [ex[:, i, :].rearrange("p (b h) -> p b h", h=H) for i in range(2)]
                m3 = [mm[:, i, :].rearrange("p (b h) -> p b h", h=H) for i in range(3)]
                has = m.has[0][:, half * HALF:(half + 1) * HALF]
                M = HF + H
                dve.tensor_scalar(mm[:, 2, 0:HALF], has, BIG, -BIG, ALU.mult, ALU.add)
                dve.drain()
                dve.tensor_tensor(m3[0], c3[:, :, M:S0W], bcast(mm[:, 2, 0:HALF], 2, H), ALU.add)
                dve.drain()
                dve.tensor_tensor(m3[1], m3[0], g3[:, :, M:S0W], ALU.max)
                dve.drain()
                dve.tensor_tensor(a3[0], g3[:, :, M:S0W], m3[1], ALU.subtract)
                dve.tensor_tensor(a3[1], m3[0], m3[1], ALU.subtract)
                dve.drain().then_inc(s_arg, 1)
                dve.wait_ge(s_ex, half + 1)
                for i, t in enumerate((g3, c3)):
                    dve.tensor_tensor(t[:, :, HF:M], t[:, :, HF:M], x2[i], ALU.mult)
                    for k in range(H):
                        v = t[:, :, k * F:(k + 1) * F]
                        dve.tensor_tensor(v, v, bcast(x2[i][:, :, k], 2, F), ALU.mult)
                dve.drain()
                dve.tensor_tensor(g3[:, :, 0:M], g3[:, :, 0:M], c3[:, :, 0:M], ALU.add)
                dve.drain()
                dve.tensor_scalar(m3[2], g3[:, :, HF:M], 1.0e-30, float(H), ALU.max, ALU.mult)
                dve.drain()
                dve.reciprocal(mm[:, 2, :], mm[:, 2, :])
                dve.drain()
                if half == 1:
                    dve.wait_ge(s_at, HALF)
                for k in range(H):
                    dve.tensor_tensor(c3[:, :, k * F:(k + 1) * F], g3[:, :, k * F:(k + 1) * F], bcast(m3[2][:, :, k], 2, F), ALU.mult)
                dve.drain().then_inc(s_agg, 1)
                for b in range(half * HALF, (half + 1) * HALF):
                    dve.wait_ge(s_o, b + 1)
                    dve.tensor_tensor(m.x[:, b * F:(b + 1) * F], m.x[:, b * F:(b + 1) * F], ps_o[b % 2][:, 0:F], ALU.add).then_inc(s_oc, 1)
            dve.drain()
            layer_norm(nc, m, dve, s_var, s_std, 1)

        @block.tensor
        def _(pe):
            pe.wait_ge(s_rep, 1)
            pe.transpose(ps_t[:, 0:P], m.fin[:, 0:HF], m.ident[:, :])
            pe.transpose(ps_t[:, P:2 * P], rep[:, 0, :], m.ident[:, :])
            pe.transpose(ps_t[:, 2 * P:3 * P], rep[:, 1, :], m.ident[:, :])
            pe.transpose(ps_t[:, 3 * P:4 * P], rep[:, 2, :], m.ident[:, :]).then_inc(s_tr, 1)
            pe.wait_ge(s_shift, 1)
            for i in range(3):
                last = pe.transpose(ps_b[:, i * P:(i + 1) * P], shifted[:, i, :], m.ident[:, :])
            last.then_inc(s_back, 1)
            pe.wait_ge(s_tab, 1)
            pe.wait_ge(s_w, 48)
            for half in range(2):
                for b in range(half * HALF, (half + 1) * HALF):
                    pe.wait_ge(s_sel, b + 1)
                    if b >= 2:
                        pe.wait_ge(s_cc, b - 1)
                    pe.matmul(ps_c[b % 2][:, 0:S0W], sel[:, b % 4, :], table[:, :], start=True, stop=True).then_inc(s_cps, 1)
                pe.wait_ge(s_agg, half + 1)
                for b in range(half * HALF, (half + 1) * HALF):
                    o = b % HALF
                    if b >= 2:
                        pe.wait_ge(s_atc, b - 1)
                    pe.transpose(ps_a[b % 2][:, 0:P], ce[:, o * S0W:o * S0W + HF], m.ident[:, :]).then_inc(s_at, 1)
                    pe.wait_ge(s_atc, b + 1)
                    if b >= 2:
                        pe.wait_ge(s_oc, b - 1)
                    pe.matmul(ps_o[b % 2][:, 0:F], at[:, b % 2, :], ws[:, :], start=True, stop=True).then_inc(s_o, 1)

        @block.scalar
        def _(act):
            act.wait_ge(s_dg, 1)
            act.activation(edg[:, :, :], dg[:, :, :], ACT.Exp).then_inc(s_edg, 1)
            for half in range(2):
                if half == 1:
                    act.wait_ge(s_at, HALF)
                for b in range(half * HALF, (half + 1) * HALF):
                    o = b % HALF
                    act.wait_ge(s_cps, b + 1)
                    act.activation(ce[:, o * S0W:(o + 1) * S0W], ps_c[b % 2][:, 0:S0W], ACT.Copy).then_inc(s_cc, 1)
                act.wait_ge(s_arg, half + 1)
                act.activation(ex[:, :, :], arg[:, :, :], ACT.Exp).then_inc(s_ex, 1)
                for b in range(half * HALF, (half + 1) * HALF):
                    if b >= 2:
                        act.wait_ge(s_o, b - 1)
                    act.wait_ge(s_at, b + 1)
                    act.activation(at[:, b % 2, :], ps_a[b % 2][:, 0:P], ACT.Copy).then_inc(s_atc, 1)
            root(nc, m, act, s_var, s_std, 1)


def stage_spline_table(nc, m, w1):
    K = 16
    with ExitStack() as ctx:
        def sb(name, shape, dt=F32):
            return ctx.enter_context(nc.sbuf_tensor(name, shape, dt))
        def sem(n):
            return ctx.enter_context(nc.semaphore(n))
        wp = sb("w_padded", [P, 4, K * F])
        xt = sb("xt1", [P, 2, P])
        rows = [sb(f"t1_rows{i}", [P, CELLS * T1W]) for i in range(4)]
        ps_t = [ctx.enter_context(nc.psum_tensor(f"ps_t1{i}", [P, 512], F32)) for i in range(2)]
        ps_y = [ctx.enter_context(nc.psum_tensor(f"ps_y{i}", [P, 512], F32)) for i in range(4)]
        s_zero, s_w, s_xt, s_xc, s_y = (sem(n) for n in ("s_zero", "s_w", "s_xt", "s_xc", "s_y"))
        s_copied = [sem("s_copied_act"), sem("s_copied_dve")]
        s_out = [sem(f"s_out{i}") for i in range(4)]
        block = ctx.enter_context(nc.Block())

        def corners(b):
            t = rows[b % 4][:, :].rearrange("p (u v k o) -> p u v k o", u=3, v=3, k=4)
            y = ps_y[b % 4][:, :].rearrange("p (u v o) -> p u v o", u=4, v=4)
            for i in range(2):
                for j in range(2):
                    yield t[:, :, :, i * 2 + j, :], y[:, i:i + 3, j:j + 3, :]

        @block.sync
        def _(sp):
            sp.wait_ge(s_zero, 1)
            for b in range(4):
                sp.dma_start(wp[b * F:(b + 1) * F, b, :].rearrange("f (k o) -> f k o", o=F),
                             w1.rearrange("u v f o -> f (u v) o")).then_inc(s_w, 16)
            for b in range(B):
                sp.wait_ge(s_copied[b % 2], b // 2 + 1)
                sp.dma_start(m.t1[b * P * CELLS:(b + 1) * P * CELLS, :].rearrange("(p c) w -> p (c w)", c=CELLS),
                             rows[b % 4][:, :]).then_inc(s_out[b % 4], 16)
            for i in range(4):
                sp.wait_ge(s_out[i], 16 * len(range(i, B, 4)))

        @block.vector
        def _(dve):
            dve.memset(wp[:, :, :], 0.0).then_inc(s_zero, 1)
            for b in range(1, B, 2):
                dve.wait_ge(s_y, b + 1)
                if b >= 4:
                    dve.wait_ge(s_out[b % 4], 16 * (b // 4))
                for o, i in corners(b):
                    last = dve.tensor_copy(o, i)
                last.then_inc(s_copied[1], 1)

        @block.scalar
        def _(act):
            for b in range(0, B, 2):
                if b % 4 == 0:
                    g = b // 4
                    act.wait_ge(s_xt, g + 1)
                    act.activation(xt[:, g % 2, :], ps_t[g % 2][:, 0:P], ACT.Copy).then_inc(s_xc, 1)
                act.wait_ge(s_y, b + 1)
                if b >= 4:
                    act.wait_ge(s_out[b % 4], 16 * (b // 4))
                for o, i in corners(b):
                    last = act.activation(o, i, ACT.Copy)
                last.then_inc(s_copied[0], 1)

        @block.tensor
        def _(pe):
            pe.wait_ge(s_w, 64)
            for g in range(GROUPS):
                if g >= 2:
                    pe.wait_ge(s_xc, g - 1)
                pe.transpose(ps_t[g % 2][:, 0:P], m.x[:, g * P:(g + 1) * P], m.ident[:, :]).then_inc(s_xt, 1)
                pe.wait_ge(s_xc, g + 1)
                for b in range(4 * g, min(4 * g + 4, B)):
                    if b >= 4:
                        pe.wait_ge(s_copied[b % 2], b // 2 - 1)
                    pe.matmul(ps_y[b % 4][:, :], xt[:, g % 2, :], wp[:, b % 4, :], start=True, stop=True).then_inc(s_y, 1)


def stage_spline(nc, m):
    TURNS = CHUNKS // 2
    with ExitStack() as ctx:
        def sb(name, shape, dt=F32):
            return ctx.enter_context(nc.sbuf_tensor(name, shape, dt))
        def sem(n):
            return ctx.enter_context(nc.semaphore(n))
        w4 = sb("w4", [P, J * 4])
        idx = sb("idx_cell", [P, J + 2 * C])
        ask = [sb(f"ask1{h}", [P, C], I32) for h in range(2)]
        got = [sb(f"got1{h}", [P, C * T1W]) for h in range(2)]
        sc = [sb(f"scanned1{h}", [P, C * F]) for h in range(2)]
        cell = [sb(f"cell{a}", [P, J]) for a in range(2)]
        tent = sb("tent", [P, J])
        R = 4
        wa, wb = sb("w_lane", [P, R, P]), sb("w_block", [P, R, B])
        ps_w = ctx.enter_context(nc.psum_tensor("ps_w", [P, 512], F32))
        s_hot, s_used, s_sum = sem("s_hot"), sem("s_used"), sem("s_sum")
        msg = sb("msg", [P, C * F])
        s_ask, s_done = sem("s_ask"), sem("s_done")
        s_got = [sem(f"s_got{h}") for h in range(2)]
        s_put = [sem(f"s_put{h}") for h in range(2)]
        block = ctx.enter_context(nc.Block())
        rec3 = m.recs[:, :].rearrange("p (j w) -> p j w", w=REC)
        step = 2.0 / 3.0

        @block.sync
        def _(sp):
            prime(sp, m, s_put)
            out = m.s1[0:EP, :].rearrange("(p j) w -> p (j w)", p=P)
            with sp.Fori(0, TURNS) as it:
                for h in range(2):
                    sp.wait_ge(s_done, it * 2 + (h + 1))
                    sp.sem_inc(m.step_sp, 1)
                    sp.dma_start(out[:, bass.ds((it * 2 + h) * (C * F), C * F)], sc[h][:, :]).then_inc(s_put[h], 16)
            for h in range(2):
                sp.wait_ge(s_put[h], 16 + 16 * TURNS)

        @block.gpsimd
        def _(pool):
            with pool.Fori(0, TURNS) as it:
                for h in range(2):
                    pool.wait_ge(s_ask, it * 2 + (h + 1))
                    pool.sem_inc(m.step_pool, 1)
                    for c in range(C):
                        pool.indirect_dma_start(out=got[h][:, c * T1W:(c + 1) * T1W], out_offset=None, in_=m.t1,
                                                in_offset=bass.IndirectOffsetOnAxis(ap=ask[h][:, c:c + 1], axis=0)).then_inc(s_got[h], 16)

        @block.vector
        def _(dve):
            dve.memset(idx[:, :], 0.0)
            dve.memset(sc[1][:, :], 0.0)
            dve.drain()
            dve.tensor_scalar(idx[:, 0:J], rec3[:, :, 1], float(CELLS), None, ALU.mult)
            dve.drain()
            for a in range(2):
                u = rec3[:, :, 2 + a]
                dve.tensor_scalar(cell[a][:, :], u, -1.0 + step, None, ALU.is_ge)
                dve.drain()
                dve.scalar_tensor_tensor(cell[a][:, :], u, -1.0 + 2 * step, cell[a][:, :], ALU.is_ge, ALU.add)
                dve.drain()
                dve.scalar_tensor_tensor(idx[:, 0:J], cell[a][:, :], float(3 if a == 0 else 1), idx[:, 0:J], ALU.mult, ALU.add)
                dve.drain()
            for h in range(2):
                dve.tensor_copy(ask[h][:, :], idx[:, h * C:(h + 1) * C])
            dve.drain().then_inc(s_ask, 2)
            for a in range(2):
                dve.scalar_tensor_tensor(cell[a][:, :], cell[a][:, :], -step, rec3[:, :, 2 + a], ALU.mult, ALU.add)
                dve.drain()
                for i in range(2):
                    dve.tensor_scalar(tent[:, :], cell[a][:, :], 1.0 - step * i, None, ALU.add)
                    dve.drain()
                    dve.scalar_tensor_tensor(tent[:, :], tent[:, :], -1.0, tent[:, :], ALU.mult, ALU.max)
                    dve.drain()
                    dve.tensor_scalar(tent[:, :], tent[:, :], -1.0 / step, 1.0, ALU.mult, ALU.add)
                    dve.drain()
                    for j in range(2):
                        if a == 0:
                            dve.tensor_scalar(w4[:, 2 * i + j::4], tent[:, :], 0.0, None, ALU.max)
                        else:
                            dve.scalar_tensor_tensor(w4[:, 2 * j + i::4], tent[:, :], 0.0, w4[:, 2 * j + i::4], ALU.max, ALU.mult)
                    dve.drain()
            with dve.Fori(0, TURNS) as it:
                for h in range(2):
                    n = it * 2 + h
                    dve.wait_ge(s_got[h], (it + 1) * (16 * C))
                    dve.wait_ge(s_put[h], (it + 1) * 16)
                    dve.sem_inc(m.step_dve, 1)
                    for c in range(C):
                        dve.wait_ge(s_used, n * C + (c + 1))
                        dve.tensor_scalar(wa[:, c % R, :], m.lane[:, :], m.lo[1][:, bass.ds(n * C + c, 1)], None, ALU.is_equal)
                        dve.tensor_scalar(wb[:, c % R, :], m.lane[:, 0:B], m.hi[1][:, bass.ds(n * C + c, 1)],
                                          m.w[:, bass.ds(n * C + c, 1)], ALU.is_equal, ALU.mult).then_inc(s_hot, 1)
                    g3 = got[h][:, :].rearrange("p (c f) -> p c f", f=F)
                    dve.tensor_tensor(g3, g3, bcast(w4[:, bass.ds(n * (C * 4), C * 4)], 2, F), ALU.mult)
                    dve.drain()
                    dve.tensor_reduce(msg[:, :].rearrange("p (c f) -> p c f", f=F),
                                      got[h][:, :].rearrange("p (c k f) -> p c f k", k=4, f=F), AX, ALU.add)
                    dve.drain()
                    for f in range(F):
                        dve.tensor_tensor_scan(sc[h][:, f::F], m.same[:, bass.ds(n * C, C)], msg[:, f::F],
                                               sc[1 - h][:, (C - 1) * F + f:(C - 1) * F + f + 1], ALU.mult, ALU.add)
                    dve.tensor_copy(ask[h][:, :], idx[:, bass.ds((n + 2) * C, C)])
                    dve.drain().then_inc(s_done, 1)
                    dve.sem_inc(s_ask, 1)
            dve.tensor_copy(m.fin[:, 0:F], sc[1][:, (C - 1) * F:C * F])
            dve.wait_ge(s_sum, 1)
            dve.tensor_copy(m.sumw[:, :], ps_w[:, 0:B])

        @block.tensor
        def _(pe):
            pe.matmul(ps_w[:, 0:B], m.zero[:, :], m.zero[:, 0:B], start=True, stop=False)
            pe.sem_inc(s_used, R)
            with pe.Fori(0, J // R) as it:
                for c in range(R):
                    pe.wait_ge(s_hot, it * R + (c + 1))
                    pe.sem_inc(m.step_pe, 1)
                    pe.matmul(ps_w[:, 0:B], wa[:, c, :], wb[:, c, :], start=False, stop=False).then_inc(s_used, 1)
            pe.matmul(ps_w[:, 0:B], m.zero[:, :], m.zero[:, 0:B], start=False, stop=True).then_inc(s_sum, 1)


def node_sums(nc, m, ctx, block, k, sums, then_dve, then_pe, then_act, then_sp=None, loads=0, s_w=None):
    def sb(name, shape, dt=F32):
        return ctx.enter_context(nc.sbuf_tensor(f"{name}{k}", shape, dt))
    def sem(n):
        return ctx.enter_context(nc.semaphore(n))
    PER = 16
    banks = -(-B // PER)
    rep = sb("rep_s", [P, F])
    tr = sb("tr_s", [F, 2, P])
    shifted = sb("shifted_s", [F, P])
    table = sb("table_s", [P, F])
    row = sb("row_s", [P, NN], BF16)
    sel = sb("sel_s", [P, 4, P])
    ge = sb("ends_s", [P, B * F])
    ps_t = ctx.enter_context(nc.psum_tensor(f"ps_ts{k}", [P, 512], F32))
    ps_c = [ctx.enter_context(nc.psum_tensor(f"ps_cs{k}{i}", [P, 512], F32)) for i in range(2)]
    s_row, s_end, s_carry, s_turned, s_sel, s_cps, s_cc = (sem(n) for n in (
        "s_row", "s_end", "s_carry", "s_turned", "s_sel", "s_cps", "s_cc"))

    @block.sync
    def _(sp):
        sp.dma_start(row[:, :], m.carry_row[k].partition_broadcast(P)).then_inc(s_row, 16)
        sp.wait_ge(s_row, 16)
        if then_sp:
            then_sp(sp)

    @block.gpsimd
    def _(pool):
        for b in range(B):
            pool.indirect_dma_start(out=ge[:, b * F:(b + 1) * F], out_offset=None, in_=sums,
                                    in_offset=bass.IndirectOffsetOnAxis(ap=m.i_end[k][:, b:b + 1], axis=0)).then_inc(s_end, 16)

    @block.vector
    def _(dve):
        dve.tensor_copy(rep[:, :], m.whole[k][:, 0:1].broadcast_to([P, F]))
        dve.drain().then_inc(s_carry, 1)
        dve.wait_ge(s_turned, 1)
        dve.tensor_copy(tr[:, :, :], ps_t[0:F, 0:2 * P].rearrange("p (a q) -> p a q", q=P))
        dve.memset(shifted[:, 0:1], 0.0)
        dve.drain()
        dve.tensor_tensor_scan(shifted[:, 1:P], tr[:, 1, 0:P - 1], tr[:, 0, 0:P - 1], 0.0, ALU.mult, ALU.add)
        dve.drain().then_inc(s_carry, 1)
        dve.wait_ge(s_turned, 2)
        dve.tensor_copy(table[:, :], ps_t[:, 2 * P:2 * P + F])
        dve.drain().then_inc(s_carry, 1)
        dve.wait_ge(s_row, 16)
        for b in range(B):
            if b >= 4:
                dve.wait_ge(s_cps, b - 3)
            dve.tensor_scalar(sel[:, b % 4, :], row[:, b * P:(b + 1) * P], m.part[:, 0:1], None, ALU.is_equal).then_inc(s_sel, 1)
            if (b + 1) % PER == 0 or b == B - 1:
                q, w = b // PER, (b % PER + 1) * F
                dve.wait_ge(s_end, 16 * B)
                dve.wait_ge(s_cps, b + 1)
                g = ge[:, q * PER * F:q * PER * F + w]
                dve.tensor_tensor(g, g, ps_c[q % 2][:, 0:w], ALU.add).then_inc(s_cc, 1)
        dve.drain()
        then_dve(dve, ge)

    @block.tensor
    def _(pe):
        pe.wait_ge(s_carry, 1)
        pe.transpose(ps_t[0:F, 0:P], m.fin[:, 0:F], m.ident[:, :])
        pe.transpose(ps_t[0:F, P:2 * P], rep[:, :], m.ident[:, :]).then_inc(s_turned, 1)
        pe.wait_ge(s_carry, 2)
        pe.transpose(ps_t[:, 2 * P:2 * P + F], shifted[:, :], m.ident[0:F, 0:F]).then_inc(s_turned, 1)
        pe.wait_ge(s_carry, 3)
        for b in range(B):
            q = b // PER
            pe.wait_ge(s_sel, b + 1)
            if b % PER == 0 and q >= 2:
                pe.wait_ge(s_cc, q - 1)
            pe.matmul(ps_c[q % 2][:, (b % PER) * F:(b % PER + 1) * F], sel[:, b % 4, :], table[:, :], start=True, stop=True).then_inc(s_cps, 1)
        then_pe(pe)

    @block.scalar
    def _(act):
        then_act(act)


def stage_spline_nodes(nc, m):
    with ExitStack() as ctx:
        s_var = ctx.enter_context(nc.semaphore("s_var"))
        s_std = ctx.enter_context(nc.semaphore("s_std"))
        block = ctx.enter_context(nc.Block())

        def dve_part(dve, ge):
            dve.tensor_tensor(m.x[:, 0:B * F], m.x[:, 0:B * F], ge[:, :], ALU.add)
            dve.drain()
            layer_norm(nc, m, dve, s_var, s_std, 1)
            x3 = m.x[:, 0:B * F].rearrange("p (b f) -> p b f", f=F)
            q3 = m.sq[:, :].rearrange("p (b f) -> p b f", f=F)
            dve.tensor_tensor(q3, x3, bcast(m.sumw[:, :], 2, F), ALU.mult)
            dve.drain()
            dve.tensor_tensor(m.x[:, 0:B * F], m.x[:, 0:B * F], m.sq[:, :], ALU.add)
            dve.drain()
            layer_norm(nc, m, dve, s_var, s_std, 2)

        def act_part(act):
            root(nc, m, act, s_var, s_std, 1)
            root(nc, m, act, s_var, s_std, 2)

        node_sums(nc, m, ctx, block, 0, m.s1, dve_part, lambda pe: None, act_part)


def stage_starts(nc, m):
    with ExitStack() as ctx:
        s_sc = ctx.enter_context(nc.semaphore("s_sc"))
        s_x = ctx.enter_context(nc.semaphore("s_x"))
        block = ctx.enter_context(nc.Block())

        @block.sync
        def _(sp):
            sp.dma_start(m.x3t.rearrange("(b p) f -> p b f", p=P), m.x[:, 0:B * F].rearrange("p (b f) -> p b f", f=F)).then_inc(s_x, 16)
            sp.wait_ge(s_x, 16)

        @block.gpsimd
        def _(pool):
            for b in range(B):
                pool.indirect_dma_start(out=m.h3, out_offset=bass.IndirectOffsetOnAxis(ap=m.i_start[:, b:b + 1], axis=0),
                                        in_=m.x[:, b * F:(b + 1) * F], in_offset=None,
                                        bounds_check=EP - 1, oob_is_err=False).then_inc(s_sc, 16)
            pool.wait_ge(s_sc, 16 * B)


def stage_exchange(nc, m):
    TURNS = CHUNKS // 2
    with ExitStack() as ctx:
        def sb(name, shape, dt=F32):
            return ctx.enter_context(nc.sbuf_tensor(name, shape, dt))
        def sem(n):
            return ctx.enter_context(nc.semaphore(n))
        first = sb("first3", [P, 1], I32)
        first_x = sb("first_x", [P, F])
        starts = [sb(f"starts{h}", [P, C * F]) for h in range(2)]
        rows = [sb(f"xd_rows{h}", [P, C * XDW]) for h in range(2)]
        to = [sb(f"to{h}", [P, C], I32) for h in range(2)]
        w = Places(nc, ctx, "1")
        lo_b, hi_b = sb("dst_lane_b", [P, J], BF16), sb("dst_block_b", [P, J], BF16)
        zero = sb("zero_b3", [P, P], BF16)
        oa = [sb(f"dst_onelane{h}", [P, C, P], BF16) for h in range(2)]
        ob = [sb(f"dst_oneblock{h}", [P, C, B], BF16) for h in range(2)]
        ps_n = ctx.enter_context(nc.psum_tensor("ps_count_dst", [P, 512], F32))
        s_first, s_begin, s_done, s_free = (sem(n) for n in ("s_first", "s_begin", "s_done", "s_free"))
        s_made, s_used, s_sum, s_st = (sem(n) for n in ("s_made", "s_used", "s_sum", "s_st"))
        s_in = [sem(f"s_in{h}") for h in range(2)]
        s_sent = [sem(f"s_sent{h}") for h in range(2)]
        block = ctx.enter_context(nc.Block())
        rec3 = m.recs[:, :].rearrange("p (j w) -> p j w", w=REC)
        reci = m.recs[:, :].bitcast(I32)

        @block.sync
        def _(sp):
            src = m.h3.rearrange("(p j) f -> p (j f)", p=P)
            with sp.Fori(0, TURNS) as it:
                for h in range(2):
                    sp.wait_ge(s_free, it * 2 + (h + 1))
                    sp.sem_inc(m.step_sp, 1)
                    sp.dma_start(starts[h][:, :], src[:, bass.ds((it * 2 + h) * (C * F), C * F)]).then_inc(s_in[h], 16)
            sp.wait_ge(w.s_vc, 1)
            sp.dma_start(m.carry_row[1].rearrange("(b p) -> b p", p=P), w.vb[:, 1, :]).then_inc(s_st, 16)
            sp.wait_ge(s_st, 16)

        @block.gpsimd
        def _(pool):
            prime(pool, m, s_sent)
            pool.wait_ge(s_first, 1)
            pool.indirect_dma_start(out=first_x[:, :], out_offset=None, in_=m.x3t,
                                    in_offset=bass.IndirectOffsetOnAxis(ap=first[:, 0:1], axis=0)).then_inc(s_begin, 16)
            with pool.Fori(0, TURNS) as it:
                for h in range(2):
                    pool.wait_ge(s_done, it * 2 + (h + 1))
                    pool.sem_inc(m.step_pool, 1)
                    for c in range(C):
                        pool.indirect_dma_start(out=m.xd, out_offset=bass.IndirectOffsetOnAxis(ap=to[h][:, c:c + 1], axis=0),
                                                in_=rows[h][:, c * XDW:(c + 1) * XDW], in_offset=None).then_inc(s_sent[h], 16)
            for h in range(2):
                pool.wait_ge(s_sent[h], 16 + 16 * C * TURNS)

        @block.vector
        def _(dve):
            dve.sem_inc(s_free, 2)
            dve.memset(w.zb[:, :], 0.0)
            dve.memset(zero[:, :], 0.0)
            dve.tensor_copy(first[:, :], rec3[:, 0, 0:1])
            dve.drain().then_inc(s_first, 1)
            dve.tensor_copy(lo_b[:, :], m.lo[1][:, 0:J])
            dve.tensor_copy(hi_b[:, :], m.hi[1][:, 0:J])
            dve.wait_ge(s_begin, 16)
            dve.tensor_copy(rows[1][:, (C - 1) * XDW:(C - 1) * XDW + F], first_x[:, :])
            dve.drain()
            with dve.Fori(0, TURNS) as it:
                for h in range(2):
                    n = it * 2 + h
                    dve.wait_ge(s_in[h], (it + 1) * 16)
                    dve.wait_ge(s_sent[h], it * (16 * C) + 16)
                    dve.sem_inc(m.step_dve, 1)
                    for f in range(F):
                        dve.tensor_tensor_scan(rows[h][:, f::XDW], m.same[:, bass.ds(n * C, C)], starts[h][:, f::F],
                                               rows[1 - h][:, (C - 1) * XDW + f:(C - 1) * XDW + f + 1], ALU.mult, ALU.add)
                    dve.tensor_copy(rows[h][:, F::XDW], m.recs[:, bass.ds(n * (C * REC), C * REC)].rearrange("p (c w) -> p c w", w=REC)[:, :, 1])
                    dve.tensor_copy(to[h][:, :], reci[:, bass.ds(n * (C * REC), C * REC)].rearrange("p (c w) -> p c w", w=REC)[:, :, 4])
                    dve.drain().then_inc(s_done, 1)
                    dve.sem_inc(s_free, 1)
                    dve.wait_ge(s_used, it * 2 + (h + 1))
                    dve.sem_inc(m.step_dve, 1)
                    dve.tensor_tensor(oa[h][:, :, :], bcast(m.lane_b[:, :], 1, C), bcast(lo_b[:, bass.ds(n * C, C)], 2, P), ALU.is_equal)
                    dve.tensor_tensor(ob[h][:, :, :], bcast(m.lane_b[:, 0:B], 1, C), bcast(hi_b[:, bass.ds(n * C, C)], 2, B), ALU.is_equal).then_inc(s_made, 1)
            dve.wait_ge(s_sum, 1)
            dve.tensor_copy(m.cnt[1][:, :], ps_n[:, 0:B])
            dve.drain().then_inc(s_used, 1)
            places_dve(dve, m, w, 1, 0)

        @block.tensor
        def _(pe):
            pe.wait_ge(s_first, 1)
            pe.matmul(ps_n[:, 0:B], zero[:, :], zero[:, 0:B], start=True, stop=False)
            pe.sem_inc(s_used, 2)
            with pe.Fori(0, TURNS) as it:
                for h in range(2):
                    pe.wait_ge(s_made, it * 2 + (h + 1))
                    pe.sem_inc(m.step_pe, 1)
                    for c in range(C):
                        last = pe.matmul(ps_n[:, 0:B], oa[h][:, c, :], ob[h][:, c, :], start=False, stop=False)
                    last.then_inc(s_used, 1)
            pe.matmul(ps_n[:, 0:B], zero[:, :], zero[:, 0:B], start=False, stop=True).then_inc(s_sum, 1)
            pe.wait_ge(s_used, CHUNKS + 3)
            places_pe(pe, m, w, 1, 0)


def stage_neighbours(nc, m):
    C = J // 8
    TURNS = J // (2 * C)
    with ExitStack() as ctx:
        def sb(name, shape, dt=F32):
            return ctx.enter_context(nc.sbuf_tensor(name, shape, dt))
        def sem(n):
            return ctx.enter_context(nc.semaphore(n))
        rows = [sb(f"rows3{h}", [P, C * XDW]) for h in range(2)]
        sc = [sb(f"scanned3{h}", [P, C * F]) for h in range(2)]
        same = sb("same_d", [P, C])
        low = sb("low", [P, 1])
        prev = sb("prev_d", [P, 1])
        s_prev, s_done, s_free = (sem(n) for n in ("s_prev", "s_done", "s_free"))
        s_in = [sem(f"s_in{h}") for h in range(2)]
        s_put = [sem(f"s_put{h}") for h in range(2)]
        block = ctx.enter_context(nc.Block())

        @block.sync
        def _(sp):
            sp.dma_start(prev[:, :], m.xd[0:EP, :].rearrange("(p j) w -> p j w", p=P)[:, 0, F:XDW], allow_slow_non_contiguous=True).then_inc(s_prev, 16)
            src = m.xd[1:EP + 1, :].rearrange("(p j) w -> p (j w)", p=P)
            with sp.Fori(0, TURNS) as it:
                for h in range(2):
                    sp.wait_ge(s_free, it * 2 + (h + 1))
                    sp.sem_inc(m.step_sp, 1)
                    sp.dma_start(rows[h][:, :], src[:, bass.ds((it * 2 + h) * (C * XDW), C * XDW)]).then_inc(s_in[h], 16)

        @block.scalar
        def _(act):
            prime(act, m, s_put)
            out = m.s3[0:EP, :].rearrange("(p j) w -> p (j w)", p=P)
            with act.Fori(0, TURNS) as it:
                for h in range(2):
                    act.wait_ge(s_done, it * 2 + (h + 1))
                    act.sem_inc(m.step_act, 1)
                    act.dma_start(out[:, bass.ds((it * 2 + h) * (C * F), C * F)], sc[h][:, :]).then_inc(s_put[h], 16)
            for h in range(2):
                act.wait_ge(s_put[h], 16 + 16 * TURNS)

        @block.vector
        def _(dve):
            dve.sem_inc(s_free, 2)
            dve.memset(sc[1][:, :], 0.0)
            dve.memset(m.whole[1][:, :], 1.0)
            dve.drain()
            dve.wait_ge(s_prev, 16)
            with dve.Fori(0, TURNS) as it:
                for h in range(2):
                    n = it * 2 + h
                    dve.wait_ge(s_in[h], (it + 1) * 16)
                    dve.wait_ge(s_put[h], (it + 1) * 16)
                    dve.sem_inc(m.step_dve, 1)
                    key = rows[h][:, F::XDW]
                    dve.tensor_tensor(same[:, 1:C], key[:, 1:C], key[:, 0:C - 1], ALU.is_equal)
                    dve.tensor_tensor(same[:, 0:1], key[:, 0:1], prev[:, :], ALU.is_equal)
                    dve.drain()
                    dve.tensor_copy(prev[:, :], key[:, C - 1:C])
                    dve.tensor_reduce(low[:, :], same[:, :], AX, ALU.min)
                    dve.drain()
                    dve.tensor_tensor(m.whole[1][:, :], m.whole[1][:, :], low[:, :], ALU.min)
                    for f in range(F):
                        dve.tensor_tensor_scan(sc[h][:, f::F], same[:, :], rows[h][:, f::XDW],
                                               sc[1 - h][:, (C - 1) * F + f:(C - 1) * F + f + 1], ALU.mult, ALU.add)
                    dve.drain().then_inc(s_done, 1)
                    dve.sem_inc(s_free, 1)
            dve.tensor_copy(m.fin[:, 0:F], sc[1][:, (C - 1) * F:C * F])


def stage_neighbour_nodes(nc, m, w3, b3, out):
    with ExitStack() as ctx:
        def sb(name, shape, dt=F32):
            return ctx.enter_context(nc.sbuf_tensor(name, shape, dt))
        def sem(n):
            return ctx.enter_context(nc.semaphore(n))
        ws = sb("w3_sb", [2 * F, F])
        bs = sb("b3_rows", [P, F])
        cat = sb("cat", [P, B * 2 * F])
        inv = sb("inv", [P, B])
        ct = sb("cat_t", [2 * F, 2, P])
        ps_x = [ctx.enter_context(nc.psum_tensor(f"ps_x3{i}", [P, 512], F32)) for i in range(2)]
        ps_o = [ctx.enter_context(nc.psum_tensor(f"ps_o3{i}", [P, 512], F32)) for i in range(2)]
        s_var, s_std, s_w, s_cat, s_ct, s_ctc, s_o, s_oc, s_fin, s_out = (
            sem(n) for n in ("s_var", "s_std", "s_w", "s_cat", "s_ct", "s_ctc", "s_o", "s_oc", "s_fin", "s_out"))
        block = ctx.enter_context(nc.Block())

        def sp_part(sp):
            sp.dma_start(ws[:, :], w3).then_inc(s_w, 16)
            sp.dma_start(bs[:, :], b3.partition_broadcast(P)).then_inc(s_w, 16)
            sp.wait_ge(s_fin, 1)
            sp.dma_start(out[0:(B - 1) * P, :].rearrange("(b p) f -> p b f", p=P),
                         m.x[:, 0:(B - 1) * F].rearrange("p (b f) -> p b f", f=F)).then_inc(s_out, 16)
            sp.dma_start(out[(B - 1) * P:N, :], m.x[0:LASTBLOCK, (B - 1) * F:B * F]).then_inc(s_out, 16)
            sp.wait_ge(s_out, 32)

        def dve_part(dve, ge):
            c3 = cat[:, :].rearrange("p (b w) -> p b w", w=2 * F)
            x3 = m.x[:, 0:B * F].rearrange("p (b f) -> p b f", f=F)
            dve.tensor_scalar(inv[:, :], m.cnt[1][:, :], 1.0, None, ALU.max)
            dve.tensor_copy(c3[:, :, 0:F], x3)
            dve.drain()
            dve.reciprocal(inv[:, :], inv[:, :])
            dve.drain()
            dve.tensor_tensor(c3[:, :, F:2 * F], ge[:, :].rearrange("p (b f) -> p b f", f=F), bcast(inv[:, :], 2, F), ALU.mult)
            dve.drain().then_inc(s_cat, 1)
            dve.wait_ge(s_w, 32)
            for b in range(B):
                q = m.sq[:, b * F:(b + 1) * F]
                dve.wait_ge(s_o, b + 1)
                dve.tensor_tensor(q, ps_o[b % 2][:, 0:F], bs[:, :], ALU.add).then_inc(s_oc, 1)
            dve.drain()
            dve.scalar_tensor_tensor(m.x[:, 0:B * F], m.sq[:, :], 0.0, m.x[:, 0:B * F], ALU.max, ALU.add)
            dve.drain()
            layer_norm(nc, m, dve, s_var, s_std, 1)
            dve.drain().then_inc(s_fin, 1)

        def pe_part(pe):
            pe.wait_ge(s_cat, 1)
            pe.wait_ge(s_w, 32)
            for b in range(B):
                if b >= 2:
                    pe.wait_ge(s_ctc, b - 1)
                pe.transpose(ps_x[b % 2][0:2 * F, 0:P], cat[:, b * 2 * F:(b + 1) * 2 * F], m.ident[:, :]).then_inc(s_ct, 1)
                pe.wait_ge(s_ctc, b + 1)
                if b >= 2:
                    pe.wait_ge(s_oc, b - 1)
                pe.matmul(ps_o[b % 2][:, 0:F], ct[:, b % 2, :], ws[:, :], start=True, stop=True).then_inc(s_o, 1)

        def act_part(act):
            for b in range(B):
                if b >= 2:
                    act.wait_ge(s_o, b - 1)
                act.wait_ge(s_ct, b + 1)
                act.activation(ct[:, b % 2, :], ps_x[b % 2][0:2 * F, 0:P], ACT.Copy).then_inc(s_ctc, 1)
            root(nc, m, act, s_var, s_std, 1)

        node_sums(nc, m, ctx, block, 1, m.s3, dve_part, pe_part, act_part, sp_part)


class Memory:
    pass


def gnn(nc, x, src, dst, edge_attr_2, edge_weight, w0, fc_w, fc_b, bias0, w1, w3, b3, out):
    m = Memory()

    def dram(name, shape, dt=F32):
        return nc.dram_tensor(f"{name}_dram", shape, dt).ap()

    m.keyrow = [dram(f"keyrow{k}", (EP,), I16) for k in range(2)]
    m.lorow = [dram(f"lorow{k}", (EP,), BF16) for k in range(2)]
    m.carry_row = [dram(f"carry_row{k}", (NN,), BF16) for k in range(2)]
    m.rec = dram("rec", (EP + 1, REC))
    m.xd = dram("xd", (EP + 1, XDW))
    m.t0, m.asrc_t, m.asrc_at = dram("t0", (NN, T0W)), dram("asrc_t", (NN, H)), dram("asrc_at", (EP, H))
    m.t1 = dram("t1", (NN * CELLS, T1W))
    m.x3t, m.h3 = dram("x3t", (NN, F)), dram("h3", (EP, F))
    m.s0, m.s1, m.s3 = dram("s0", (EP + 1, S0W)), dram("s1", (EP + 1, F)), dram("s3", (EP + 1, F))

    with ExitStack() as ctx:
        def sb(name, shape, dt=F32):
            return ctx.enter_context(nc.sbuf_tensor(name, shape, dt))
        m.step_pool, m.step_sp, m.step_act, m.step_dve, m.step_pe = (
            ctx.enter_context(nc.semaphore(f"step_{n}")) for n in ("pool", "sp", "act", "dve", "pe"))
        m.x = sb("x_sb", [P, GROUPS * 4 * F])
        m.sq = sb("sq", [P, B * F])
        m.mean, m.var, m.std = sb("mean", [P, B]), sb("var", [P, B]), sb("std", [P, B])
        m.lane, m.lane_b, m.part = sb("lane", [P, P]), sb("lane_b", [P, P], BF16), sb("part_index", [P, 1])
        m.ident, m.above, m.below, m.ones, m.zero, m.undo = (sb(n, [P, P]) for n in ("ident", "above", "below", "ones", "zero", "undo"))
        m.cnt_first, m.next_half = sb("cnt_first", [P, B]), sb("next_half", [P, B])
        m.unsorted = sb("unsorted", [P, 1], I32)
        m.minus, m.eps = sb("minus", [P, XDW]), sb("eps", [P, 1])
        m.cnt, m.start, m.next, m.has = ([sb(f"{n}{k}", [P, B]) for k in range(2)] for n in ("cnt", "start", "next", "has"))
        m.i_end = [sb(f"i_end{k}", [P, B], I32) for k in range(2)]
        m.i_start = sb("i_start", [P, B], I32)
        m.sumw = sb("sumw", [P, B])
        m.spare, m.primed, m.first_word = sb("spare", [1, 16]), 0, x[0:1, 0:1]
        m.fin = sb("fin", [P, S0W])
        m.whole = [sb(f"whole{k}", [P, 1]) for k in range(2)]
        m.recs = sb("recs_sb", [P, J * REC])
        m.same = sb("same", [P, J])
        m.lo, m.hi = [None, sb("lo1", [P, J + 4])], [None, sb("hi1", [P, J + 4])]
        with ExitStack() as middle:
            def sm(name, shape, dt=F32):
                return middle.enter_context(nc.sbuf_tensor(name, shape, dt))
            m.w = sm("w", [P, J])
            with ExitStack() as front:
                def sf(name, shape, dt=F32):
                    return front.enter_context(nc.sbuf_tensor(name, shape, dt))
                m.key = [sf(f"key{k}", [P, J]) for k in range(2)]
                m.attr, m.lo[0], m.hi[0] = m.recs[:, 0:2 * J], m.recs[:, 2 * J:3 * J + 4], m.recs[:, 3 * J:4 * J + 4]
                m.natural = m.recs[:, 4 * J:5 * J].bitcast(I32)
                with ExitStack() as early:
                    def se(name, shape, dt=F32):
                        return early.enter_context(nc.sbuf_tensor(name, shape, dt))
                    m.lo_b, m.hi_b = ([se(f"{n}{k}", [P, J], BF16) for k in range(2)] for n in ("lo_b", "hi_b"))
                    m.half_minus_lo = [se(f"half_minus_lo{k}", [P, J]) for k in range(2)]
                    m.zeros = se("zeros_f", [P, H * J])
                    stage_load(nc, m, x, src, dst, edge_attr_2, edge_weight)
                    stage_count(nc, m)
                stage_places(nc, m, w0, fc_w, fc_b)
                stage_rank(nc, m)
            stage_attend(nc, m)
            stage_attend_nodes(nc, m, w0, bias0)
            stage_spline_table(nc, m, w1)
            stage_spline(nc, m)
        stage_spline_nodes(nc, m)
        stage_starts(nc, m)
        stage_exchange(nc, m)
        stage_neighbours(nc, m)
        stage_neighbour_nodes(nc, m, w3, b3, out)


_INS = ['x', 'src', 'dst', 'edge_attr_2', 'edge_weight', 'L0_gnn_w', 'L0_gnn_fc_w', 'L0_gnn_fc_b', 'L0_gnn_bias',
        'L1_gnn_weight', 'L3_gnn_W', 'L3_gnn_b']
_OUTS = [((N, F), 'float32')]


def kernel(**inputs):
    import numpy as _np
    import concourse.bacc as _bacc
    from concourse import mybir as _mybir
    from concourse.bass_utils import run_bass_kernel_spmd as _run

    nc = _bacc.Bacc("TRN2", target_bir_lowering=False, num_devices=1)
    arrays, args = {}, []
    for name in _INS:
        a = _np.ascontiguousarray(inputs[name])
        arrays[f"in_{name}_dram"] = a
        args.append(nc.dram_tensor(f"in_{name}_dram", a.shape, _mybir.dt.from_np(a.dtype), kind="ExternalInput").ap())
    for i, (shape, dtype) in enumerate(_OUTS):
        dt = _mybir.dt.from_np(_np.dtype(dtype))
        args.append(nc.dram_tensor(f"out_{i}_dram", shape, dt, kind="ExternalOutput").ap())
    gnn(nc, *args)
    r = _run(nc, [arrays], core_ids=[0])
    got = tuple(r.results[0][f"out_{i}_dram"] for i in range(len(_OUTS)))
    return got[0]
```

```python
import numpy as np
from contextlib import ExitStack

import concourse.bass as bass
from concourse import mybir

F32 = mybir.dt.float32
I32 = mybir.dt.int32
I16 = mybir.dt.int16
BF16 = mybir.dt.bfloat16
ALU = mybir.AluOpType
ACT = mybir.ActivationFunctionType
AX = mybir.AxisListType.X

P = 128
N = 12500
E = 212500
F = 32
H = 4
B = -(-N // P)
NN = B * P
PAD = NN - 1
C = 32
J = -(-E // (P * 2 * C)) * 2 * C
EP = P * J
CHUNKS = J // C
LASTROW = E - (P - 1) * J
LASTBLOCK = N - (B - 1) * P
GROUPS = -(-B // 4)
REC = 5
T0W = F + H
S0W = H * F + 2 * H
K = 4
KK = K * K
T1W = (K + 2) * F
XDW = F + 1
SPLIT = 2 * -(-B // 4)
PARTS = ((0, SPLIT), (SPLIT, B))
BIG = 1.0e30
EPS = 1e-5


def bcast(ap, axis, n):
    a = ap.unsqueeze(axis)
    shape = list(a.shape)
    shape[axis] = n
    return a.broadcast_to(shape)


def load_split(eng, dst, src, sem):
    w = dst.shape[1] // J
    n = 0
    for lo, hi in ((0, 112), (112, P - 1)):
        eng.dma_start(dst[lo:hi, :], src[lo * J * w:hi * J * w].rearrange("(p j) -> p j", p=hi - lo)).then_inc(sem, 16)
        n += 16
    eng.dma_start(dst[P - 1:P, 0:LASTROW * w], src[(P - 1) * J * w:E * w].rearrange("(p j) -> p j", p=1)).then_inc(sem, 16)
    return n + 16


def prime(eng, m, sems):
    for sem in sems:
        eng.dma_start(m.spare[0:1, m.primed:m.primed + 1], m.first_word).then_inc(sem, 16)
        m.primed += 1


def stage_load(nc, m, x, src, dst, edge_attr, edge_weight):
    with ExitStack() as ctx:
        ki = [ctx.enter_context(nc.sbuf_tensor(f"key_int{k}", [P, J], I32)) for k in range(2)]
        part = ctx.enter_context(nc.sbuf_tensor("part", [P, J], I32))
        row_i = ctx.enter_context(nc.sbuf_tensor("row_i", [P, P], I32))
        col_i = ctx.enter_context(nc.sbuf_tensor("col_i", [P, 1], I32))
        row16 = ctx.enter_context(nc.sbuf_tensor("row16", [P, 2, J], I16))
        row_b = ctx.enter_context(nc.sbuf_tensor("row_b", [P, 2, J], BF16))
        last_i = ctx.enter_context(nc.sbuf_tensor("last_i", [P, 1], I32))
        last_f = ctx.enter_context(nc.sbuf_tensor("last_f", [P, 1], F32))
        down = ctx.enter_context(nc.sbuf_tensor("down", [P, J], F32))
        downs = ctx.enter_context(nc.sbuf_tensor("downs", [P, 1], F32))
        off = ctx.enter_context(nc.sbuf_tensor("off", [P, P], F32))
        off2 = ctx.enter_context(nc.sbuf_tensor("off2", [P, P], F32))
        zeros = m.zeros
        pst = [ctx.enter_context(nc.psum_tensor(f"ps_rows{i}", [P, P], F32)) for i in range(4)]
        ps_all = ctx.enter_context(nc.psum_tensor("ps_all", [P, 512], F32))
        s_downs = ctx.enter_context(nc.semaphore("s_downs"))
        s_all = ctx.enter_context(nc.semaphore("s_all"))
        s_clear = ctx.enter_context(nc.semaphore("s_clear"))
        s_iota = ctx.enter_context(nc.semaphore("s_iota"))
        s_in = ctx.enter_context(nc.semaphore("s_in"))
        s_keys = ctx.enter_context(nc.semaphore("s_keys"))
        s_turned = ctx.enter_context(nc.semaphore("s_turned"))
        s_row = ctx.enter_context(nc.semaphore("s_row"))
        s_out = ctx.enter_context(nc.semaphore("s_out"))
        block = ctx.enter_context(nc.Block())
        blocks = J // P
        arrays = 4
        INPUTS = 15

        @block.sync
        def _(sp):
            sp.wait_ge(s_clear, 1)
            n = 0
            for k, a in enumerate((src, dst)):
                n += load_split(sp, ki[k], a, s_in)
            sp.dma_start(m.x[:, 0:(B - 1) * F].rearrange("p (b f) -> p b f", f=F),
                         x[0:(B - 1) * P, :].rearrange("(b p) f -> p b f", p=P)).then_inc(s_in, 16)
            sp.dma_start(m.x[0:LASTBLOCK, (B - 1) * F:B * F], x[(B - 1) * P:N, :]).then_inc(s_in, 16)
            n += 32
            n += load_split(sp, m.attr, edge_attr.rearrange("e a -> (e a)"), s_in)
            n += load_split(sp, m.w, edge_weight, s_in)
            sp.dma_start(last_i[1:P, :], dst[0:(P - 1) * J].rearrange("(p j) -> p j", j=J)[:, J - 1:J],
                         allow_slow_non_contiguous=True).then_inc(s_in, 16)
            n += 16
            assert n == INPUTS * 16
            sp.dma_start(m.asrc_at.rearrange("(p j) h -> p (j h)", p=P), zeros[:, :]).then_inc(s_out, 16)
            sp.dma_start(m.rec[0:1, :], m.minus[0:1, 0:REC]).then_inc(s_out, 16)
            sp.dma_start(m.xd[0:1, :], m.minus[0:1, 0:XDW]).then_inc(s_out, 16)
            sp.dma_start(m.s0[EP:EP + 1, :], zeros[0:1, 0:S0W]).then_inc(s_out, 16)
            sp.dma_start(m.s1[EP:EP + 1, :], zeros[0:1, 0:F]).then_inc(s_out, 16)
            sp.dma_start(m.s3[EP:EP + 1, :], zeros[0:1, 0:F]).then_inc(s_out, 16)
            sp.wait_ge(s_row, 4 * blocks)
            for k in range(2):
                for a, t in ((m.keyrow[k], row16), (m.lorow[k], row_b)):
                    sp.dma_start(a.rearrange("(b t p) -> t b p", t=P, p=P),
                                 t[:, k, :].rearrange("t (b p) -> t b p", p=P)).then_inc(s_out, 16)
            sp.wait_ge(s_out, 16 * (1 + 5 + 4))

        @block.gpsimd
        def _(pool):
            pool.iota(row_i[:, :], pattern=[[1, P]], base=0, channel_multiplier=0).then_inc(s_iota, 1)
            pool.iota(col_i[:, :], pattern=[[0, 1]], base=0, channel_multiplier=1).then_inc(s_iota, 1)
            pool.iota(m.natural[:, :], pattern=[[1, J]], base=1, channel_multiplier=J).then_inc(s_iota, 1)

        @block.vector
        def _(dve):
            for k in range(2):
                dve.memset(ki[k][:, :], PAD)
            dve.memset(m.x[:, :], 0.0)
            dve.memset(m.attr[:, :], 0.0)
            dve.memset(m.w[:, :], 0.0)
            dve.memset(zeros[:, :], 0.0)
            dve.memset(m.zero[:, :], 0.0)
            dve.memset(m.ones[:, :], 1.0)
            dve.memset(m.eps[:, :], EPS)
            dve.memset(last_i[:, :], 0)
            dve.memset(m.lo[1][:, J:J + 4], 0.0)
            dve.memset(m.hi[1][:, J:J + 4], 0.0)
            dve.memset(m.minus[:, :], -1.0).then_inc(s_clear, 1)
            dve.wait_ge(s_iota, 3)
            dve.tensor_copy(m.lane[:, :], row_i[:, :])
            dve.tensor_copy(m.part[:, :], col_i[:, :])
            dve.drain()
            dve.tensor_copy(m.lane_b[:, :], m.lane[:, :])
            dve.tensor_scalar(m.ident[:, :], m.lane[:, :], m.part[:, 0:1], None, ALU.is_equal)
            dve.tensor_scalar(m.above[:, :], m.lane[:, :], m.part[:, 0:1], None, ALU.is_gt)
            dve.tensor_scalar(m.below[:, :], m.lane[:, :], m.part[:, 0:1], None, ALU.is_lt)
            dve.wait_ge(s_in, INPUTS * 16)
            for k in range(2):
                dve.tensor_copy(m.key[k][:, :], ki[k][:, :])
                dve.tensor_scalar(part[:, :], ki[k][:, :], 7, None, ALU.logical_shift_right)
                dve.drain()
                dve.tensor_copy(m.hi[k][:, 0:J], part[:, :])
                dve.drain()
                dve.tensor_scalar(part[:, :], ki[k][:, :], P - 1, None, ALU.bitwise_and)
                dve.drain()
                dve.tensor_copy(m.lo[k][:, 0:J], part[:, :])
                dve.drain()
            dve.drain().then_inc(s_keys, 1)
            for k in range(2):
                dve.tensor_copy(m.lo_b[k][:, :], m.lo[k][:, 0:J])
                dve.tensor_copy(m.hi_b[k][:, :], m.hi[k][:, 0:J])
                dve.tensor_scalar(m.half_minus_lo[k][:, :], m.lo[k][:, 0:J], -1.0, 0.5, ALU.mult, ALU.add)
            dve.tensor_copy(last_f[:, :], last_i[:, :])
            dve.tensor_tensor(down[:, 1:J], m.key[1][:, 1:J], m.key[1][:, 0:J - 1], ALU.is_lt)
            dve.drain()
            dve.tensor_tensor(down[:, 0:1], m.key[1][:, 0:1], last_f[:, :], ALU.is_lt)
            dve.drain()
            dve.tensor_reduce(downs[:, :], down[:, :], AX, ALU.add)
            dve.tensor_scalar(off[:, :], m.lane[:, :], m.part[:, 0:1], None, ALU.subtract)
            dve.drain()
            dve.tensor_scalar(m.undo[:, :], off[:, :], 0.0, 0.5, ALU.is_equal, ALU.mult)
            dve.tensor_scalar(off2[:, :], off[:, :], 1.0, -0.5, ALU.is_equal, ALU.mult)
            dve.drain()
            dve.tensor_tensor(m.undo[:, :], m.undo[:, :], off2[:, :], ALU.add)
            dve.drain()
            dve.tensor_scalar(off2[:, :], off[:, :], float(1 - P), 0.5, ALU.is_equal, ALU.mult)
            dve.drain()
            dve.tensor_tensor(m.undo[:, :], m.undo[:, :], off2[:, :], ALU.add)
            dve.drain().then_inc(s_downs, 1)
            dve.wait_ge(s_all, 1)
            dve.tensor_copy(m.unsorted[:, :], ps_all[:, 0:1])
            dve.drain()

        @block.tensor
        def _(pe):
            pe.wait_ge(s_keys, 1)
            for i in range(arrays * blocks):
                a, b = divmod(i, blocks)
                s = (m.key[0], m.lo[0], m.key[1], m.lo[1])[a]
                if i >= 4:
                    pe.wait_ge(s_row, i - 3)
                pe.transpose(pst[i % 4][:, :], s[:, b * P:(b + 1) * P], m.ident[:, :]).then_inc(s_turned, 1)
            pe.wait_ge(s_downs, 1)
            pe.matmul(ps_all[:, 0:1], m.ones[:, :], downs[:, :], start=True, stop=True).then_inc(s_all, 1)

        @block.scalar
        def _(act):
            for i in range(arrays * blocks):
                a, b = divmod(i, blocks)
                t = (row16, row_b)[a % 2]
                act.wait_ge(s_turned, i + 1)
                act.activation(t[:, a // 2, b * P:(b + 1) * P], pst[i % 4][:, :], ACT.Copy).then_inc(s_row, 1)


def if_unsorted(eng, m, work):
    downs = eng.value_load(m.unsorted[0:1, 0:1], min_val=0, max_val=E)
    with eng.If(downs > 0):
        work()


def stage_count(nc, m):
    T = 16
    SIGNS = 9
    ONES = T - SIGNS
    TURNS = J // (2 * T)
    with ExitStack() as ctx:
        def sb(name, shape, dt=BF16):
            return ctx.enter_context(nc.sbuf_tensor(name, shape, dt))
        def sem(n):
            return ctx.enter_context(nc.semaphore(n))
        oa = [sb(f"onelane{h}", [P, ONES, P]) for h in range(2)]
        sg = [sb(f"signlane{h}", [P, SIGNS, P]) for h in range(2)]
        ob = [sb(f"oneblock{h}", [P, T, B]) for h in range(2)]
        zero = sb("zero_b", [P, P])
        cum = sb("cum", [P, 2, B], F32)
        part = sb("part_counts", [P, B], F32)
        ps_ones = [ctx.enter_context(nc.psum_tensor(f"ps_ones{i}", [P, 512], F32)) for i in range(2)]
        ps_signs = [ctx.enter_context(nc.psum_tensor(f"ps_signs{i}", [P, 512], F32)) for i in range(2)]
        ps_d = ctx.enter_context(nc.psum_tensor("ps_diff", [P, 512], F32))
        s_banks, s_made, s_signs, s_free, s_sum, s_cum, s_diff = (
            sem(n) for n in ("s_banks", "s_made", "s_signs", "s_free", "s_sum", "s_cum", "s_diff"))
        s_fill = sem("s_fill")
        block = ctx.enter_context(nc.Block())

        @block.sync
        def _(sp):
            hv = m.h3.rearrange("(p j) f -> p (j f)", p=P)
            for i in range(F // H):
                sp.dma_start(hv[:, i * H * J:(i + 1) * H * J], m.zeros[:, :]).then_inc(s_fill, 16)
            sp.wait_ge(s_fill, 16 * (F // H))

        @block.vector
        def _(dve):
            def count(k):
                with dve.Fori(0, TURNS) as it:
                    for h in range(2):
                        n = it * 2 + h
                        dve.wait_ge(s_free, it * 2 + (h + 1 + k * 2 * TURNS))
                        dve.sem_inc(m.step_dve, 1)
                        dve.tensor_tensor(oa[h][:, :, :], bcast(m.lane_b[:, :], 1, ONES), bcast(m.lo_b[k][:, bass.ds(n * T, ONES)], 2, P), ALU.is_equal)
                        dve.tensor_tensor(ob[h][:, :, :], bcast(m.lane_b[:, 0:B], 1, T), bcast(m.hi_b[k][:, bass.ds(n * T, T)], 2, B), ALU.is_equal).then_inc(s_made, 1)
                dve.wait_ge(s_sum, k + 1)
                for i in range(2):
                    dve.tensor_copy(cum[:, i, :], ps_signs[i][:, 0:B])
                dve.drain().then_inc(s_cum, 1)
                dve.tensor_copy(part[:, :], ps_ones[0][:, 0:B])
                dve.drain()
                dve.tensor_tensor(m.cnt[k][:, :], part[:, :], ps_ones[1][:, 0:B], ALU.add)
                dve.wait_ge(s_diff, k + 1)
                if k == 0:
                    dve.tensor_tensor(m.cnt_first[:, :], part[:, :], ps_d[:, 0:B], ALU.add)
                for i in range(2):
                    dve.drain()
                    dve.tensor_tensor(m.cnt[k][:, :], m.cnt[k][:, :], ps_d[:, i * B:(i + 1) * B], ALU.add)
                dve.drain().then_inc(s_banks, 1)
            dve.memset(m.cnt[1][:, :], 0.0)
            dve.memset(zero[:, :], 0.0).then_inc(s_banks, 1)
            count(0)
            if_unsorted(dve, m, lambda: count(1))

        @block.scalar
        def _(act):
            def count(k):
                with act.Fori(0, TURNS) as it:
                    for h in range(2):
                        act.wait_ge(s_free, it * 2 + (h + 1 + k * 2 * TURNS))
                        act.sem_inc(m.step_act, 1)
                        for t in range(SIGNS):
                            last = act.activation(sg[h][:, t, :], m.lane_b[:, :], ACT.Sign,
                                                  bias=m.half_minus_lo[k][:, bass.ds((it * 2 + h) * T + (ONES + t), 1)])
                        last.then_inc(s_signs, 1)
            count(0)
            if_unsorted(act, m, lambda: count(1))

        @block.tensor
        def _(pe):
            def count(k):
                pe.wait_ge(s_banks, k + 1)
                for bank in (*ps_ones, *ps_signs):
                    pe.matmul(bank[:, 0:B], zero[:, :], zero[:, 0:B], start=True, stop=False)
                for half in range(2):
                    with pe.Fori(half * TURNS // 2, (half + 1) * TURNS // 2) as it:
                        for h in range(2):
                            pe.wait_ge(s_made, it * 2 + (h + 1 + k * 2 * TURNS))
                            pe.wait_ge(s_signs, it * 2 + (h + 1 + k * 2 * TURNS))
                            pe.sem_inc(m.step_pe, 1)
                            for t in range(ONES):
                                pe.matmul(ps_ones[half][:, 0:B], oa[h][:, t, :], ob[h][:, t, :], start=False, stop=False)
                            for t in range(SIGNS):
                                last = pe.matmul(ps_signs[half][:, 0:B], sg[h][:, t, :], ob[h][:, ONES + t, :], start=False, stop=False)
                            last.then_inc(s_free, 1)
                for bank in (*ps_ones, *ps_signs):
                    last = pe.matmul(bank[:, 0:B], zero[:, :], zero[:, 0:B], start=False, stop=True)
                last.then_inc(s_sum, 1)
                pe.wait_ge(s_cum, k + 1)
                pe.matmul(ps_d[:, 0:2 * B], m.undo[:, :], cum[:, :, :], start=True, stop=True).then_inc(s_diff, 1)
            pe.sem_inc(s_free, 2)
            count(0)
            if_unsorted(pe, m, lambda: count(1))


class Places:

    def __init__(self, nc, ctx, tag):
        def sb(name, shape, dt=F32):
            return ctx.enter_context(nc.sbuf_tensor(name + tag, shape, dt))
        self.tot, self.incl, self.end, self.ne, self.r, self.t1, self.t2 = (
            sb(n, [P, B]) for n in ("tot", "incl", "end", "nonempty", "ratio", "work1", "work2"))
        self.ri = sb("ratio_i", [P, B], I32)
        self.zb = sb("zb", [P, B])
        self.vb = sb("carry_of_b", [B, 2, P], BF16)
        self.ps_a, self.ps_b, self.ps_v = (ctx.enter_context(nc.psum_tensor(n + tag, [P, 512], F32)) for n in ("ps_a", "ps_b", "ps_v"))
        self.s_products, self.s_operands, self.s_vc = (
            ctx.enter_context(nc.semaphore(n)) for n in ("s_products", "s_operands", "s_vc"))


def places_pe(pe, m, w, k, turn):
    if turn:
        pe.wait_ge(w.s_operands, 2 * turn)
    pe.matmul(w.ps_a[:, 0:B], m.above[:, :], m.cnt[k][:, :], start=True, stop=True)
    pe.matmul(w.ps_b[:, 0:B], m.ones[:, :], m.cnt[k][:, :], start=True, stop=True).then_inc(w.s_products, 1)
    pe.wait_ge(w.s_operands, 2 * turn + 2)
    pe.transpose(w.ps_v[0:B, k * P:(k + 1) * P], w.t2[:, :], m.ident[:, :]).then_inc(w.s_products, 1)


def places_dve(dve, m, w, k, turn):
    tot, incl, end, ne, r, t1, t2, ri = w.tot, w.incl, w.end, w.ne, w.r, w.t1, w.t2, w.ri
    dve.wait_ge(w.s_products, 2 * turn + 1)
    dve.tensor_copy(tot[:, :], w.ps_b[:, 0:B])
    dve.drain()
    dve.tensor_tensor_scan(incl[:, :], w.zb[:, :], tot[:, :], 0.0, ALU.add, ALU.add)
    dve.drain()
    dve.tensor_tensor(incl[:, :], incl[:, :], tot[:, :], ALU.subtract)
    dve.drain()
    dve.tensor_tensor(m.start[k][:, :], incl[:, :], w.ps_a[:, 0:B], ALU.add)
    dve.drain().then_inc(w.s_operands, 1)
    dve.tensor_scalar(m.next[k][:, :], m.start[k][:, :], 1.0, None, ALU.add)
    dve.tensor_tensor(end[:, :], m.start[k][:, :], m.cnt[k][:, :], ALU.add)
    dve.tensor_scalar(ne[:, :], m.cnt[k][:, :], 1.0, None, ALU.min)
    dve.drain()
    dve.tensor_scalar(end[:, :], end[:, :], 1.0, None, ALU.subtract)
    dve.drain()
    dve.scalar_tensor_tensor(t1[:, :], end[:, :], float(EP), ne[:, :], ALU.subtract, ALU.mult)
    dve.drain()
    dve.tensor_scalar(m.i_end[k][:, :], t1[:, :], float(EP), None, ALU.add)
    dve.tensor_scalar(ri[:, :], end[:, :], 1.0 / J, None, ALU.mult)
    dve.drain()
    dve.tensor_copy(r[:, :], ri[:, :])
    dve.drain()
    dve.scalar_tensor_tensor(t1[:, :], r[:, :], float(J), end[:, :], ALU.mult, ALU.is_gt)
    dve.drain()
    dve.tensor_tensor(r[:, :], r[:, :], t1[:, :], ALU.subtract)
    dve.drain()
    dve.tensor_scalar(t1[:, :], r[:, :], 1.0, float(J), ALU.add, ALU.mult)
    dve.drain()
    dve.tensor_tensor(t1[:, :], t1[:, :], end[:, :], ALU.is_le)
    dve.drain()
    dve.tensor_tensor(r[:, :], r[:, :], t1[:, :], ALU.add)
    dve.drain()
    dve.scalar_tensor_tensor(t1[:, :], r[:, :], float(J), m.start[k][:, :], ALU.mult, ALU.is_gt)
    dve.drain()
    dve.tensor_tensor(m.has[k][:, :], t1[:, :], ne[:, :], ALU.mult)
    dve.drain()
    dve.scalar_tensor_tensor(t1[:, :], r[:, :], 1.0, m.has[k][:, :], ALU.add, ALU.mult)
    dve.drain()
    dve.tensor_scalar(t2[:, :], t1[:, :], 1.0, None, ALU.subtract)
    dve.drain().then_inc(w.s_operands, 1)
    if k == 0:
        dve.tensor_tensor(m.next_half[:, :], m.next[0][:, :], m.cnt_first[:, :], ALU.add)
        dve.tensor_scalar(t1[:, :], ne[:, :], -1.0e6, 1.0e6, ALU.mult, ALU.add)
        dve.drain()
        dve.tensor_tensor(m.i_start[:, :], t1[:, :], m.start[k][:, :], ALU.add)
        dve.drain()
    dve.wait_ge(w.s_products, 2 * turn + 2)
    dve.tensor_copy(w.vb[:, k, :], w.ps_v[0:B, k * P:(k + 1) * P])
    dve.drain().then_inc(w.s_vc, 1)


def stage_places(nc, m, w0, fc_w, fc_b):
    PER = 512 // (8 * H)
    with ExitStack() as ctx:
        def sb(name, shape, dt=F32):
            return ctx.enter_context(nc.sbuf_tensor(name, shape, dt))
        w = Places(nc, ctx, "0")
        wl = sb("w_heads", [P, H * F])
        fc = sb("fc_rows", [P, 2 * F])
        fcb = sb("fcb_rows", [P, 1])
        prod = sb("w_times_fc", [P, 2 * H * F])
        v8 = sb("v8", [P, 2 * H])
        vblk = sb("vblk", [P, 4 * 2 * H])
        xt = sb("xt", [P, 2, P])
        a8 = sb("a8", [P, GROUPS * 4 * 2 * H])
        t0 = sb("t0_rows", [P, B * T0W])
        ps_t = [ctx.enter_context(nc.psum_tensor(f"ps_t{i}", [P, 512], F32)) for i in range(2)]
        ps_m = [ctx.enter_context(nc.psum_tensor(f"ps_m{i}", [P, 512], F32)) for i in range(2)]
        names = ("s_w", "s_vblk", "s_xt", "s_xc", "s_m", "s_rows", "s_st")
        s_w, s_vblk, s_xt, s_xc, s_m, s_rows, s_st = (
            ctx.enter_context(nc.semaphore(n)) for n in names)
        block = ctx.enter_context(nc.Block())

        @block.sync
        def _(sp):
            for b in range(4):
                sp.dma_start(wl[b * F:(b + 1) * F, :].rearrange("f (h o) -> f h o", h=H),
                             w0.rearrange("h f o -> f h o")).then_inc(s_w, 16)
            sp.dma_start(fc[:, :], fc_w[0, :].partition_broadcast(P)).then_inc(s_w, 16)
            sp.dma_start(fcb[:, :], fc_b[:].partition_broadcast(P)).then_inc(s_w, 16)
            sp.wait_ge(w.s_vc, 2)
            for k in range(2):
                sp.dma_start(m.carry_row[k].rearrange("(b p) -> b p", p=P), w.vb[:, k, :]).then_inc(s_st, 16)
            sp.wait_ge(s_rows, 1)
            sp.dma_start(m.t0.rearrange("(b p) w -> p b w", p=P), t0[:, :].rearrange("p (b w) -> p b w", w=T0W)).then_inc(s_st, 16)
            sp.dma_start(m.asrc_t.rearrange("(b p) w -> p b w", p=P), m.asrc_rows[:, :].rearrange("p (b w) -> p b w", w=H)).then_inc(s_st, 16)
            sp.wait_ge(s_st, 64)

        @block.vector
        def _(dve):
            dve.memset(w.zb[:, :], 0.0)
            dve.memset(m.x[:, B * F:GROUPS * 4 * F], 0.0)
            for k in range(2):
                places_dve(dve, m, w, k, k)
            dve.wait_ge(s_w, 96)
            for i in range(2):
                dve.tensor_tensor(prod[:, i * H * F:(i + 1) * H * F].rearrange("p (h o) -> p h o", h=H),
                                  wl[:, :].rearrange("p (h o) -> p h o", h=H),
                                  bcast(fc[:, i * F:(i + 1) * F], 1, H), ALU.mult)
            dve.memset(vblk[:, :], 0.0)
            dve.drain()
            dve.tensor_reduce(v8[:, :], prod[:, :].rearrange("p (h o) -> p h o", o=F), AX, ALU.add)
            dve.drain()
            for b in range(4):
                dve.tensor_copy(vblk[b * F:(b + 1) * F, b * 2 * H:(b + 1) * 2 * H], v8[b * F:(b + 1) * F, :])
            dve.drain().then_inc(s_vblk, 1)
            for i, g in enumerate(range(0, GROUPS, PER)):
                end = min(g + PER, GROUPS)
                dve.wait_ge(s_m, end)
                dve.tensor_copy(a8[:, g * 8 * H:end * 8 * H], ps_m[i][:, 0:(end - g) * 8 * H])
            dve.drain()
            a8v = a8[:, :].rearrange("p (b w) -> p b w", w=2 * H)
            t0v = t0[:, :].rearrange("p (b w) -> p b w", w=T0W)
            dve.tensor_copy(t0v[:, :, 0:F], m.x[:, 0:B * F].rearrange("p (b f) -> p b f", f=F))
            dve.tensor_copy(t0v[:, :, F:T0W], a8v[:, 0:B, H:2 * H])
            dve.tensor_scalar(m.asrc_rows[:, :].rearrange("p (b h) -> p b h", h=H), a8v[:, 0:B, 0:H], fcb[:, 0:1], None, ALU.add)
            dve.drain().then_inc(s_rows, 1)

        @block.tensor
        def _(pe):
            for k in range(2):
                places_pe(pe, m, w, k, k)
            pe.wait_ge(s_vblk, 1)
            for g in range(GROUPS + 1):
                if g < GROUPS:
                    if g >= 2:
                        pe.wait_ge(s_xc, g - 1)
                    pe.transpose(ps_t[g % 2][:, 0:P], m.x[:, g * P:(g + 1) * P], m.ident[:, :]).then_inc(s_xt, 1)
                if g >= 1:
                    q, c = divmod(g - 1, PER)
                    pe.wait_ge(s_xc, g)
                    pe.matmul(ps_m[q][:, c * 8 * H:(c + 1) * 8 * H], xt[:, (g - 1) % 2, :], vblk[:, :], start=True, stop=True).then_inc(s_m, 1)

        @block.scalar
        def _(act):
            for g in range(GROUPS):
                if g >= 2:
                    act.wait_ge(s_m, g - 1)
                act.wait_ge(s_xt, g + 1)
                act.activation(xt[:, g % 2, :], ps_t[g % 2][:, 0:P], ACT.Copy).then_inc(s_xc, 1)


def stage_rank(nc, m):
    T = 16
    R = 4
    LAG = 2
    BOTH = ((0, 0), (1, 0))
    HALVES = ((0, 0), (0, J // 2))
    CHAINS = range(2)
    with ExitStack() as ctx:
        def sb(name, shape, dt=F32):
            return ctx.enter_context(nc.sbuf_tensor(name, shape, dt))
        krow = [[sb(f"krow{h}{c}", [P, T * P], I16) for c in CHAINS] for h in range(2)]
        lrow = [[sb(f"lrow{h}{c}", [P, T * P], BF16) for c in CHAINS] for h in range(2)]
        oat = [[sb(f"lane_onehot_t{h}{c}", [P, T * P]) for c in CHAINS] for h in range(2)]
        oa = [sb(f"lane_onehot{c}", [P, R, P], BF16) for c in CHAINS]
        ob = [sb(f"block_onehot{c}", [P, R, B], BF16) for c in CHAINS]
        nxt = [sb(f"next_sb{c}", [P, 2, B]) for c in CHAINS]
        junk = sb("junk", [P, R, 4, P], BF16)
        base = [sb(f"base{c}", [P, T]) for c in CHAINS]
        rank = [sb(f"rank{c}", [P, T]) for c in CHAINS]
        place = [sb(f"place{h}", [P, 2 * T], I32) for h in range(2)]
        recs = [sb(f"recs{h}", [P, 2 * T * REC]) for h in range(2)]
        ps_n = [ctx.enter_context(nc.psum_tensor(f"ps_next{c}", [P, 512], F32)) for c in CHAINS]
        ps_f = [[ctx.enter_context(nc.psum_tensor(f"ps_fetch{c}{i}", [P, 512], F32)) for i in range(2)] for c in CHAINS]
        def sem(n):
            return ctx.enter_context(nc.semaphore(n))
        s_row = [sem(f"s_row{h}") for h in range(2)]
        s_rowfree = sem("s_rowfree")
        s_lane = [sem(f"s_lane{c}") for c in CHAINS]
        s_hot, s_upd, s_cur, s_fet, s_sel = ([sem(f"{n}{c}") for c in CHAINS] for n in ("s_hot", "s_upd", "s_cur", "s_fet", "s_sel"))
        s_rec, s_sc = sem("s_rec"), sem("s_sc")
        s_sent = [sem(f"s_sent{h}") for h in range(2)]
        block = ctx.enter_context(nc.Block())

        def either(eng, ranked):
            downs = eng.value_load(m.unsorted[0:1, 0:1], min_val=0, max_val=E)
            with eng.If(downs == 0):
                ranked(HALVES, J // (4 * T), 2 * T)
            with eng.Else():
                ranked(BOTH, J // (2 * T), T)

        @block.sync
        def _(sp):
            def ranked(chains, turns, tiles):
                with sp.Fori(0, turns) as it:
                    for h in range(2):
                        sp.wait_ge(s_rowfree, it * 2 + (h + 1))
                        sp.sem_inc(m.step_sp, 1)
                        for c, (k, col) in enumerate(chains):
                            for t, a in ((krow[h][c], m.keyrow[k]), (lrow[h][c], m.lorow[k])):
                                sp.dma_start(t[:, :], a[bass.ds((it * 2 + h) * (T * P) + col * P, T * P)].partition_broadcast(P)).then_inc(s_row[h], 16)
                sp.wait_ge(s_rowfree, turns * 2 + 1)
                for c, (k, col) in enumerate(chains):
                    for t, a in ((krow[0][c], m.keyrow[k]), (lrow[0][c], m.lorow[k])):
                        sp.dma_start(t[:, :], a[0:T * P].partition_broadcast(P)).then_inc(s_row[0], 16)
                sp.wait_ge(s_row[0], (turns + 1) * 64)
            either(sp, ranked)

        @block.gpsimd
        def _(pool):
            def ranked(chains, turns, tiles):
                with pool.Fori(0, turns) as it:
                    for h in range(2):
                        pool.wait_ge(s_rec, it * 2 + (h + 1))
                        pool.sem_inc(m.step_pool, 1)
                        for t in range(tiles):
                            pool.indirect_dma_start(out=m.rec, out_offset=bass.IndirectOffsetOnAxis(ap=place[h][:, t:t + 1], axis=0),
                                                    in_=recs[h][:, t * REC:(t + 1) * REC], in_offset=None).then_inc(s_sent[h], 16)
            prime(pool, m, s_sent)
            for b in range(B):
                pool.indirect_dma_start(out=m.asrc_at, out_offset=bass.IndirectOffsetOnAxis(ap=m.i_start[:, b:b + 1], axis=0),
                                        in_=m.asrc_rows[:, b * H:(b + 1) * H], in_offset=None,
                                        bounds_check=EP - 1, oob_is_err=False).then_inc(s_sc, 16)
            pool.wait_ge(s_sc, 16 * B)
            either(pool, ranked)
            for h in range(2):
                pool.wait_ge(s_sent[h], 16 + 16 * J // 2)

        @block.vector
        def _(dve):
            def make(chains, n, t):
                s = t % R
                for c, (k, col) in enumerate(chains):
                    dve.wait_ge(s_upd[c], n + (t + 1))
                    dve.tensor_scalar(oa[c][:, s, :], m.lane_b[:, :], m.lo[k][:, bass.ds(n + (t + col), 1)], None, ALU.is_equal)
                    dve.tensor_scalar(ob[c][:, s, :], m.lane_b[:, 0:B], m.hi[k][:, bass.ds(n + (t + col), 1)], None, ALU.is_equal).then_inc(s_hot[c], 1)

            def select(chains, n, h, t):
                for c, (k, col) in enumerate(chains):
                    dve.scalar_tensor_tensor(junk[:, t % R, 2 * c, :], krow[h][c][:, t * P:(t + 1) * P], m.key[k][:, bass.ds(n + (t + col), 1)], m.below[:, :],
                                             ALU.is_equal, ALU.mult, accum_out=rank[c][:, t:t + 1])
                    dve.wait_ge(s_fet[c], n + (t + 1 + 2))
                    dve.scalar_tensor_tensor(junk[:, t % R, 2 * c + 1, 0:B], m.lane[:, 0:B], m.hi[k][:, bass.ds(n + (t + col), 1)], ps_f[c][t % 2][:, 0:B],
                                             ALU.is_equal, ALU.mult, accum_out=base[c][:, t:t + 1]).then_inc(s_sel[c], 1)

            def lanes(h, count):
                dve.wait_ge(s_row[h], count)
                dve.sem_inc(m.step_dve, 1)
                for c in CHAINS:
                    dve.tensor_scalar(oat[h][c][:, :], lrow[h][c][:, :], m.part[:, 0:1], None, ALU.is_equal).then_inc(s_lane[c], 1)

            def ranked(chains, turns, tiles):
                lanes(0, 64)
                for t in range(LAG):
                    make(chains, 0, t)
                with dve.Fori(0, turns) as it:
                    for h in range(2):
                        n = (it * 2 + h) * T
                        for t in range(T):
                            make(chains, n, t + LAG)
                            if t == T - 4:
                                lanes(1 - h, (it + (h + 1)) * 64)
                            select(chains, n, h, t)
                        dve.drain().then_inc(s_rowfree, 1)
                        dve.wait_ge(s_sent[h], it * (16 * tiles) + 16)
                        dve.sem_inc(m.step_dve, 1)
                        rv = recs[h][:, :].rearrange("p (t w) -> p t w", w=REC)
                        ri = recs[h][:, :].bitcast(I32).rearrange("p (t w) -> p t w", w=REC)
                        for c, (k, col) in enumerate(chains if chains is HALVES else chains[:1]):
                            lot = slice(c * T, (c + 1) * T)
                            dve.tensor_tensor(place[h][:, lot], base[c][:, :], rank[c][:, :], ALU.add)
                            if chains is HALVES:
                                dve.tensor_copy(ri[:, lot, 4], m.natural[:, bass.ds(n + col, T)])
                            else:
                                dve.tensor_tensor(ri[:, lot, 4], base[1][:, :], rank[1][:, :], ALU.add)
                            dve.tensor_copy(rv[:, lot, 0], m.key[0][:, bass.ds(n + col, T)])
                            dve.tensor_copy(rv[:, lot, 1], m.key[1][:, bass.ds(n + col, T)])
                            dve.tensor_copy(rv[:, lot, 2:4], m.attr[:, bass.ds(n * 2 + 2 * col, 2 * T)].rearrange("p (t a) -> p t a", a=2))
                        dve.drain().then_inc(s_rec, 1)

            dve.sem_inc(s_rowfree, 2)
            for c in CHAINS:
                dve.sem_inc(s_sel[c], 2)
            either(dve, ranked)

        @block.tensor
        def _(pe):
            def ranked(chains, turns, tiles):
                for c, (k, col) in enumerate(chains):
                    table = m.next[k] if col == 0 else m.next_half
                    pe.matmul(ps_n[c][:, 0:B], m.ident[:, :], table[:, :], start=True, stop=True).then_inc(s_upd[c], R)
                    pe.sem_inc(s_fet[c], 2)
                with pe.Fori(0, turns) as it:
                    for h, t in ((h, t) for h in range(2) for t in range(T)):
                        n = it * (2 * T) + (h * T + t + 1)
                        for c in CHAINS:
                            if t == 0:
                                pe.wait_ge(s_lane[c], it * 2 + (h + 1))
                            pe.wait_ge(s_hot[c], n)
                            pe.wait_ge(s_cur[c], n)
                            pe.wait_ge(s_sel[c], n)
                            pe.sem_inc(m.step_pe, 1)
                            pe.matmul(ps_f[c][t % 2][:, 0:B], oat[h][c][:, t * P:(t + 1) * P], nxt[c][:, t % 2, :], start=True, stop=True).then_inc(s_fet[c], 1)
                            pe.matmul(ps_n[c][:, 0:B], m.ident[:, :], nxt[c][:, t % 2, :], start=True, stop=False)
                            pe.matmul(ps_n[c][:, 0:B], oa[c][:, t % R, :], ob[c][:, t % R, :], start=False, stop=True).then_inc(s_upd[c], 1)
            either(pe, ranked)

        @block.scalar
        def _(act):
            def ranked(chains, turns, tiles):
                with act.Fori(0, turns * T) as it:
                    for t in range(2):
                        for c in CHAINS:
                            act.wait_ge(s_upd[c], it * 2 + (R + t))
                            act.wait_ge(s_fet[c], it * 2 + (t + 1))
                            act.sem_inc(m.step_act, 1)
                            act.activation(nxt[c][:, t, :], ps_n[c][:, 0:B], ACT.Copy).then_inc(s_cur[c], 1)
            either(act, ranked)


def stage_attend(nc, m):
    TURNS = CHUNKS // 2
    with ExitStack() as ctx:
        def sb(name, shape, dt=F32):
            return ctx.enter_context(nc.sbuf_tensor(name, shape, dt))
        def sem(n):
            return ctx.enter_context(nc.semaphore(n))
        prev = sb("prev_key", [P, 1])
        pen = sb("pen", [P, C])
        first = sb("first_i", [P, 1], I32)
        first_a = sb("first_asrc", [P, H])
        asrc = sb("asrc_edges", [P, J * H])
        idx = sb("idx_dst", [P, J + 2 * C])
        ask = [sb(f"ask{h}", [P, C], I32) for h in range(2)]
        got = [sb(f"got{h}", [P, C * T0W]) for h in range(2)]
        sc = [sb(f"scanned{h}", [P, C * S0W]) for h in range(2)]
        e = sb("logits", [P, C * H])
        arg = sb("exp_args", [P, C * 2 * H])
        ex = sb("exps", [P, C * 2 * H])
        prod = sb("p_times_x", [P, C * H * F])
        s_load, s_first, s_begin = sem("s_load"), sem("s_first"), sem("s_begin")
        s_ask = sem("s_ask")
        s_got = [sem(f"s_got{h}") for h in range(2)]
        s_arg, s_exp, s_done = sem("s_arg"), sem("s_exp"), sem("s_done")
        s_put = [sem(f"s_put{h}") for h in range(2)]
        block = ctx.enter_context(nc.Block())
        rec3 = m.recs[:, :].rearrange("p (j w) -> p j w", w=REC)

        @block.sync
        def _(sp):
            prime(sp, m, s_put)
            sp.dma_start(m.recs[:, :], m.rec[1:EP + 1, :].rearrange("(p j) w -> p (j w)", p=P)).then_inc(s_load, 16)
            sp.dma_start(prev[:, :], m.rec[0:EP, :].rearrange("(p j) w -> p j w", p=P)[:, 0, 0:1], allow_slow_non_contiguous=True).then_inc(s_load, 16)
            sp.dma_start(asrc[:, :], m.asrc_at.rearrange("(p j) h -> p (j h)", p=P)).then_inc(s_load, 16)
            out = m.s0[0:EP, :].rearrange("(p j) w -> p (j w)", p=P)
            with sp.Fori(0, TURNS) as it:
                for h in range(2):
                    sp.wait_ge(s_done, it * 2 + (h + 1))
                    sp.sem_inc(m.step_sp, 1)
                    sp.dma_start(out[:, bass.ds((it * 2 + h) * (C * S0W), C * S0W)], sc[h][:, :]).then_inc(s_put[h], 16)
            for h in range(2):
                sp.wait_ge(s_put[h], 16 + 16 * TURNS)

        @block.gpsimd
        def _(pool):
            pool.wait_ge(s_first, 1)
            pool.indirect_dma_start(out=first_a[:, :], out_offset=None, in_=m.asrc_t,
                                    in_offset=bass.IndirectOffsetOnAxis(ap=first[:, 0:1], axis=0)).then_inc(s_begin, 16)
            with pool.Fori(0, TURNS) as it:
                for h in range(2):
                    pool.wait_ge(s_ask, it * 2 + (h + 1))
                    pool.sem_inc(m.step_pool, 1)
                    for c in range(C):
                        pool.indirect_dma_start(out=got[h][:, c * T0W:(c + 1) * T0W], out_offset=None, in_=m.t0,
                                                in_offset=bass.IndirectOffsetOnAxis(ap=ask[h][:, c:c + 1], axis=0)).then_inc(s_got[h], 16)

        @block.vector
        def _(dve):
            dve.memset(idx[:, :], 0.0)
            dve.memset(sc[1][:, :], 0.0)
            dve.drain()
            dve.memset(sc[1][:, C * S0W - H:C * S0W], -BIG)
            dve.wait_ge(s_load, 48)
            dve.tensor_copy(first[:, :], rec3[:, 0, 0:1])
            dve.drain().then_inc(s_first, 1)
            dve.tensor_copy(idx[:, 0:J], rec3[:, :, 1])
            dve.tensor_tensor(m.same[:, 1:J], rec3[:, 1:J, 0], rec3[:, 0:J - 1, 0], ALU.is_equal)
            dve.tensor_tensor(m.same[:, 0:1], rec3[:, 0, 0:1], prev[:, :], ALU.is_equal)
            dve.drain()
            for h in range(2):
                dve.tensor_copy(ask[h][:, :], idx[:, h * C:(h + 1) * C])
            dve.drain().then_inc(s_ask, 2)
            dve.tensor_reduce(m.whole[0][:, :], m.same[:, :], AX, ALU.min)
            dve.wait_ge(s_begin, 16)
            for k in range(H):
                dve.tensor_tensor_scan(asrc[:, k::H], m.same[:, :], asrc[:, k::H], first_a[:, k:k + 1], ALU.mult, ALU.add)
            dve.drain()
            with dve.Fori(0, TURNS) as it:
                for h in range(2):
                    n = it * 2 + h
                    g3 = got[h][:, :].rearrange("p (c w) -> p c w", w=T0W)
                    s3 = sc[h][:, :].rearrange("p (c w) -> p c w", w=S0W)
                    before = sc[1 - h][:, (C - 1) * S0W:C * S0W]
                    e3 = e[:, :].rearrange("p (c h) -> p c h", h=H)
                    a3 = arg[:, :].rearrange("p (c w) -> p c w", w=2 * H)
                    x3 = ex[:, :].rearrange("p (c w) -> p c w", w=2 * H)
                    M = S0W - H
                    dve.wait_ge(s_got[h], (it + 1) * (16 * C))
                    dve.wait_ge(s_put[h], (it + 1) * 16)
                    dve.sem_inc(m.step_dve, 1)
                    dve.tensor_scalar(pen[:, :], m.same[:, bass.ds(n * C, C)], BIG, -BIG, ALU.mult, ALU.add)
                    dve.tensor_tensor(e3, g3[:, :, F:T0W], asrc[:, bass.ds(n * (C * H), C * H)].rearrange("p (c h) -> p c h", h=H), ALU.add)
                    dve.drain()
                    dve.scalar_tensor_tensor(e[:, :], e[:, :], 0.2, e[:, :], ALU.mult, ALU.max)
                    dve.drain()
                    for k in range(H):
                        dve.tensor_tensor_scan(s3[:, :, M + k], pen[:, :], e[:, k::H], before[:, M + k:M + k + 1], ALU.add, ALU.max)
                    dve.drain()
                    dve.tensor_tensor(a3[:, 1:C, 0:H], s3[:, 0:C - 1, M:S0W], s3[:, 1:C, M:S0W], ALU.subtract)
                    dve.tensor_tensor(a3[:, 0, 0:H], before[:, M:S0W], s3[:, 0, M:S0W], ALU.subtract)
                    dve.tensor_tensor(a3[:, :, H:2 * H], e3, s3[:, :, M:S0W], ALU.subtract)
                    dve.drain()
                    dve.tensor_scalar(arg[:, :], arg[:, :], 0.0, None, ALU.min)
                    dve.drain().then_inc(s_arg, 1)
                    dve.wait_ge(s_exp, n + 1)
                    dve.sem_inc(m.step_dve, 1)
                    dve.tensor_tensor(x3[:, :, 0:H], x3[:, :, 0:H], bcast(m.same[:, bass.ds(n * C, C)], 2, H), ALU.mult)
                    dve.tensor_tensor(prod[:, :].rearrange("p (c h f) -> p c h f", h=H, f=F),
                                      bcast(g3[:, :, 0:F], 2, H), bcast(x3[:, :, H:2 * H], 3, F), ALU.mult)
                    dve.drain()
                    for k in range(H):
                        dve.tensor_tensor_scan(s3[:, :, H * F + k], ex[:, k::2 * H], ex[:, H + k::2 * H], before[:, H * F + k:H * F + k + 1], ALU.mult, ALU.add)
                        for f in range(k * F, (k + 1) * F):
                            dve.tensor_tensor_scan(s3[:, :, f], ex[:, k::2 * H], prod[:, f::H * F], before[:, f:f + 1], ALU.mult, ALU.add)
                    dve.tensor_copy(ask[h][:, :], idx[:, bass.ds((n + 2) * C, C)])
                    dve.drain().then_inc(s_done, 1)
                    dve.sem_inc(s_ask, 1)
            dve.tensor_copy(m.fin[:, :], sc[1][:, (C - 1) * S0W:C * S0W])

        @block.scalar
        def _(act):
            with act.Fori(0, CHUNKS) as it:
                act.wait_ge(s_arg, it + 1)
                act.activation(ex[:, :], arg[:, :], ACT.Exp).then_inc(s_exp, 1)


def layer_norm(nc, m, dve, s_var, s_std, count, blocks):
    a, b = blocks
    x, sq = m.x[:, a * F:b * F], m.sq[:, a * F:b * F]
    mean, var, std = m.mean[:, a:b], m.var[:, a:b], m.std[:, a:b]
    x3 = x.rearrange("p (b f) -> p b f", f=F)
    dve.tensor_reduce(mean, x3, AX, ALU.add)
    dve.drain()
    dve.tensor_scalar(mean, mean, 1.0 / F, None, ALU.mult)
    dve.drain()
    dve.tensor_tensor(x3, x3, bcast(mean, 2, F), ALU.subtract)
    dve.drain()
    dve.tensor_tensor(sq, x, x, ALU.mult)
    dve.drain()
    dve.tensor_reduce(var, sq.rearrange("p (b f) -> p b f", f=F), AX, ALU.add)
    dve.drain().then_inc(s_var, 1)
    dve.wait_ge(s_std, count)
    dve.reciprocal(std, std)
    dve.drain()
    dve.tensor_tensor(x3, x3, bcast(std, 2, F), ALU.mult)
    dve.drain()


def root(nc, m, act, s_var, s_std, count, blocks):
    a, b = blocks
    act.wait_ge(s_var, count)
    act.activation(m.std[:, a:b], m.var[:, a:b], ACT.Sqrt, bias=m.eps[:, 0:1], scale=1.0 / F).then_inc(s_std, 1)


def stage_attend_nodes(nc, m, w0, bias0):
    HALF = B // 2
    PER = 7
    HF = H * F
    with ExitStack() as ctx:
        def sb(name, shape, dt=F32):
            return ctx.enter_context(nc.sbuf_tensor(name, shape, dt))
        def sem(n):
            return ctx.enter_context(nc.semaphore(n))
        rep = sb("rep", [P, 3, HF])
        tr = sb("tr", [P, 4, P])
        mc = sb("mc", [P, P])
        dg = sb("dg", [P, 2, P])
        edg = sb("edg", [P, 2, P])
        gs = sb("gs", [P, 2, P])
        shifted = sb("shifted", [P, 3, P])
        table = sb("carry_table", [P, S0W])
        row = sb("carry_row_sb", [P, NN], BF16)
        sel = sb("sel", [P, 4, P])
        ge = sb("ends", [P, HALF * S0W])
        ce = sb("carries", [P, HALF * S0W])
        mm = sb("mm", [P, 3, HALF * H])
        arg = sb("arg2", [P, 2, HALF * H])
        ex = sb("ex2", [P, 2, HALF * H])
        at = sb("agg_t", [P, 2, P])
        ws = sb("w_stacked", [HF, F])
        bs = sb("bias_rows", [P, F])
        ps_t = ctx.enter_context(nc.psum_tensor("ps_tr", [P, 4 * P], F32))
        ps_b = ctx.enter_context(nc.psum_tensor("ps_back", [P, 3 * P], F32))
        ps_c = [ctx.enter_context(nc.psum_tensor(f"ps_c{i}", [P, 512], F32)) for i in range(2)]
        ps_a = [ctx.enter_context(nc.psum_tensor(f"ps_at{i}", [P, 512], F32)) for i in range(2)]
        ps_o = [ctx.enter_context(nc.psum_tensor(f"ps_o{i}", [P, 512], F32)) for i in range(2)]
        (s_w, s_end, s_carry, s_turned, s_dg, s_edg, s_sel, s_cps, s_cc, s_arg, s_ex, s_agg, s_at, s_atc,
         s_o, s_oc, s_var, s_std) = (sem(n) for n in (
             "s_w", "s_end", "s_carry", "s_turned", "s_dg", "s_edg", "s_sel", "s_cps", "s_cc", "s_arg", "s_ex",
             "s_agg", "s_at", "s_atc", "s_o", "s_oc", "s_var", "s_std"))
        block = ctx.enter_context(nc.Block())

        @block.sync
        def _(sp):
            sp.dma_start(ws[:, :], w0.rearrange("h f o -> (h f) o")).then_inc(s_w, 16)
            sp.dma_start(bs[:, :], bias0.partition_broadcast(P)).then_inc(s_w, 16)
            sp.dma_start(row[:, :], m.carry_row[0].partition_broadcast(P)).then_inc(s_w, 16)
            sp.wait_ge(s_w, 48)

        @block.gpsimd
        def _(pool):
            for b in range(B):
                if b == HALF:
                    pool.wait_ge(s_agg, 1)
                o = b % HALF
                pool.indirect_dma_start(out=ge[:, o * S0W:(o + 1) * S0W], out_offset=None, in_=m.s0,
                                        in_offset=bass.IndirectOffsetOnAxis(ap=m.i_end[0][:, b:b + 1], axis=0)).then_inc(s_end, 16)

        @block.vector
        def _(dve):
            for i in range(2):
                dve.tensor_copy(rep[:, i, :].rearrange("p (h f) -> p h f", f=F), bcast(m.fin[:, HF + i * H:HF + (i + 1) * H], 2, F))
            dve.tensor_copy(rep[:, 2, :], m.whole[0][:, 0:1].broadcast_to([P, HF]))
            dve.drain().then_inc(s_carry, 1)
            dve.wait_ge(s_turned, 1)
            dve.tensor_copy(tr[:, :, :], ps_t[:, :].rearrange("p (a q) -> p a q", q=P))
            dve.drain()
            dve.tensor_scalar(dg[:, 0, :], tr[:, 3, :], BIG, -BIG, ALU.mult, ALU.add)
            dve.drain()
            dve.tensor_tensor_scan(mc[:, :], dg[:, 0, :], tr[:, 2, :], -BIG, ALU.add, ALU.max)
            dve.drain()
            dve.memset(dg[:, 0, 0:1], 0.0)
            dve.tensor_tensor(dg[:, 0, 1:P], mc[:, 0:P - 1], mc[:, 1:P], ALU.subtract)
            dve.tensor_tensor(dg[:, 1, :], tr[:, 2, :], mc[:, :], ALU.subtract)
            dve.drain()
            dve.tensor_scalar(dg[:, :, :], dg[:, :, :], 0.0, None, ALU.min)
            dve.drain().then_inc(s_dg, 1)
            dve.wait_ge(s_edg, 1)
            dve.tensor_tensor(edg[:, 0, :], edg[:, 0, :], tr[:, 3, :], ALU.mult)
            for i in range(2):
                dve.tensor_tensor(gs[:, i, :], tr[:, i, :], edg[:, 1, :], ALU.mult)
            dve.drain()
            for i in range(2):
                dve.tensor_tensor_scan(tr[:, i, :], edg[:, 0, :], gs[:, i, :], 0.0, ALU.mult, ALU.add)
            dve.memset(shifted[:, :, 0:1], 0.0)
            dve.drain()
            for i in range(2):
                dve.tensor_copy(shifted[:, i, 1:P], tr[:, i, 0:P - 1])
            dve.tensor_copy(shifted[:, 2, 1:P], mc[:, 0:P - 1])
            dve.drain().then_inc(s_carry, 1)
            dve.wait_ge(s_turned, 2)
            dve.tensor_copy(table[:, 0:HF], ps_b[:, 0:P])
            for i in range(2):
                dve.tensor_copy(table[:, HF + i * H:HF + (i + 1) * H], ps_b[:, (i + 1) * P:(i + 2) * P:F])
            dve.drain().then_inc(s_carry, 1)
            dve.wait_ge(s_w, 48)
            x3 = m.x[:, 0:B * F].rearrange("p (b f) -> p b f", f=F)
            dve.tensor_tensor(x3, x3, bcast(bs[:, :], 1, B), ALU.add)
            for half in range(2):
                for b in range(half * HALF, (half + 1) * HALF):
                    if b >= 4:
                        dve.wait_ge(s_cps, b - 3)
                    dve.tensor_scalar(sel[:, b % 4, :], row[:, b * P:(b + 1) * P], m.part[:, 0:1], None, ALU.is_equal).then_inc(s_sel, 1)
                dve.wait_ge(s_cc, (half + 1) * HALF)
                dve.wait_ge(s_end, 16 * B if half else 16 * HALF)
                g3 = ge[:, :].rearrange("p (b w) -> p b w", w=S0W)
                c3 = ce[:, :].rearrange("p (b w) -> p b w", w=S0W)
                a3 = [arg[:, i, :].rearrange("p (b h) -> p b h", h=H) for i in range(2)]
                x2 = [ex[:, i, :].rearrange("p (b h) -> p b h", h=H) for i in range(2)]
                m3 = [mm[:, i, :].rearrange("p (b h) -> p b h", h=H) for i in range(3)]
                has = m.has[0][:, half * HALF:(half + 1) * HALF]
                M = HF + H
                dve.tensor_scalar(mm[:, 2, 0:HALF], has, BIG, -BIG, ALU.mult, ALU.add)
                dve.drain()
                dve.tensor_tensor(m3[0], c3[:, :, M:S0W], bcast(mm[:, 2, 0:HALF], 2, H), ALU.add)
                dve.drain()
                dve.tensor_tensor(m3[1], m3[0], g3[:, :, M:S0W], ALU.max)
                dve.drain()
                dve.tensor_tensor(a3[0], g3[:, :, M:S0W], m3[1], ALU.subtract)
                dve.tensor_tensor(a3[1], m3[0], m3[1], ALU.subtract)
                dve.drain().then_inc(s_arg, 1)
                dve.wait_ge(s_ex, half + 1)
                for i, t in enumerate((g3, c3)):
                    dve.tensor_tensor(t[:, :, HF:M], t[:, :, HF:M], x2[i], ALU.mult)
                    for k in range(H):
                        v = t[:, :, k * F:(k + 1) * F]
                        dve.tensor_tensor(v, v, bcast(x2[i][:, :, k], 2, F), ALU.mult)
                dve.drain()
                dve.tensor_tensor(g3[:, :, 0:M], g3[:, :, 0:M], c3[:, :, 0:M], ALU.add)
                dve.drain()
                dve.tensor_scalar(m3[2], g3[:, :, HF:M], 1.0e-30, float(H), ALU.max, ALU.mult)
                dve.drain()
                dve.reciprocal(mm[:, 2, :], mm[:, 2, :])
                dve.drain()
                if half == 1:
                    dve.wait_ge(s_at, HALF)
                for k in range(H):
                    dve.tensor_tensor(c3[:, :, k * F:(k + 1) * F], g3[:, :, k * F:(k + 1) * F], bcast(m3[2][:, :, k], 2, F), ALU.mult)
                dve.drain().then_inc(s_agg, 1)
                for b in range(half * HALF, (half + 1) * HALF, PER):
                    dve.wait_ge(s_o, b + PER)
                    v = m.x[:, b * F:(b + PER) * F]
                    dve.tensor_tensor(v, v, ps_o[b // PER % 2][:, 0:PER * F], ALU.add).then_inc(s_oc, 1)
                dve.drain()
                layer_norm(nc, m, dve, s_var, s_std, half + 1, (half * HALF, (half + 1) * HALF))

        @block.tensor
        def _(pe):
            pe.wait_ge(s_carry, 1)
            pe.transpose(ps_t[:, 0:P], m.fin[:, 0:HF], m.ident[:, :])
            pe.transpose(ps_t[:, P:2 * P], rep[:, 0, :], m.ident[:, :])
            pe.transpose(ps_t[:, 2 * P:3 * P], rep[:, 1, :], m.ident[:, :])
            pe.transpose(ps_t[:, 3 * P:4 * P], rep[:, 2, :], m.ident[:, :]).then_inc(s_turned, 1)
            pe.wait_ge(s_carry, 2)
            for i in range(3):
                last = pe.transpose(ps_b[:, i * P:(i + 1) * P], shifted[:, i, :], m.ident[:, :])
            last.then_inc(s_turned, 1)
            pe.wait_ge(s_carry, 3)
            pe.wait_ge(s_w, 48)
            for half in range(2):
                for b in range(half * HALF, (half + 1) * HALF):
                    pe.wait_ge(s_sel, b + 1)
                    if b >= 2:
                        pe.wait_ge(s_cc, b - 1)
                    pe.matmul(ps_c[b % 2][:, 0:S0W], sel[:, b % 4, :], table[:, :], start=True, stop=True).then_inc(s_cps, 1)
                pe.wait_ge(s_agg, half + 1)
                for o in range(HALF + 1):
                    if o < HALF:
                        b = half * HALF + o
                        if b >= 2:
                            pe.wait_ge(s_atc, b - 1)
                        pe.transpose(ps_a[b % 2][:, 0:P], ce[:, o * S0W:o * S0W + HF], m.ident[:, :]).then_inc(s_at, 1)
                    if o >= 1:
                        b = half * HALF + o - 1
                        g, c = divmod(b, PER)
                        pe.wait_ge(s_atc, b + 1)
                        if c == 0 and g >= 2:
                            pe.wait_ge(s_oc, g - 1)
                        pe.matmul(ps_o[g % 2][:, c * F:(c + 1) * F], at[:, b % 2, :], ws[:, :], start=True, stop=True).then_inc(s_o, 1)

        @block.scalar
        def _(act):
            act.wait_ge(s_dg, 1)
            act.activation(edg[:, :, :], dg[:, :, :], ACT.Exp).then_inc(s_edg, 1)
            for half in range(2):
                if half == 1:
                    act.wait_ge(s_at, HALF)
                for b in range(half * HALF, (half + 1) * HALF):
                    o = b % HALF
                    act.wait_ge(s_cps, b + 1)
                    act.activation(ce[:, o * S0W:(o + 1) * S0W], ps_c[b % 2][:, 0:S0W], ACT.Copy).then_inc(s_cc, 1)
                act.wait_ge(s_arg, half + 1)
                act.activation(ex[:, :, :], arg[:, :, :], ACT.Exp).then_inc(s_ex, 1)
                for b in range(half * HALF, (half + 1) * HALF):
                    if b >= 2:
                        act.wait_ge(s_o, b - 1)
                    act.wait_ge(s_at, b + 1)
                    act.activation(at[:, b % 2, :], ps_a[b % 2][:, 0:P], ACT.Copy).then_inc(s_atc, 1)
                root(nc, m, act, s_var, s_std, half + 1, (half * HALF, (half + 1) * HALF))


def stage_spline_table(nc, m, w1):
    with ExitStack() as ctx:
        def sb(name, shape, dt=F32):
            return ctx.enter_context(nc.sbuf_tensor(name, shape, dt))
        def sem(n):
            return ctx.enter_context(nc.semaphore(n))
        wp = sb("w_padded", [P, 4, KK * F])
        xt = sb("xt1", [P, 2, P])
        rows = [sb(f"t1_rows{i}", [P, KK * F]) for i in range(4)]
        ps_t = [ctx.enter_context(nc.psum_tensor(f"ps_t1{i}", [P, 512], F32)) for i in range(2)]
        ps_y = [ctx.enter_context(nc.psum_tensor(f"ps_y{i}", [P, 512], F32)) for i in range(4)]
        s_zero, s_w, s_xt, s_xc, s_y = (sem(n) for n in ("s_zero", "s_w", "s_xt", "s_xc", "s_y"))
        s_copied = [sem("s_copied_act"), sem("s_copied_dve")]
        s_out = [sem(f"s_out{i}") for i in range(4)]
        block = ctx.enter_context(nc.Block())

        @block.sync
        def _(sp):
            sp.wait_ge(s_zero, 1)
            for b in range(4):
                sp.dma_start(wp[b * F:(b + 1) * F, b, :].rearrange("f (k o) -> f k o", o=F),
                             w1.rearrange("u v f o -> f (u v) o")).then_inc(s_w, 16)
            for b in range(B):
                sp.wait_ge(s_copied[b % 2], b // 2 + 1)
                sp.dma_start(m.t1[b * P:(b + 1) * P, :],
                             rows[b % 4][:, :]).then_inc(s_out[b % 4], 16)
            for i in range(4):
                sp.wait_ge(s_out[i], 16 * len(range(i, B, 4)))

        @block.vector
        def _(dve):
            dve.memset(wp[:, :, :], 0.0).then_inc(s_zero, 1)
            for b in range(1, B, 2):
                dve.wait_ge(s_y, b + 1)
                if b >= 4:
                    dve.wait_ge(s_out[b % 4], 16 * (b // 4))
                dve.tensor_copy(rows[b % 4][:, :], ps_y[b % 4][:, :]).then_inc(s_copied[1], 1)

        @block.scalar
        def _(act):
            for b in range(0, B, 2):
                if b % 4 == 0:
                    g = b // 4
                    act.wait_ge(s_xt, g + 1)
                    if g >= 2:
                        act.wait_ge(s_y, 4 * (g - 1))
                    act.activation(xt[:, g % 2, :], ps_t[g % 2][:, 0:P], ACT.Copy).then_inc(s_xc, 1)
                act.wait_ge(s_y, b + 1)
                if b >= 4:
                    act.wait_ge(s_out[b % 4], 16 * (b // 4))
                act.activation(rows[b % 4][:, :], ps_y[b % 4][:, :], ACT.Copy).then_inc(s_copied[0], 1)

        @block.tensor
        def _(pe):
            pe.wait_ge(s_w, 64)
            for g in range(GROUPS):
                for n in ((0, 1) if g == 0 else (g + 1,) if g + 1 < GROUPS else ()):
                    if n >= 2:
                        pe.wait_ge(s_xc, n - 1)
                    pe.transpose(ps_t[n % 2][:, 0:P], m.x[:, n * P:(n + 1) * P], m.ident[:, :]).then_inc(s_xt, 1)
                pe.wait_ge(s_xc, g + 1)
                for b in range(4 * g, min(4 * g + 4, B)):
                    if b >= 4:
                        pe.wait_ge(s_copied[b % 2], b // 2 - 1)
                    pe.matmul(ps_y[b % 4][:, :], xt[:, g % 2, :], wp[:, b % 4, :], start=True, stop=True).then_inc(s_y, 1)


def stage_spline(nc, m):
    TURNS = CHUNKS // 2
    with ExitStack() as ctx:
        def sb(name, shape, dt=F32):
            return ctx.enter_context(nc.sbuf_tensor(name, shape, dt))
        def sem(n):
            return ctx.enter_context(nc.semaphore(n))
        w4 = sb("w4", [P, J * 4])
        idx = sb("idx_cell", [P, J + 2 * C])
        ask = [sb(f"ask1{h}", [P, C], I32) for h in range(2)]
        got = [sb(f"got1{h}", [P, C * T1W]) for h in range(2)]
        sc = [sb(f"scanned1{h}", [P, C * F]) for h in range(2)]
        cell = [sb(f"cell{a}", [P, J]) for a in range(2)]
        tent = m.sq[:, 0:J]
        R = 4
        wa, wb = sb("w_lane", [P, R, P]), sb("w_block", [P, R, B])
        ps_w = ctx.enter_context(nc.psum_tensor("ps_w", [P, 512], F32))
        s_hot, s_used, s_sum = sem("s_hot"), sem("s_used"), sem("s_sum")
        msg = sb("msg", [P, C * F])
        s_ask, s_done = sem("s_ask"), sem("s_done")
        s_got = [sem(f"s_got{h}") for h in range(2)]
        s_put = [sem(f"s_put{h}") for h in range(2)]
        block = ctx.enter_context(nc.Block())
        rec3 = m.recs[:, :].rearrange("p (j w) -> p j w", w=REC)
        step = 2.0 / (K - 1)
        corner_rows = m.t1.rearrange("n (k f) -> (n k) f", f=F)

        @block.sync
        def _(sp):
            prime(sp, m, s_put)
            out = m.s1[0:EP, :].rearrange("(p j) w -> p (j w)", p=P)
            with sp.Fori(0, TURNS) as it:
                for h in range(2):
                    sp.wait_ge(s_done, it * 2 + (h + 1))
                    sp.sem_inc(m.step_sp, 1)
                    sp.dma_start(out[:, bass.ds((it * 2 + h) * (C * F), C * F)], sc[h][:, :]).then_inc(s_put[h], 16)
            for h in range(2):
                sp.wait_ge(s_put[h], 16 + 16 * TURNS)

        @block.gpsimd
        def _(pool):
            with pool.Fori(0, TURNS) as it:
                for h in range(2):
                    pool.wait_ge(s_ask, it * 2 + (h + 1))
                    pool.sem_inc(m.step_pool, 1)
                    for c in range(C):
                        pool.indirect_dma_start(out=got[h][:, c * T1W:(c + 1) * T1W], out_offset=None, in_=corner_rows,
                                                in_offset=bass.IndirectOffsetOnAxis(ap=ask[h][:, c:c + 1], axis=0)).then_inc(s_got[h], 16)

        @block.vector
        def _(dve):
            dve.memset(idx[:, :], 0.0)
            dve.memset(sc[1][:, :], 0.0)
            dve.drain()
            dve.tensor_scalar(idx[:, 0:J], rec3[:, :, 1], float(KK), None, ALU.mult)
            dve.drain()
            for a in range(2):
                u = rec3[:, :, 2 + a]
                dve.tensor_scalar(cell[a][:, :], u, -1.0 + step, None, ALU.is_ge)
                dve.drain()
                dve.scalar_tensor_tensor(cell[a][:, :], u, -1.0 + 2 * step, cell[a][:, :], ALU.is_ge, ALU.add)
                dve.drain()
                dve.scalar_tensor_tensor(idx[:, 0:J], cell[a][:, :], float(K if a == 0 else 1), idx[:, 0:J], ALU.mult, ALU.add)
                dve.drain()
            for h in range(2):
                dve.tensor_copy(ask[h][:, :], idx[:, h * C:(h + 1) * C])
            dve.drain().then_inc(s_ask, 2)
            for a in range(2):
                dve.scalar_tensor_tensor(cell[a][:, :], cell[a][:, :], -step, rec3[:, :, 2 + a], ALU.mult, ALU.add)
                dve.drain()
                for i in range(2):
                    dve.tensor_scalar(tent, cell[a][:, :], 1.0 - step * i, None, ALU.add)
                    dve.drain()
                    dve.scalar_tensor_tensor(tent, tent, -1.0, tent, ALU.mult, ALU.max)
                    dve.drain()
                    dve.tensor_scalar(tent, tent, -1.0 / step, 1.0, ALU.mult, ALU.add)
                    dve.drain()
                    for j in range(2):
                        if a == 0:
                            dve.tensor_scalar(w4[:, 2 * i + j::4], tent, 0.0, None, ALU.max)
                        else:
                            dve.scalar_tensor_tensor(w4[:, 2 * j + i::4], tent, 0.0, w4[:, 2 * j + i::4], ALU.max, ALU.mult)
                    dve.drain()
            with dve.Fori(0, TURNS) as it:
                for h in range(2):
                    n = it * 2 + h
                    dve.wait_ge(s_got[h], (it + 1) * (16 * C))
                    dve.wait_ge(s_put[h], (it + 1) * 16)
                    dve.sem_inc(m.step_dve, 1)
                    for c in range(C):
                        dve.wait_ge(s_used, n * C + (c + 1))
                        dve.tensor_scalar(wa[:, c % R, :], m.lane[:, :], m.lo[1][:, bass.ds(n * C + c, 1)], None, ALU.is_equal)
                        dve.tensor_scalar(wb[:, c % R, :], m.lane[:, 0:B], m.hi[1][:, bass.ds(n * C + c, 1)],
                                          m.w[:, bass.ds(n * C + c, 1)], ALU.is_equal, ALU.mult).then_inc(s_hot, 1)
                    g4 = got[h][:, :].rearrange("p (c k f) -> p c k f", k=K + 2, f=F)
                    by_u = [g4[:, :, u * K:u * K + 2, :] for u in range(2)]
                    wv = w4[:, bass.ds(n * (C * 4), C * 4)].rearrange("p (c k) -> p c k", k=4)
                    for u in range(2):
                        dve.tensor_tensor(by_u[u], by_u[u], bcast(wv[:, :, 2 * u:2 * u + 2], 3, F), ALU.mult)
                    dve.drain()
                    dve.tensor_tensor(by_u[0], by_u[0], by_u[1], ALU.add)
                    dve.drain()
                    dve.tensor_tensor(msg[:, :].rearrange("p (c f) -> p c f", f=F), g4[:, :, 0, :], g4[:, :, 1, :], ALU.add)
                    dve.drain()
                    for f in range(F):
                        dve.tensor_tensor_scan(sc[h][:, f::F], m.same[:, bass.ds(n * C, C)], msg[:, f::F],
                                               sc[1 - h][:, (C - 1) * F + f:(C - 1) * F + f + 1], ALU.mult, ALU.add)
                    dve.tensor_copy(ask[h][:, :], idx[:, bass.ds((n + 2) * C, C)])
                    dve.drain().then_inc(s_done, 1)
                    dve.sem_inc(s_ask, 1)
            dve.tensor_copy(m.fin[:, 0:F], sc[1][:, (C - 1) * F:C * F])
            dve.wait_ge(s_sum, 1)
            dve.tensor_copy(m.sumw[:, :], ps_w[:, 0:B])

        @block.tensor
        def _(pe):
            pe.matmul(ps_w[:, 0:B], m.zero[:, :], m.zero[:, 0:B], start=True, stop=False)
            pe.sem_inc(s_used, R)
            with pe.Fori(0, J // R) as it:
                for c in range(R):
                    pe.wait_ge(s_hot, it * R + (c + 1))
                    pe.sem_inc(m.step_pe, 1)
                    pe.matmul(ps_w[:, 0:B], wa[:, c, :], wb[:, c, :], start=False, stop=False).then_inc(s_used, 1)
            pe.matmul(ps_w[:, 0:B], m.zero[:, :], m.zero[:, 0:B], start=False, stop=True).then_inc(s_sum, 1)


def node_sums(nc, m, ctx, block, k, sums, then_dve, then_pe, then_act, then_sp=None, then_pool=None):
    def sb(name, shape, dt=F32):
        return ctx.enter_context(nc.sbuf_tensor(f"{name}{k}", shape, dt))
    def sem(n):
        return ctx.enter_context(nc.semaphore(n))
    PER = 16
    banks = -(-B // PER)
    rep = sb("rep_s", [P, F])
    tr = sb("tr_s", [F, 2, P])
    shifted = sb("shifted_s", [F, P])
    table = sb("table_s", [P, F])
    row = sb("row_s", [P, NN], BF16)
    sel = sb("sel_s", [P, 4, P])
    ge = sb("ends_s", [P, B * F])
    ce = sb("carries_s", [P, B * F])
    ps_t = ctx.enter_context(nc.psum_tensor(f"ps_ts{k}", [P, 512], F32))
    ps_c = [ctx.enter_context(nc.psum_tensor(f"ps_cs{k}{i}", [P, 512], F32)) for i in range(2)]
    s_end = [sem(f"s_end{i}") for i in range(2)]
    s_row, s_carry, s_turned, s_sel, s_cps, s_cc = (sem(n) for n in (
        "s_row", "s_carry", "s_turned", "s_sel", "s_cps", "s_cc"))

    @block.sync
    def _(sp):
        sp.dma_start(row[:, :], m.carry_row[k].partition_broadcast(P)).then_inc(s_row, 16)
        sp.wait_ge(s_row, 16)
        if then_sp:
            then_sp(sp)

    @block.gpsimd
    def _(pool):
        for i, (first, end) in enumerate(PARTS):
            for b in range(first, end):
                pool.indirect_dma_start(out=ge[:, b * F:(b + 1) * F], out_offset=None, in_=sums,
                                        in_offset=bass.IndirectOffsetOnAxis(ap=m.i_end[k][:, b:b + 1], axis=0)).then_inc(s_end[i], 16)
        if then_pool:
            then_pool(pool)

    @block.vector
    def _(dve):
        dve.tensor_copy(rep[:, :], m.whole[k][:, 0:1].broadcast_to([P, F]))
        dve.drain().then_inc(s_carry, 1)
        dve.wait_ge(s_turned, 1)
        dve.tensor_copy(tr[:, :, :], ps_t[0:F, 0:2 * P].rearrange("p (a q) -> p a q", q=P))
        dve.memset(shifted[:, 0:1], 0.0)
        dve.drain()
        dve.tensor_tensor_scan(shifted[:, 1:P], tr[:, 1, 0:P - 1], tr[:, 0, 0:P - 1], 0.0, ALU.mult, ALU.add)
        dve.drain().then_inc(s_carry, 1)
        dve.wait_ge(s_turned, 2)
        dve.tensor_copy(table[:, :], ps_t[:, 2 * P:2 * P + F])
        dve.drain().then_inc(s_carry, 1)
        dve.wait_ge(s_row, 16)
        for b in range(B):
            if b >= 4:
                dve.wait_ge(s_cps, b - 3)
            dve.tensor_scalar(sel[:, b % 4, :], row[:, b * P:(b + 1) * P], m.part[:, 0:1], None, ALU.is_equal).then_inc(s_sel, 1)
        dve.wait_ge(s_cc, banks)
        for i, (first, end) in enumerate(PARTS):
            dve.wait_ge(s_end[i], 16 * (end - first))
            g = ge[:, first * F:end * F]
            dve.tensor_tensor(g, g, ce[:, first * F:end * F], ALU.add)
            dve.drain()
            then_dve(dve, ge, i)

    @block.tensor
    def _(pe):
        pe.wait_ge(s_carry, 1)
        pe.transpose(ps_t[0:F, 0:P], m.fin[:, 0:F], m.ident[:, :])
        pe.transpose(ps_t[0:F, P:2 * P], rep[:, :], m.ident[:, :]).then_inc(s_turned, 1)
        pe.wait_ge(s_carry, 2)
        pe.transpose(ps_t[:, 2 * P:2 * P + F], shifted[:, :], m.ident[0:F, 0:F]).then_inc(s_turned, 1)
        pe.wait_ge(s_carry, 3)
        for b in range(B):
            q = b // PER
            pe.wait_ge(s_sel, b + 1)
            if b % PER == 0 and q >= 2:
                pe.wait_ge(s_cc, q - 1)
            pe.matmul(ps_c[q % 2][:, (b % PER) * F:(b % PER + 1) * F], sel[:, b % 4, :], table[:, :], start=True, stop=True).then_inc(s_cps, 1)
        then_pe(pe)

    @block.scalar
    def _(act):
        for q in range(banks):
            end = min((q + 1) * PER, B)
            act.wait_ge(s_cps, end)
            act.activation(ce[:, q * PER * F:end * F], ps_c[q % 2][:, 0:(end - q * PER) * F], ACT.Copy).then_inc(s_cc, 1)
        then_act(act)


def stage_spline_nodes(nc, m):
    with ExitStack() as ctx:
        s_var, s_std, s_rows, s_sc, s_x = (ctx.enter_context(nc.semaphore(n)) for n in ("s_var", "s_std", "s_rows", "s_sc", "s_x"))
        block = ctx.enter_context(nc.Block())

        def dve_part(dve, ge, i):
            a, b = PARTS[i]
            x, q, g = (t[:, a * F:b * F] for t in (m.x, m.sq, ge))
            dve.tensor_tensor(x, x, g, ALU.add)
            dve.drain()
            layer_norm(nc, m, dve, s_var, s_std, 2 * i + 1, PARTS[i])
            dve.tensor_tensor(q.rearrange("p (b f) -> p b f", f=F), x.rearrange("p (b f) -> p b f", f=F),
                              bcast(m.sumw[:, a:b], 2, F), ALU.mult)
            dve.drain()
            dve.tensor_tensor(x, x, q, ALU.add)
            dve.drain()
            layer_norm(nc, m, dve, s_var, s_std, 2 * i + 2, PARTS[i])
            dve.drain().then_inc(s_rows, 1)

        def act_part(act):
            for i in range(2):
                root(nc, m, act, s_var, s_std, 2 * i + 1, PARTS[i])
                root(nc, m, act, s_var, s_std, 2 * i + 2, PARTS[i])

        def pool_part(pool):
            for i, (a, b) in enumerate(PARTS):
                pool.wait_ge(s_rows, i + 1)
                for c in range(a, b):
                    pool.indirect_dma_start(out=m.h3, out_offset=bass.IndirectOffsetOnAxis(ap=m.i_start[:, c:c + 1], axis=0),
                                            in_=m.x[:, c * F:(c + 1) * F], in_offset=None,
                                            bounds_check=EP - 1, oob_is_err=False).then_inc(s_sc, 16)
            pool.wait_ge(s_sc, 16 * B)

        def sp_part(sp):
            sp.wait_ge(s_rows, 2)
            sp.dma_start(m.x3t.rearrange("(b p) f -> p b f", p=P), m.x[:, 0:B * F].rearrange("p (b f) -> p b f", f=F)).then_inc(s_x, 16)
            sp.wait_ge(s_x, 16)

        node_sums(nc, m, ctx, block, 0, m.s1, dve_part, lambda pe: None, act_part, sp_part, pool_part)


def stage_exchange(nc, m):
    TURNS = CHUNKS // 2
    with ExitStack() as ctx:
        def sb(name, shape, dt=F32):
            return ctx.enter_context(nc.sbuf_tensor(name, shape, dt))
        def sem(n):
            return ctx.enter_context(nc.semaphore(n))
        first = sb("first3", [P, 1], I32)
        first_x = sb("first_x", [P, F])
        starts = [sb(f"starts{h}", [P, C * F]) for h in range(2)]
        rows = [sb(f"xd_rows{h}", [P, C * XDW]) for h in range(2)]
        to = [sb(f"to{h}", [P, C], I32) for h in range(2)]
        w = Places(nc, ctx, "1")
        lo_b, hi_b = sb("dst_lane_b", [P, J], BF16), sb("dst_block_b", [P, J], BF16)
        zero = sb("zero_b3", [P, P], BF16)
        oa = [sb(f"dst_onelane{h}", [P, C, P], BF16) for h in range(2)]
        ob = [sb(f"dst_oneblock{h}", [P, C, B], BF16) for h in range(2)]
        ps_n = ctx.enter_context(nc.psum_tensor("ps_count_dst", [P, 512], F32))
        s_first, s_begin, s_done, s_free = (sem(n) for n in ("s_first", "s_begin", "s_done", "s_free"))
        s_made, s_used, s_sum, s_st = (sem(n) for n in ("s_made", "s_used", "s_sum", "s_st"))
        s_in = [sem(f"s_in{h}") for h in range(2)]
        s_sent = [sem(f"s_sent{h}") for h in range(2)]
        block = ctx.enter_context(nc.Block())
        rec3 = m.recs[:, :].rearrange("p (j w) -> p j w", w=REC)
        reci = m.recs[:, :].bitcast(I32)

        @block.sync
        def _(sp):
            src = m.h3.rearrange("(p j) f -> p (j f)", p=P)
            with sp.Fori(0, TURNS) as it:
                for h in range(2):
                    sp.wait_ge(s_free, it * 2 + (h + 1))
                    sp.sem_inc(m.step_sp, 1)
                    sp.dma_start(starts[h][:, :], src[:, bass.ds((it * 2 + h) * (C * F), C * F)]).then_inc(s_in[h], 16)
            sp.wait_ge(w.s_vc, 1)
            sp.dma_start(m.carry_row[1].rearrange("(b p) -> b p", p=P), w.vb[:, 1, :]).then_inc(s_st, 16)
            sp.wait_ge(s_st, 16)

        @block.gpsimd
        def _(pool):
            prime(pool, m, s_sent)
            pool.wait_ge(s_first, 1)
            pool.indirect_dma_start(out=first_x[:, :], out_offset=None, in_=m.x3t,
                                    in_offset=bass.IndirectOffsetOnAxis(ap=first[:, 0:1], axis=0)).then_inc(s_begin, 16)
            with pool.Fori(0, TURNS) as it:
                for h in range(2):
                    pool.wait_ge(s_done, it * 2 + (h + 1))
                    pool.sem_inc(m.step_pool, 1)
                    for c in range(C):
                        pool.indirect_dma_start(out=m.xd, out_offset=bass.IndirectOffsetOnAxis(ap=to[h][:, c:c + 1], axis=0),
                                                in_=rows[h][:, c * XDW:(c + 1) * XDW], in_offset=None).then_inc(s_sent[h], 16)
            for h in range(2):
                pool.wait_ge(s_sent[h], 16 + 16 * C * TURNS)

        @block.vector
        def _(dve):
            dve.sem_inc(s_free, 2)
            dve.memset(w.zb[:, :], 0.0)
            dve.memset(zero[:, :], 0.0)
            dve.tensor_copy(first[:, :], rec3[:, 0, 0:1])
            dve.drain().then_inc(s_first, 1)
            dve.tensor_copy(lo_b[:, :], m.lo[1][:, 0:J])
            dve.tensor_copy(hi_b[:, :], m.hi[1][:, 0:J])
            dve.wait_ge(s_begin, 16)
            dve.tensor_copy(rows[1][:, (C - 1) * XDW:(C - 1) * XDW + F], first_x[:, :])
            dve.drain()
            with dve.Fori(0, TURNS) as it:
                for h in range(2):
                    n = it * 2 + h
                    dve.wait_ge(s_in[h], (it + 1) * 16)
                    dve.wait_ge(s_sent[h], it * (16 * C) + 16)
                    dve.sem_inc(m.step_dve, 1)
                    for f in range(F):
                        dve.tensor_tensor_scan(rows[h][:, f::XDW], m.same[:, bass.ds(n * C, C)], starts[h][:, f::F],
                                               rows[1 - h][:, (C - 1) * XDW + f:(C - 1) * XDW + f + 1], ALU.mult, ALU.add)
                    dve.tensor_copy(rows[h][:, F::XDW], m.recs[:, bass.ds(n * (C * REC), C * REC)].rearrange("p (c w) -> p c w", w=REC)[:, :, 1])
                    dve.tensor_copy(to[h][:, :], reci[:, bass.ds(n * (C * REC), C * REC)].rearrange("p (c w) -> p c w", w=REC)[:, :, 4])
                    dve.drain().then_inc(s_done, 1)
                    dve.sem_inc(s_free, 1)
                    dve.wait_ge(s_used, it * 2 + (h + 1))
                    dve.sem_inc(m.step_dve, 1)
                    dve.tensor_tensor(oa[h][:, :, :], bcast(m.lane_b[:, :], 1, C), bcast(lo_b[:, bass.ds(n * C, C)], 2, P), ALU.is_equal)
                    dve.tensor_tensor(ob[h][:, :, :], bcast(m.lane_b[:, 0:B], 1, C), bcast(hi_b[:, bass.ds(n * C, C)], 2, B), ALU.is_equal).then_inc(s_made, 1)
            dve.wait_ge(s_sum, 1)
            dve.tensor_copy(m.cnt[1][:, :], ps_n[:, 0:B])
            dve.drain().then_inc(s_used, 1)
            places_dve(dve, m, w, 1, 0)

        @block.tensor
        def _(pe):
            pe.wait_ge(s_first, 1)
            pe.matmul(ps_n[:, 0:B], zero[:, :], zero[:, 0:B], start=True, stop=False)
            pe.sem_inc(s_used, 2)
            with pe.Fori(0, TURNS) as it:
                for h in range(2):
                    pe.wait_ge(s_made, it * 2 + (h + 1))
                    pe.sem_inc(m.step_pe, 1)
                    for c in range(C):
                        last = pe.matmul(ps_n[:, 0:B], oa[h][:, c, :], ob[h][:, c, :], start=False, stop=False)
                    last.then_inc(s_used, 1)
            pe.matmul(ps_n[:, 0:B], zero[:, :], zero[:, 0:B], start=False, stop=True).then_inc(s_sum, 1)
            pe.wait_ge(s_used, CHUNKS + 3)
            places_pe(pe, m, w, 1, 0)


def stage_neighbours(nc, m):
    C = J // 8
    TURNS = J // (2 * C)
    with ExitStack() as ctx:
        def sb(name, shape, dt=F32):
            return ctx.enter_context(nc.sbuf_tensor(name, shape, dt))
        def sem(n):
            return ctx.enter_context(nc.semaphore(n))
        rows = [sb(f"rows3{h}", [P, C * XDW]) for h in range(2)]
        sc = [sb(f"scanned3{h}", [P, C * F]) for h in range(2)]
        same = sb("same_d", [P, C])
        low = sb("low", [P, 1])
        prev = sb("prev_d", [P, 1])
        s_prev, s_done, s_free = (sem(n) for n in ("s_prev", "s_done", "s_free"))
        s_in = [sem(f"s_in{h}") for h in range(2)]
        s_put = [sem(f"s_put{h}") for h in range(2)]
        block = ctx.enter_context(nc.Block())

        @block.sync
        def _(sp):
            sp.dma_start(prev[:, :], m.xd[0:EP, :].rearrange("(p j) w -> p j w", p=P)[:, 0, F:XDW], allow_slow_non_contiguous=True).then_inc(s_prev, 16)
            src = m.xd[1:EP + 1, :].rearrange("(p j) w -> p (j w)", p=P)
            with sp.Fori(0, TURNS) as it:
                for h in range(2):
                    sp.wait_ge(s_free, it * 2 + (h + 1))
                    sp.sem_inc(m.step_sp, 1)
                    sp.dma_start(rows[h][:, :], src[:, bass.ds((it * 2 + h) * (C * XDW), C * XDW)]).then_inc(s_in[h], 16)

        @block.scalar
        def _(act):
            prime(act, m, s_put)
            out = m.s3[0:EP, :].rearrange("(p j) w -> p (j w)", p=P)
            with act.Fori(0, TURNS) as it:
                for h in range(2):
                    act.wait_ge(s_done, it * 2 + (h + 1))
                    act.sem_inc(m.step_act, 1)
                    act.dma_start(out[:, bass.ds((it * 2 + h) * (C * F), C * F)], sc[h][:, :]).then_inc(s_put[h], 16)
            for h in range(2):
                act.wait_ge(s_put[h], 16 + 16 * TURNS)

        @block.vector
        def _(dve):
            dve.sem_inc(s_free, 2)
            dve.memset(sc[1][:, :], 0.0)
            dve.memset(m.whole[1][:, :], 1.0)
            dve.drain()
            dve.wait_ge(s_prev, 16)
            with dve.Fori(0, TURNS) as it:
                for h in range(2):
                    n = it * 2 + h
                    dve.wait_ge(s_in[h], (it + 1) * 16)
                    dve.wait_ge(s_put[h], (it + 1) * 16)
                    dve.sem_inc(m.step_dve, 1)
                    key = rows[h][:, F::XDW]
                    dve.tensor_tensor(same[:, 1:C], key[:, 1:C], key[:, 0:C - 1], ALU.is_equal)
                    dve.tensor_tensor(same[:, 0:1], key[:, 0:1], prev[:, :], ALU.is_equal)
                    dve.drain()
                    dve.tensor_copy(prev[:, :], key[:, C - 1:C])
                    dve.tensor_reduce(low[:, :], same[:, :], AX, ALU.min)
                    dve.drain()
                    dve.tensor_tensor(m.whole[1][:, :], m.whole[1][:, :], low[:, :], ALU.min)
                    for f in range(F):
                        dve.tensor_tensor_scan(sc[h][:, f::F], same[:, :], rows[h][:, f::XDW],
                                               sc[1 - h][:, (C - 1) * F + f:(C - 1) * F + f + 1], ALU.mult, ALU.add)
                    dve.drain().then_inc(s_done, 1)
                    dve.sem_inc(s_free, 1)
            dve.tensor_copy(m.fin[:, 0:F], sc[1][:, (C - 1) * F:C * F])


def stage_neighbour_nodes(nc, m, w3, b3, out):
    PER = 512 // (2 * F)
    LOTS = [(n, min(n + PER, b // 2)) for a, b in PARTS for n in range(a // 2, b // 2, PER)]
    with ExitStack() as ctx:
        def sb(name, shape, dt=F32):
            return ctx.enter_context(nc.sbuf_tensor(name, shape, dt))
        def sem(n):
            return ctx.enter_context(nc.semaphore(n))
        ws = sb("w3_twice", [4 * F, 2 * F])
        bs = sb("b3_rows", [P, F])
        cat = sb("cat", [P, B * 2 * F])
        inv = sb("inv", [P, B])
        ct = sb("cat_t", [4 * F, 2, P])
        ps_x = [ctx.enter_context(nc.psum_tensor(f"ps_x3{i}", [P, 512], F32)) for i in range(2)]
        ps_o = [ctx.enter_context(nc.psum_tensor(f"ps_o3{i}", [P, 512], F32)) for i in range(2)]
        s_var, s_std, s_w, s_cat, s_ct, s_ctc, s_o, s_oc, s_fin, s_out, s_zero = (
            sem(n) for n in ("s_var", "s_std", "s_w", "s_cat", "s_ct", "s_ctc", "s_o", "s_oc", "s_fin", "s_out", "s_zero"))
        block = ctx.enter_context(nc.Block())

        def sp_part(sp):
            sp.wait_ge(s_zero, 1)
            for i in range(2):
                sp.dma_start(ws[i * 2 * F:(i + 1) * 2 * F, i * F:(i + 1) * F], w3).then_inc(s_w, 16)
            sp.dma_start(bs[:, :], b3.partition_broadcast(P)).then_inc(s_w, 16)
            for i, (a, b) in enumerate(PARTS):
                sp.wait_ge(s_fin, i + 1)
                b = min(b, B - 1)
                sp.dma_start(out[a * P:b * P, :].rearrange("(b p) f -> p b f", p=P),
                             m.x[:, a * F:b * F].rearrange("p (b f) -> p b f", f=F)).then_inc(s_out, 16)
            sp.dma_start(out[(B - 1) * P:N, :], m.x[0:LASTBLOCK, (B - 1) * F:B * F]).then_inc(s_out, 16)
            sp.wait_ge(s_out, 48)

        def dve_part(dve, ge, i):
            a, b = PARTS[i]
            if i == 0:
                dve.memset(ws[:, :], 0.0).then_inc(s_zero, 1)
                dve.tensor_scalar(inv[:, :], m.cnt[1][:, :], 1.0, None, ALU.max)
                dve.tensor_copy(cat[:, :].rearrange("p (b w) -> p b w", w=2 * F)[:, :, 0:F],
                                m.x[:, 0:B * F].rearrange("p (b f) -> p b f", f=F))
                dve.drain()
                dve.reciprocal(inv[:, :], inv[:, :])
                dve.drain()
            dve.tensor_tensor(cat[:, a * 2 * F:b * 2 * F].rearrange("p (b w) -> p b w", w=2 * F)[:, :, F:2 * F],
                              ge[:, a * F:b * F].rearrange("p (b f) -> p b f", f=F), bcast(inv[:, a:b], 2, F), ALU.mult)
            dve.drain().then_inc(s_cat, 1)
            dve.wait_ge(s_w, 48)
            for q, (g, end) in enumerate(LOTS):
                if a <= 2 * g < b:
                    dve.wait_ge(s_o, end)
                    dve.tensor_tensor(m.sq[:, g * 2 * F:end * 2 * F].rearrange("p (b f) -> p b f", f=F),
                                      ps_o[q % 2][:, 0:(end - g) * 2 * F].rearrange("p (b f) -> p b f", f=F),
                                      bcast(bs[:, :], 1, 2 * (end - g)), ALU.add).then_inc(s_oc, 1)
            dve.drain()
            x = m.x[:, a * F:b * F]
            dve.scalar_tensor_tensor(x, m.sq[:, a * F:b * F], 0.0, x, ALU.max, ALU.add)
            dve.drain()
            layer_norm(nc, m, dve, s_var, s_std, i + 1, PARTS[i])
            dve.drain().then_inc(s_fin, 1)

        def pe_part(pe):
            pe.wait_ge(s_w, 48)
            for i, (a, b) in enumerate(PARTS):
                pe.wait_ge(s_cat, i + 1)
                for n in range(a // 2, b // 2 + 1):
                    if n < b // 2:
                        if n >= 2:
                            pe.wait_ge(s_ctc, n - 1)
                        pe.transpose(ps_x[n % 2][:, 0:P], cat[:, n * P:(n + 1) * P], m.ident[:, :]).then_inc(s_ct, 1)
                    if n > a // 2:
                        q = next(q for q, (g, end) in enumerate(LOTS) if g <= n - 1 < end)
                        c = n - 1 - LOTS[q][0]
                        pe.wait_ge(s_ctc, n)
                        if c == 0 and q >= 2:
                            pe.wait_ge(s_oc, q - 1)
                        pe.matmul(ps_o[q % 2][:, c * 2 * F:(c + 1) * 2 * F], ct[:, (n - 1) % 2, :], ws[:, :], start=True, stop=True).then_inc(s_o, 1)

        def act_part(act):
            for i, (a, b) in enumerate(PARTS):
                for n in range(a // 2, b // 2):
                    if n >= 2:
                        act.wait_ge(s_o, n - 1)
                    act.wait_ge(s_ct, n + 1)
                    act.activation(ct[:, n % 2, :], ps_x[n % 2][:, 0:P], ACT.Copy).then_inc(s_ctc, 1)
                root(nc, m, act, s_var, s_std, i + 1, PARTS[i])

        node_sums(nc, m, ctx, block, 1, m.s3, dve_part, pe_part, act_part, sp_part)


class Memory:
    pass


def gnn(nc, x, src, dst, edge_attr_2, edge_weight, w0, fc_w, fc_b, bias0, w1, w3, b3, out):
    m = Memory()

    def dram(name, shape, dt=F32):
        return nc.dram_tensor(f"{name}_dram", shape, dt).ap()

    m.keyrow = [dram(f"keyrow{k}", (EP,), I16) for k in range(2)]
    m.lorow = [dram(f"lorow{k}", (EP,), BF16) for k in range(2)]
    m.carry_row = [dram(f"carry_row{k}", (NN,), BF16) for k in range(2)]
    m.rec = dram("rec", (EP + 1, REC))
    m.xd = dram("xd", (EP + 1, XDW))
    m.t0, m.asrc_t, m.asrc_at = dram("t0", (NN, T0W)), dram("asrc_t", (NN, H)), dram("asrc_at", (EP, H))
    m.t1 = dram("t1", (NN, KK * F))
    m.x3t, m.h3 = dram("x3t", (NN, F)), dram("h3", (EP, F))
    m.s0, m.s1, m.s3 = dram("s0", (EP + 1, S0W)), dram("s1", (EP + 1, F)), dram("s3", (EP + 1, F))

    with ExitStack() as ctx:
        def sb(name, shape, dt=F32):
            return ctx.enter_context(nc.sbuf_tensor(name, shape, dt))
        m.step_pool, m.step_sp, m.step_act, m.step_dve, m.step_pe = (
            ctx.enter_context(nc.semaphore(f"step_{n}")) for n in ("pool", "sp", "act", "dve", "pe"))
        m.x = sb("x_sb", [P, GROUPS * 4 * F])
        m.sq = sb("sq", [P, B * F])
        m.mean, m.var, m.std = sb("mean", [P, B]), sb("var", [P, B]), sb("std", [P, B])
        m.lane, m.lane_b, m.part = sb("lane", [P, P]), sb("lane_b", [P, P], BF16), sb("part_index", [P, 1])
        m.ident, m.above, m.below, m.ones, m.zero, m.undo = (sb(n, [P, P]) for n in ("ident", "above", "below", "ones", "zero", "undo"))
        m.cnt_first, m.next_half = sb("cnt_first", [P, B]), sb("next_half", [P, B])
        m.unsorted = sb("unsorted", [P, 1], I32)
        m.minus, m.eps = sb("minus", [P, XDW]), sb("eps", [P, 1])
        m.cnt, m.start, m.next, m.has = ([sb(f"{n}{k}", [P, B]) for k in range(2)] for n in ("cnt", "start", "next", "has"))
        m.i_end = [sb(f"i_end{k}", [P, B], I32) for k in range(2)]
        m.i_start = sb("i_start", [P, B], I32)
        m.asrc_rows = sb("asrc_rows", [P, B * H])
        m.sumw = sb("sumw", [P, B])
        m.spare, m.primed, m.first_word = sb("spare", [1, 16]), 0, x[0:1, 0:1]
        m.fin = sb("fin", [P, S0W])
        m.whole = [sb(f"whole{k}", [P, 1]) for k in range(2)]
        m.recs = sb("recs_sb", [P, J * REC])
        m.same = sb("same", [P, J])
        m.lo, m.hi = [None, sb("lo1", [P, J + 4])], [None, sb("hi1", [P, J + 4])]
        with ExitStack() as middle:
            def sm(name, shape, dt=F32):
                return middle.enter_context(nc.sbuf_tensor(name, shape, dt))
            m.w = sm("w", [P, J])
            with ExitStack() as front:
                def sf(name, shape, dt=F32):
                    return front.enter_context(nc.sbuf_tensor(name, shape, dt))
                m.key = [sf(f"key{k}", [P, J]) for k in range(2)]
                m.attr, m.lo[0], m.hi[0] = m.recs[:, 0:2 * J], m.recs[:, 2 * J:3 * J + 4], m.recs[:, 3 * J:4 * J + 4]
                m.natural = m.recs[:, 4 * J:5 * J].bitcast(I32)
                with ExitStack() as early:
                    def se(name, shape, dt=F32):
                        return early.enter_context(nc.sbuf_tensor(name, shape, dt))
                    m.lo_b, m.hi_b = ([se(f"{n}{k}", [P, J], BF16) for k in range(2)] for n in ("lo_b", "hi_b"))
                    m.half_minus_lo = [se(f"half_minus_lo{k}", [P, J]) for k in range(2)]
                    m.zeros = se("zeros_f", [P, H * J])
                    stage_load(nc, m, x, src, dst, edge_attr_2, edge_weight)
                    stage_count(nc, m)
                stage_places(nc, m, w0, fc_w, fc_b)
                stage_rank(nc, m)
            stage_attend(nc, m)
            stage_attend_nodes(nc, m, w0, bias0)
            stage_spline_table(nc, m, w1)
            stage_spline(nc, m)
        stage_spline_nodes(nc, m)
        stage_exchange(nc, m)
        stage_neighbours(nc, m)
        stage_neighbour_nodes(nc, m, w3, b3, out)


_INS = ['x', 'src', 'dst', 'edge_attr_2', 'edge_weight', 'L0_gnn_w', 'L0_gnn_fc_w', 'L0_gnn_fc_b', 'L0_gnn_bias',
        'L1_gnn_weight', 'L3_gnn_W', 'L3_gnn_b']
_OUTS = [((N, F), 'float32')]


def kernel(**inputs):
    import numpy as _np
    import concourse.bacc as _bacc
    from concourse import mybir as _mybir
    from concourse.bass_utils import run_bass_kernel_spmd as _run

    nc = _bacc.Bacc("TRN2", target_bir_lowering=False, num_devices=1)
    arrays, args = {}, []
    for name in _INS:
        a = _np.ascontiguousarray(inputs[name])
        arrays[f"in_{name}_dram"] = a
        args.append(nc.dram_tensor(f"in_{name}_dram", a.shape, _mybir.dt.from_np(a.dtype), kind="ExternalInput").ap())
    for i, (shape, dtype) in enumerate(_OUTS):
        dt = _mybir.dt.from_np(_np.dtype(dtype))
        args.append(nc.dram_tensor(f"out_{i}_dram", shape, dt, kind="ExternalOutput").ap())
    gnn(nc, *args)
    r = _run(nc, [arrays], core_ids=[0])
    got = tuple(r.results[0][f"out_{i}_dram"] for i in range(len(_OUTS)))
    return got[0]
```
